# Optimizing a Trainium2 kernel written in Bass

```python
import numpy as np
import jax
import jax.numpy as jnp

def _softmax(x, axis=-1):
    return jax.nn.softmax(x, axis=axis)

def _gelu(x):
    return jax.nn.gelu(x, approximate=True)

def _silu(x):
    return jax.nn.silu(x)

def _sigmoid(x):
    return jax.nn.sigmoid(x)

def _layernorm(x, axis=-1, eps=1e-05):
    m = jnp.mean(x, axis=axis, keepdims=True)
    v = jnp.var(x, axis=axis, keepdims=True)
    return (x - m) / jnp.sqrt(v + eps)

def _scatter_add(tgt, idx, src, axis=0):
    return tgt.at[idx].add(src)

def _segment_sum(src, seg, n):
    return jax.ops.segment_sum(src, seg, n)
kernel_name = 'mk_gnn_resnorm_d2_gnn_r8_c6bc2f'

def setup_inputs(seed: int=0):
    np.random.seed(seed)
    _w = jnp.asarray

    def _rec_inputs():
        import jax
        import jax.numpy as jnp
        _gk = jax.random.key(seed)
        x = -0.000202 + 1 * jax.random.normal(jax.random.fold_in(_gk, 1), (6250, 128), jnp.float32)
        src = jax.random.randint(jax.random.fold_in(_gk, 2), (100000,), 0, 6250, jnp.int32)
        dst = jax.random.randint(jax.random.fold_in(_gk, 3), (100000,), 0, 6250, jnp.int32)
        _o = jnp.argsort(dst, stable=True)
        src = src[_o]
        dst = dst[_o]
        edge_attr_32 = 0.000196303 + 1.00016 * jax.random.normal(jax.random.fold_in(_gk, 13), (100000, 32), jnp.float32)
        edge_weight1 = jax.random.uniform(jax.random.fold_in(_gk, 15), (100000, 1), jnp.float32, 0.0, 1)
        node_vec1 = jax.random.uniform(jax.random.fold_in(_gk, 16), (6250, 1), jnp.float32, 0.0, 1)
        return (x, src, dst, edge_attr_32, edge_weight1, node_vec1)
    x, src, dst, edge_attr_32, edge_weight1, node_vec1 = _rec_inputs()

    def _L0_gnn_setup():
        import jax, jax.numpy as jnp
        import numpy as np
        N_NODES = 6250
        N_EDGES = 100000
        D_IN = 128
        D_OUT = 128
        key = jax.random.key(seed)
        k1, k2, k3 = jax.random.split(key, 3)
        x = jax.random.normal(k1, (N_NODES, D_IN), dtype=jnp.float32)
        edge_index = jax.random.randint(k2, (2, N_EDGES), 0, N_NODES, dtype=jnp.int64)
        limit = float(np.sqrt(6.0 / (D_IN + D_OUT)))
        W = jax.random.uniform(k3, (D_IN, D_OUT), dtype=jnp.float32, minval=-limit, maxval=limit)
        b = jnp.zeros((D_OUT,), dtype=jnp.float32)
        return {'x': x, 'edge_index': edge_index, 'W': W, 'b': b}
    _L0_gnn_all = _L0_gnn_setup()
    _L0_gnn_in = {k: v for k, v in _L0_gnn_all.items() if k in ('W', 'b')}
    del _L0_gnn_all

    def _L1_gnn_setup():
        import jax, jax.numpy as jnp
        import numpy as np
        N, E = (6250, 100000)
        C, A_ALL, RAD_IN, FC1, FC2 = (128, 256, 32, 64, 64)
        H, AH, VH = (8, 16, 16)

        def _radial_mlp(x, w1, b1, w2, b2, w3, b3):
            x = jax.nn.silu(x @ w1 + b1)
            x = jax.nn.silu(x @ w2 + b2)
            return x @ w3 + b3

        def _smooth_leaky_relu(x, a=0.2):
            return 0.5 * (1.0 + a) * x + 0.5 * (1.0 - a) * x * (2.0 * jax.nn.sigmoid(x) - 1.0)

        def _segment_softmax(scores, seg, num_segments):
            m = jax.ops.segment_max(scores, seg, num_segments=num_segments)
            m = jnp.where(jnp.isfinite(m), m, 0.0)
            e = jnp.exp(scores - m[seg])
            s = jax.ops.segment_sum(e, seg, num_segments=num_segments)
            return e / (s[seg] + 1e-16)
        key = jax.random.key(seed)
        ks = jax.random.split(key, 16)

        def g(k, shape):
            scale = 1.0 / np.sqrt(shape[0])
            return jax.random.normal(k, shape, dtype=jnp.float32) * scale
        return {'node_input': jax.random.normal(ks[0], (N, C), dtype=jnp.float32), 'node_attr': jnp.ones((N, 1), jnp.float32), 'edge_attr': jax.random.uniform(ks[1], (E, 1), dtype=jnp.float32), 'edge_scalars': jax.random.normal(ks[2], (E, RAD_IN), dtype=jnp.float32), 'edge_src': jax.random.randint(ks[3], (E,), 0, N, dtype=jnp.int32), 'edge_dst': jax.random.randint(ks[4], (E,), 0, N, dtype=jnp.int32), 'batch': jnp.zeros((N,), jnp.int32), 'w_src': g(ks[5], (C, C)), 'b_src': jnp.zeros((C,), jnp.float32), 'w_dst': g(ks[6], (C, C)), 'fc_w1': g(ks[7], (RAD_IN, FC1)), 'fc_b1': jnp.zeros((FC1,), jnp.float32), 'fc_w2': g(ks[8], (FC1, FC2)), 'fc_b2': jnp.zeros((FC2,), jnp.float32), 'fc_w3': g(ks[9], (FC2, C)), 'fc_b3': jnp.zeros((C,), jnp.float32), 'w_sep': g(ks[10], (C, A_ALL)), 'b_sep': jnp.zeros((A_ALL,), jnp.float32), 'alpha_dot': jax.random.normal(ks[11], (1, H, AH), dtype=jnp.float32) * np.sqrt(2.0 / (H * AH)), 'w_proj': g(ks[12], (H * VH, C)), 'b_proj': jnp.zeros((C,), jnp.float32)}
    _L1_gnn_all = _L1_gnn_setup()
    _L1_gnn_in = {k: v for k, v in _L1_gnn_all.items() if k in ('w_src', 'b_src', 'w_dst', 'fc_w1', 'fc_b1', 'fc_w2', 'fc_b2', 'fc_w3', 'fc_b3', 'w_sep', 'b_sep', 'alpha_dot', 'w_proj', 'b_proj')}
    del _L1_gnn_all
    return {'x': x, 'src': src, 'dst': dst, 'edge_attr_32': edge_attr_32, 'edge_weight1': edge_weight1, 'node_vec1': node_vec1, 'L0_gnn_W': _L0_gnn_in['W'], 'L0_gnn_b': _L0_gnn_in['b'], 'L1_gnn_w_src': _L1_gnn_in['w_src'], 'L1_gnn_b_src': _L1_gnn_in['b_src'], 'L1_gnn_w_dst': _L1_gnn_in['w_dst'], 'L1_gnn_fc_w1': _L1_gnn_in['fc_w1'], 'L1_gnn_fc_b1': _L1_gnn_in['fc_b1'], 'L1_gnn_fc_w2': _L1_gnn_in['fc_w2'], 'L1_gnn_fc_b2': _L1_gnn_in['fc_b2'], 'L1_gnn_fc_w3': _L1_gnn_in['fc_w3'], 'L1_gnn_fc_b3': _L1_gnn_in['fc_b3'], 'L1_gnn_w_sep': _L1_gnn_in['w_sep'], 'L1_gnn_b_sep': _L1_gnn_in['b_sep'], 'L1_gnn_alpha_dot': _L1_gnn_in['alpha_dot'], 'L1_gnn_w_proj': _L1_gnn_in['w_proj'], 'L1_gnn_b_proj': _L1_gnn_in['b_proj']}

def reference(x, src, dst, edge_attr_32, edge_weight1, node_vec1, L0_gnn_W, L0_gnn_b, L1_gnn_w_src, L1_gnn_b_src, L1_gnn_w_dst, L1_gnn_fc_w1, L1_gnn_fc_b1, L1_gnn_fc_w2, L1_gnn_fc_b2, L1_gnn_fc_w3, L1_gnn_fc_b3, L1_gnn_w_sep, L1_gnn_b_sep, L1_gnn_alpha_dot, L1_gnn_w_proj, L1_gnn_b_proj):
    import jax
    import jax.numpy as jnp

    def _L0_gnn_ref(x, edge_index, W, b):
        import jax, jax.numpy as jnp
        import numpy as np
        N_NODES = 6250
        N_EDGES = 100000
        D_IN = 128
        D_OUT = 128
        N = x.shape[0]
        h = x @ W
        src = edge_index[0]
        dst = edge_index[1]
        loop = jnp.arange(N, dtype=src.dtype)
        src = jnp.concatenate([src, loop])
        dst = jnp.concatenate([dst, loop])
        ew = jnp.ones(src.shape[0], dtype=h.dtype)
        deg = jax.ops.segment_sum(ew, dst, num_segments=N)
        deg_inv_sqrt = jnp.where(deg > 0, jax.lax.rsqrt(jnp.maximum(deg, 1e-12)), 0.0)
        norm = deg_inv_sqrt[src] * ew * deg_inv_sqrt[dst]
        msg = norm[:, None] * h[src]
        out = jax.ops.segment_sum(msg, dst, num_segments=N)
        return out + b

    def _L1_gnn_ref(node_input, node_attr, edge_attr, edge_scalars, edge_src, edge_dst, batch, w_src, b_src, w_dst, fc_w1, fc_b1, fc_w2, fc_b2, fc_w3, fc_b3, w_sep, b_sep, alpha_dot, w_proj, b_proj):
        import jax, jax.numpy as jnp
        import numpy as np
        N, E = (6250, 100000)
        C, A_ALL, RAD_IN, FC1, FC2 = (128, 256, 32, 64, 64)
        H, AH, VH = (8, 16, 16)

        def _radial_mlp(x, w1, b1, w2, b2, w3, b3):
            x = jax.nn.silu(x @ w1 + b1)
            x = jax.nn.silu(x @ w2 + b2)
            return x @ w3 + b3

        def _smooth_leaky_relu(x, a=0.2):
            return 0.5 * (1.0 + a) * x + 0.5 * (1.0 - a) * x * (2.0 * jax.nn.sigmoid(x) - 1.0)

        def _segment_softmax(scores, seg, num_segments):
            m = jax.ops.segment_max(scores, seg, num_segments=num_segments)
            m = jnp.where(jnp.isfinite(m), m, 0.0)
            e = jnp.exp(scores - m[seg])
            s = jax.ops.segment_sum(e, seg, num_segments=num_segments)
            return e / (s[seg] + 1e-16)
        n_nodes = node_input.shape[0]
        n_edges = edge_src.shape[0]
        msg_src = node_input @ w_src + b_src
        msg_dst = node_input @ w_dst
        message = msg_src[edge_src] + msg_dst[edge_dst]
        rad_w = _radial_mlp(edge_scalars, fc_w1, fc_b1, fc_w2, fc_b2, fc_w3, fc_b3)
        message = message * edge_attr * rad_w
        message = message @ w_sep + b_sep
        msg_h = message.reshape(n_edges, H, AH + VH)
        alpha = _smooth_leaky_relu(msg_h[:, :, :AH])
        value = msg_h[:, :, AH:]
        score = jnp.einsum('ehk,ahk->eh', alpha, alpha_dot)
        att = _segment_softmax(score, edge_dst, n_nodes)[..., None]
        out = jax.ops.segment_sum(value * att, edge_dst, num_segments=n_nodes)
        out = out.reshape(n_nodes, H * VH)
        return out @ w_proj + b_proj
    edge_index = jnp.stack([src, dst])
    batch0 = jnp.zeros((6250,), jnp.int32)
    x = _layernorm(x + _L0_gnn_ref(x, edge_index, L0_gnn_W, L0_gnn_b), axis=-1)
    x = _layernorm(x + _L1_gnn_ref(x, node_vec1, edge_weight1, edge_attr_32, src, dst, batch0, L1_gnn_w_src, L1_gnn_b_src, L1_gnn_w_dst, L1_gnn_fc_w1, L1_gnn_fc_b1, L1_gnn_fc_w2, L1_gnn_fc_b2, L1_gnn_fc_w3, L1_gnn_fc_b3, L1_gnn_w_sep, L1_gnn_b_sep, L1_gnn_alpha_dot, L1_gnn_w_proj, L1_gnn_b_proj), axis=-1)
    return x

_drawn_inputs = setup_inputs


def setup_inputs(seed=0):
    import zlib

    import numpy as np

    out = dict(_drawn_inputs(seed))
    spreads = {'L0_gnn_b': (0.0, 0.1),
     'L1_gnn_b_src': (0.0, 0.8),
     'L1_gnn_fc_b1': (0.0, 0.584),
     'L1_gnn_fc_b2': (0.0, 0.336),
     'L1_gnn_fc_b3': (0.0, 0.1),
     'L1_gnn_b_sep': (0.0, 0.1),
     'L1_gnn_b_proj': (0.0, 0.1)}
    factors = {'L1_gnn_alpha_dot': 5.297}
    for name, (base, spread) in spreads.items():
        noise = np.random.default_rng([zlib.crc32(name.encode()), seed]).standard_normal(out[name].shape)
        drawn = base * np.exp(spread * noise) if base else spread * noise
        out[name] = jnp.asarray(drawn.astype(out[name].dtype))
    for name, factor in factors.items():
        out[name] = (out[name] * factor).astype(out[name].dtype)
    return out
```

```python
import numpy as np
from contextlib import ExitStack

N_NODES, N_EDGES, C = 6250, 100000, 128
P = 128
NB = (N_NODES + P - 1) // P
NP = NB * P
GE = 512
TPG = GE // P
NG = (N_EDGES + GE - 1) // GE
EP = NG * GE
NT = EP // P
NSB, GPS = 14, 14
PPS = GPS // 2
WIN = 64
NW = NP + WIN
CB = 7
NCH = NB // CB
CC = CB * P
H, K = 8, 16
RAD, FC = 32, 64
DEG_T = 14
DEG_STEPS = NT // DEG_T
BIG = 1.0e30
LN_EPS = 1e-5
assert NSB * GPS == NG and NCH * CB == NB and DEG_STEPS * DEG_T == NT


def build(nc, a, out):
    import concourse.bass as bass
    from concourse import mybir

    f32, bf16, i32 = mybir.dt.float32, mybir.dt.bfloat16, mybir.dt.int32
    ALU, ACT, AX = mybir.AluOpType, mybir.ActivationFunctionType, mybir.AxisListType
    ds = bass.ds

    g_tab = nc.dram_tensor("g_tab", [NP, C], f32, kind="Internal").ap()
    ms_tab = nc.dram_tensor("ms_tab", [NP, C], f32, kind="Internal").ap()
    md_tab = nc.dram_tensor("md_tab", [NW, C], f32, kind="Internal").ap()
    rad_tab = nc.dram_tensor("rad_tab", [NG, P, GE], f32, kind="Internal").ap()

    top = ExitStack()
    made = [0]

    def sbuf(shape, dt, st=top):
        made[0] += 1
        return st.enter_context(nc.sbuf_tensor(f"sb{made[0]}", shape, dt))
    sem = lambda name: top.enter_context(nc.semaphore(name))

    with top:
        acc = sbuf([P, 2, NW], f32)
        g_nodes = acc[:, 1, 0:NP].rearrange("p (b c) -> p b c", c=C)
        x1_nodes = sbuf([P, NB, C], f32)
        hold = sbuf([P, GPS, GE], f32)
        gcn_acc = hold[:].rearrange("p a b -> p (a b)")[:, 0:NW]
        src_i = sbuf([P, NT + TPG], i32)
        dst_rel = sbuf([P, NT], f32)
        win_i = sbuf([P, NG], i32)
        win_f = sbuf([P, NG], f32)
        last_f = sbuf([P, NG], f32)
        win_iota = sbuf([P, NG], f32)
        iota_i = sbuf([P, P], i32)
        iota_f = sbuf([P, P], f32)
        iota_b = sbuf([P, P], bf16)
        part_i = sbuf([P, 1], i32)
        part_f = sbuf([P, 1], f32)
        ident = sbuf([P, P], f32)
        dis = sbuf([P, NB], f32)
        slot_first = sbuf([P, 2, NG], f32)
        slot_prev = sbuf([P, 2, NG], f32)
        max_first = sbuf([GPS * H, NSB], f32)
        max_last = sbuf([GPS * H, NSB], f32)
        idx = sbuf([P, 4 * TPG], i32)
        gath = sbuf([P, 2, TPG, C], f32)
        onehot = sbuf([P, 2, TPG, WIN], f32)
        mrad = sbuf([P, 2, GE], f32)
        w_gcn = sbuf([P, C], f32)
        w_sd = sbuf([P, 2 * C], f32)
        w1_bd = sbuf([P, 2, P], f32)
        w2_bd = sbuf([P, P], f32)
        w3_2 = sbuf([P, C], f32)
        w_alpha = sbuf([P, P], f32)
        w_value = sbuf([P, P], f32)
        a_dot = sbuf([P, H], f32)
        w_proj = sbuf([P, C], f32)
        b_gcn, b_src, b_proj = (sbuf([P, C], f32) for _ in range(3))
        b1_2, b2_2, b3, b_alpha, b_alpha_half, b_value = (sbuf([P, 1], f32) for _ in range(6))
        neg_edge = sbuf([GPS * H, GE + 1], f32)
        small = sbuf([P, 64], f32)
        zeros = sbuf([WIN, C], f32)

        with ExitStack() as st:
            dst_i = sbuf([P, NT], i32, st)
            lo_i, hi_i = sbuf([P, NT], i32, st), sbuf([P, NT], i32, st)
            lo_b, hi_b = sbuf([P, NT], bf16, st), sbuf([P, NT], bf16, st)
            last_i = sbuf([P, NG], i32, st)
            lo_hot = sbuf([P, 2, DEG_T, P], bf16, st)
            hi_hot = sbuf([P, 2, DEG_T, NB], bf16, st)
            xT = sbuf([P, CC], f32, st)
            attr = sbuf([P, 2, P], f32, st)
            ea_row = sbuf([P, 2, GE], f32, st)
            h1 = sbuf([P, 2 * P], f32, st)
            h2 = sbuf([P, 2 * P], f32, st)
        with ExitStack() as st:
            stage = sbuf([P, CC], f32, st)
            x_chunk = sbuf([P, CB, C], f32, st)
            y = sbuf([P, CB, C], f32, st)
            y2 = sbuf([P, CB, C], f32, st)
            xc = sbuf([P, CB, C], f32, st)
            x1T = sbuf([P, CC], f32, st)
            ms_out = sbuf([P, CB, C], f32, st)
            md_out = sbuf([P, CB, C], f32, st)
            expand = sbuf([GPS * H, GPS, P], f32, st)
            mrg = [sbuf([P, NG], f32, st) for _ in range(12)]
            mrg2 = sbuf([P, 2, NG], f32, st)
            totals = sbuf([P, 2, NG], f32, st)
        with ExitStack() as st:
            dst_row = sbuf([WIN, 2, GE], i32, st)
            md_win = sbuf([WIN, 2, C], f32, st)
            hotT = sbuf([WIN, 2, GE], f32, st)
            msg = sbuf([P, 2, GE], f32, st)
            pre = sbuf([P, 2, GE], f32, st)
            tanh = sbuf([P, 2, GE], f32, st)
            act_a = sbuf([P, 2, GE], f32, st)
            wval = sbuf([P, 2, GE], f32, st)
            wts = sbuf([P, 2, GE], f32, st)
            scores = sbuf([P, TPG, GPS * H], f32, st)
            seg_row = sbuf([GPS * H, GE], i32, st)
            fwd = sbuf([GPS * H, GE], f32, st)
            seg_max = sbuf([GPS * H, GE], f32, st)
            shifted = sbuf([GPS * H, GE], f32, st)
            p_row = sbuf([GPS * H, GE], f32, st)
            p_edge = sbuf([P, TPG, GPS, H], f32, st)

        ps = top.enter_context(nc.psum_tensor("psum", [P, 8, 512], f32))
        psflat = ps[:].rearrange("p b n -> p (b n)")

        s_in = sem("s_inputs_loaded")
        s_const = sem("s_pool_constants")
        s_prep = sem("s_vector_prepared")
        s_xT = sem("s_xT_loaded")
        s_xw = sem("s_xw_product")
        s_xw_copied = sem("s_xw_copied")
        s_hot = sem("s_degree_onehots")
        s_deg = sem("s_degree_products")
        s_sqrt, s_dis, s_g = sem("s_degree_sqrt"), sem("s_dis"), sem("s_g")
        s_gtab = sem("s_g_table_stored")
        s_idx = sem("s_indices_copied")
        s_g1 = [sem(f"s_pass1_rows_{j}") for j in range(2)]
        s_in1 = [sem(f"s_pass1_loads_{j}") for j in range(2)]
        s_st1 = [sem(f"s_radial_stored_{j}") for j in range(2)]
        s_hot1, s_sum1, s_acc1 = sem("s_onehot1"), sem("s_sum1"), sem("s_acc1")
        s_l1, s_a1, s_l2, s_a2, s_l3, s_rad = (sem(n) for n in (
            "s_mlp1", "s_silu1", "s_mlp2", "s_silu2", "s_mlp3", "s_radial"))
        s_stage, s_t1, s_xin, s_x1, s_t2, s_x1T, s_mm, s_mso, s_mdo, s_x1c = (sem(n) for n in (
            "s_staged", "s_sums_turned", "s_x_chunk", "s_x1_chunk", "s_x1_turned", "s_x1T",
            "s_tables_product", "s_ms_ready", "s_md_ready", "s_x1_kept"))
        s_tab = sem("s_tables_stored")
        s_zero = sem("s_acc_zeroed")
        s_ln1, s_ln2 = sem("s_ln_variance"), sem("s_ln_sqrt")
        s_g2 = [sem(f"s_pass2_rows_{j}") for j in range(2)]
        s_in2 = [sem(f"s_pass2_loads_{j}") for j in range(2)]
        s_hotT, s_x, s_m, s_sep, s_pre, s_held, s_u, s_sc = (sem(n) for n in (
            "s_hotT", "s_msg_sum", "s_msg", "s_sep", "s_pre", "s_held", "s_act", "s_scores"))
        s_v, s_agg, s_accd = sem("s_weighted"), sem("s_aggregated"), sem("s_accumulated")
        s_seg, s_sccopy, s_turn, s_shift, s_exp, s_back, s_p = (sem(n) for n in (
            "s_segment_rows", "s_scores_copied", "s_scores_turned", "s_shifted", "s_exp", "s_p_turned", "s_p"))
        s_mx, s_mxe, s_me, s_tot, s_wb = (sem(n) for n in (
            "s_max_product", "s_merge_shift", "s_merge_exp", "s_totals", "s_written_back"))
        s_o, s_pr, s_y, s_out = sem("s_o"), sem("s_projected"), sem("s_y_ready"), sem("s_out_stored")
        s_sm, s_maxes, s_ln_own, s_v_own2 = (sem(n) for n in ("s_softmax_steps", "s_group_maxima", "s_norm_steps", "s_chunk_steps"))
        s_slot = sem("s_slot_seen_free")
        s_v_own, s_a_own, s_p_own = sem("s_vector_own"), sem("s_scalar_own"), sem("s_pool_own")

        block = top.enter_context(nc.Block())
        N_IN = 0
        bcast = lambda ap, n: ap.partition_broadcast(n)

        loads = [
            (dst_i[:], a["dstE"]), (src_i[:], a["srcE"]),
            (win_i[:], a["first"].partition_broadcast(P)), (last_i[:], a["last"].partition_broadcast(P)),
            (w_gcn[:], a["w_gcn"]), (w_sd[:, 0:C], a["w_src"]), (w_sd[:, C:2 * C], a["w_dst"]),
            (w3_2[0:FC, :], a["fc_w3"]), (w3_2[FC:2 * FC, :], a["fc_w3"]),
            (w_alpha[:], a["w_alpha"]), (w_value[:], a["w_value"]), (w_proj[:], a["w_proj"]),
            (b_gcn[:], a["b_gcn"].partition_broadcast(P)), (b_src[:], a["b_src"].partition_broadcast(P)),
            (b_proj[:], a["b_proj"].partition_broadcast(P)),
            (b1_2[0:FC, :], a["fc_b1"]), (b1_2[FC:2 * FC, :], a["fc_b1"]),
            (b2_2[0:FC, :], a["fc_b2"]), (b2_2[FC:2 * FC, :], a["fc_b2"]),
            (b3[:], a["fc_b3"]), (b_alpha[:], a["b_alpha"]), (b_value[:], a["b_value"]),
        ]
        placed = [(w1_bd[RAD * t:RAD * t + RAD, t % 2, FC * (t // 2):FC * (t // 2) + FC], a["fc_w1"]) for t in range(4)]
        placed += [(w2_bd[FC * t:FC * t + FC, FC * t:FC * t + FC], a["fc_w2"]) for t in range(2)]
        placed += [(a_dot[K * h:K * h + K, h:h + 1], a["alpha_dot"][K * h:K * h + K, :]) for h in range(H)]
        N_IN = 16 * (len(loads) + len(placed))

        def node_rows(tab, c):
            return tab[0:NP, :].rearrange("(b p) c -> p b c", p=P)[:, ds(c * CB, CB), :]

        @block.sync
        def _(sp):
            for dst, src in loads:
                sp.dma_start(dst, src).then_inc(s_in, 16)
            sp.wait_ge(s_const, 1)
            for dst, src in placed:
                sp.dma_start(dst, src).then_inc(s_in, 16)
            sp.dma_start(xT[:], a["xT"][:, 0:CC]).then_inc(s_xT, 16)
            with sp.Fori(1, NCH) as c:
                sp.wait_ge(s_xw, c)
                sp.dma_start(xT[:], a["xT"][:, ds(c * CC, CC)]).then_inc(s_xT, 16)
            sp.wait_ge(s_g, 1)
            sp.dma_start(g_tab.rearrange("(b p) c -> p b c", p=P), g_nodes).then_inc(s_gtab, 16)

            def load1(g, j):
                sp.dma_start(attr[:, j, :], a["attrT"][:, ds(g * P, P)]).then_inc(s_in1[j], 16)
                sp.dma_start(ea_row[:, j, :], a["ea_row"][:, ds(g * GE, GE)].partition_broadcast(P)).then_inc(s_in1[j], 16)

            def store1(g, j):
                sp.wait_ge(s_rad, g + 1)
                sp.dma_start(rad_tab[ds(g, 1), :, :], mrad[:, j, :]).then_inc(s_st1[j], 16)

            for j in range(2):
                load1(j, j)
            with sp.Fori(0, NG // 2 - 1) as q:
                for j in range(2):
                    store1(q * 2 + j, j)
                    load1(q * 2 + j + 2, j)
            for j in range(2):
                store1(NG - 2 + j, j)

            with sp.Fori(0, NCH) as c:
                sp.wait_ge(s_stage, c + 1)
                sp.dma_start(x_chunk[:], node_rows(a["xN"], c)).then_inc(s_xin, 16)
                sp.wait_ge(s_mso, c + 1)
                sp.dma_start(node_rows(ms_tab, c), ms_out[:]).then_inc(s_tab, 16)
                sp.wait_ge(s_mdo, c + 1)
                sp.dma_start(node_rows(md_tab, c), md_out[:]).then_inc(s_tab, 16)
            sp.dma_start(md_tab[NP:NW, :], zeros[:]).then_inc(s_tab, 16)
            sp.wait_ge(s_tab, 16 * (2 * NCH + 1))
            for j in range(2):
                sp.wait_ge(s_st1[j], 16 * (NG // 2))

            def load2(g, j):
                w = sp.value_load(win_i[0:1, ds(g, 1)], min_val=0, max_val=NP - 1)
                sp.dma_start(md_win[:, j, :], md_tab[ds(w, WIN), :]).then_inc(s_in2[j], 16)
                sp.dma_start(dst_row[:, j, :], a["dst_row"][:, ds(g * GE, GE)].partition_broadcast(WIN)).then_inc(s_in2[j], 16)
                sp.dma_start(mrad[:, j, :], rad_tab[ds(g, 1), :, :]).then_inc(s_in2[j], 16)

            def seg_load(b):
                rows = a["dst_row"][:, ds(b * (GPS * GE), GPS * GE)].rearrange("o (g e) -> g o e", g=GPS)
                sp.dma_start(seg_row[:], rows.broadcast_to([GPS, H, GE])).then_inc(s_seg, 16)

            for j in range(2):
                load2(j, j)
            seg_load(0)
            with sp.Fori(1, PPS) as q:
                for j in range(2):
                    sp.wait_ge(s_m, q * 2 + j - 1)
                    load2(q * 2 + j, j)
            with sp.Fori(1, NSB) as b:
                with sp.Fori(0, PPS) as k:
                    for j in range(2):
                        sp.wait_ge(s_m, b * GPS + k * 2 + (j - 1))
                        load2(b * GPS + k * 2 + j, j)
                sp.wait_ge(s_shift, b)
                seg_load(b)

            with sp.Fori(0, NCH) as c:
                sp.wait_ge(s_y, c + 1)
                sp.dma_start(node_rows(out, c), xc[:]).then_inc(s_out, 16)
            sp.wait_ge(s_out, 16 * NCH)

        @block.gpsimd
        def _(pool):
            for m in (w1_bd, w2_bd, a_dot, ident):
                last = nc.gpsimd.memset(m[:], 0.0)
            last.then_inc(s_p_own, 1)
            pool.wait_ge(s_p_own, 1)
            nc.gpsimd.affine_select(out=ident[:], in_=ident[:], compare_op=ALU.not_equal, fill=1.0, base=0,
                                    pattern=[[-1, P]], channel_multiplier=1)
            nc.gpsimd.memset(zeros[:], 0.0)
            nc.gpsimd.iota(iota_i[:], pattern=[[1, P]], base=0, channel_multiplier=0)
            nc.gpsimd.iota(part_i[:], pattern=[[0, 1]], base=0, channel_multiplier=1).then_inc(s_const, 1)

            def gathers(tab, sems, used, copies_before):
                def copy_list(g, n):
                    nc.gpsimd.tensor_copy(idx[:, n * TPG:(n + 1) * TPG], src_i[:, ds(g * TPG, TPG)]).then_inc(s_idx, 1)

                def step(i, first):
                    for n in range(4):
                        m = (n + 1) % 4
                        if not first or n == 3:
                            pool.wait_ge(sems[m % 2], i * (32 * TPG) + (16 * TPG * (m // 2 + 1) - 32 * TPG * (n < 3)))
                            pool.sem_inc(s_slot, 1)
                        copy_list(i * 4 + (n + 1), m)
                        pool.wait_ge(s_idx, i * 4 + (n + 1 + copies_before))
                        pool.sem_inc(s_slot, 1)
                        if not (first and n < 2):
                            pool.wait_ge(used, i * 4 + (n - 1))
                            pool.sem_inc(s_slot, 1)
                        for t in range(TPG):
                            pool.indirect_dma_start(gath[:, n % 2, t, :], None, tab,
                                                    bass.IndirectOffsetOnAxis(idx[:, n * TPG + t:n * TPG + t + 1], 0)
                                                    ).then_inc(sems[n % 2], 16)
                copy_list(0, 0)
                step(0, True)
                with pool.Fori(1, NG // 4) as i:
                    step(i, False)

            pool.wait_ge(s_in, N_IN)
            pool.wait_ge(s_gtab, 16)
            gathers(g_tab, s_g1, s_sum1, 0)
            pool.wait_ge(s_tab, 16 * (2 * NCH + 1))
            for j in range(2):
                pool.wait_ge(s_g1[j], 8 * TPG * NG)
            pool.wait_ge(s_idx, NG + 1)
            gathers(ms_tab, s_g2, s_x, NG + 1)
            pool.wait_ge(s_accd, NG)
            nc.gpsimd.memset(expand[:], 0.0).then_inc(s_p_own, 1)
            pool.wait_ge(s_p_own, 2)
            nc.gpsimd.affine_select(out=expand[:].rearrange("p g (h v) -> p g h v", h=H), in_=expand[:].rearrange("p g (h v) -> p g h v", h=H),
                                    compare_op=ALU.not_equal, fill=1.0, base=0,
                                    pattern=[[-H, GPS], [-1, H], [0, K]], channel_multiplier=1).then_inc(s_const, 1)

        @block.tensor
        def _(pe):
            mm = nc.tensor.matmul
            pe.wait_ge(s_in, N_IN)

            def xw(c, first):
                pe.wait_ge(s_xT, c * 16 + 16)
                if not first:
                    pe.wait_ge(s_xw_copied, c)
                for i in range(CB):
                    last = mm(psflat[:, i * P:i * P + P], xT[:, i * P:i * P + P], w_gcn[:], start=True, stop=True)
                last.then_inc(s_xw, 1)
            xw(0, True)
            with pe.Fori(1, NCH) as c:
                xw(c, False)

            def deg(s, j, first, final):
                pe.wait_ge(s_hot, s + 1)
                for i in range(DEG_T):
                    last = mm(ps[:, 7, 0:NB], lo_hot[:, j, i, :], hi_hot[:, j, i, :],
                              start=first and i == 0, stop=final and i == DEG_T - 1)
                last.then_inc(s_deg, 1)
            deg(0, 0, True, False)
            deg(1, 1, False, False)
            with pe.Fori(1, DEG_STEPS // 2 - 1) as q:
                deg(q * 2, 0, False, False)
                deg(q * 2 + 1, 1, False, False)
            deg(DEG_STEPS - 2, 0, False, False)
            deg(DEG_STEPS - 1, 1, False, True)

            def group1(q, j, first):
                g = q * 2 + j
                pe.wait_ge(s_in1[j], q * 32 + 32)
                if not (first and j == 0):
                    pe.wait_ge(s_a1, g)
                for half in range(2):
                    last = mm(ps[:, 1, half * P:half * P + P], w1_bd[:, half, :], attr[:, j, :], start=True, stop=True)
                last.then_inc(s_l1, 1)
                pe.wait_ge(s_hot1, g + 1)
                pe.wait_ge(s_g1[j], q * (16 * TPG) + 16 * TPG)
                if not (first and j == 0):
                    pe.wait_ge(s_acc1, g)
                for t in range(TPG):
                    last = mm(ps[:, 0, 0:WIN], gath[:, j, t, :], onehot[:, j, t, :], start=t == 0, stop=t == TPG - 1)
                last.then_inc(s_sum1, 1)
                pe.wait_ge(s_a1, g + 1)
                if not (first and j == 0):
                    pe.wait_ge(s_a2, g)
                mm(ps[:, 2, 0:2 * P], w2_bd[:], h1[:], start=True, stop=True).then_inc(s_l2, 1)
                pe.wait_ge(s_a2, g + 1)
                if not (first and j == 0):
                    pe.wait_ge(s_rad, g)
                for t in (0, 2, 1, 3):
                    r, e = t // 2, t % 2 * P
                    last = mm(ps[:, 3 + r, e:e + P], w3_2[FC * r:FC * r + FC, :], h2[FC * r:FC * r + FC, e:e + P], start=True, stop=True)
                last.then_inc(s_l3, 1)
            for j in range(2):
                group1(0, j, True)
            with pe.Fori(1, NG // 2) as q:
                for j in range(2):
                    group1(q, j, False)

            with pe.Fori(0, NCH) as c:
                pe.wait_ge(s_stage, c + 1)
                for i in range(CB):
                    last = nc.tensor.transpose(psflat[:, i * P:i * P + P], stage[:, i * P:i * P + P], ident[:])
                last.then_inc(s_t1, 1)
                pe.wait_ge(s_x1, c + 1)
                for i in range(CB):
                    last = nc.tensor.transpose(psflat[:, 1024 + i * P:1024 + i * P + P], xc[:, i, :], ident[:])
                last.then_inc(s_t2, 1)
                pe.wait_ge(s_x1T, c + 1)
                for i in range(CB):
                    for n in range(2):
                        o = 2048 + 1024 * n + i * P
                        last = mm(psflat[:, o:o + P], x1T[:, i * P:i * P + P], w_sd[:, n * C:(n + 1) * C], start=True, stop=True)
                last.then_inc(s_mm, 1)

            def x_of(q, g, j):
                pe.wait_ge(s_g2[j], q * (16 * TPG) + 16 * TPG)
                pe.wait_ge(s_in2[j], q * 48 + 48)
                pe.wait_ge(s_hotT, g + 1)
                for t in range(TPG):
                    o = ps[:, j, t * P:t * P + P]
                    mm(o, gath[:, j, t, :], ident[:], start=True, stop=False)
                    last = mm(o, md_win[:, j, :], hotT[:, j, t * P:t * P + P], start=False, stop=True)
                last.then_inc(s_x, 1)

            def sep_of(g, j, first):
                pe.wait_ge(s_m, g + 1)
                if not (first and j == 0):
                    pe.wait_ge(s_held, g)
                    pe.wait_ge(s_pre, g)
                for t in range(TPG):
                    mm(ps[:, 3, t * P:t * P + P], msg[:, j, t * P:t * P + P], w_value[:], start=True, stop=True)
                mm(ps[:, 2, :], w_alpha[:], msg[:, j, :], start=True, stop=True).then_inc(s_sep, 1)

            def score_of(g, k, j):
                pe.wait_ge(s_u, g + 1)
                for t in range(TPG):
                    last = mm(ps[:, 4, ds(k * (2 * TPG * H) + (j * TPG + t) * H, H)], act_a[:, j, t * P:t * P + P], a_dot[:],
                              start=True, stop=True)
                last.then_inc(s_sc, 1)

            def agg_of(g, j, first):
                pe.wait_ge(s_v, g + 1)
                if not (first and j == 0):
                    pe.wait_ge(s_accd, g)
                for t in range(TPG):
                    mm(ps[:, 5, 0:WIN], wval[:, j, t * P:t * P + P], onehot[:, j, t, :], start=t == 0, stop=t == TPG - 1)
                for t in range(TPG):
                    last = mm(ps[:, 5, WIN:2 * WIN], wts[:, j, t * P:t * P + P], onehot[:, j, t, :],
                              start=t == 0, stop=t == TPG - 1)
                last.then_inc(s_agg, 1)

            def softmax_of(b):
                pe.wait_ge(s_sccopy, b + 1)
                for t in range(TPG):
                    last = nc.tensor.transpose(ps[0:GPS * H, 6, t * P:t * P + P], scores[:, t, :], ident[:])
                last.then_inc(s_turn, 1)
                pe.wait_ge(s_exp, b + 1)
                for t in range(TPG):
                    last = nc.tensor.transpose(ps[:, 6, t * GPS * H:(t + 1) * GPS * H], p_row[:, t * P:t * P + P], ident[0:GPS * H, 0:GPS * H])
                last.then_inc(s_back, 1)

            def pair2(b, k, first, sums, first_sums):
                q, g = b * PPS + k, b * GPS + k * 2
                for j in range(2):
                    x_of(q, g + j, j)
                for j in range(2):
                    if sums:
                        agg_of(g + (j - GPS), j, first_sums)
                    sep_of(g + j, j, first)
                for j in range(2):
                    score_of(g + j, k, j)

            pe.wait_ge(s_mso, NCH)
            pair2(0, 0, True, False, False)
            with pe.Fori(1, PPS) as k:
                pair2(0, k, False, False, False)
            softmax_of(0)
            pair2(1, 0, False, True, True)
            with pe.Fori(1, PPS) as k:
                pair2(1, k, False, True, False)
            softmax_of(1)
            with pe.Fori(2, NSB) as b:
                with pe.Fori(0, PPS) as k:
                    pair2(b, k, False, True, False)
                softmax_of(b)
            with pe.Fori(0, PPS) as k:
                for j in range(2):
                    agg_of(k * 2 + (j + (NSB - 1) * GPS), j, False)

            pe.wait_ge(s_const, 2)
            for n, src in enumerate((max_first, max_last)):
                for g in range(GPS):
                    last = mm(ps[:, n, g * NSB:(g + 1) * NSB], expand[:, g, :], src[:], start=True, stop=True)
            last.then_inc(s_mx, 1)
            with pe.Fori(0, NCH) as c:
                pe.wait_ge(s_o, c + 1)
                for i in range(CB):
                    last = mm(psflat[:, 1024 + i * P:1024 + i * P + P], stage[:, i * P:i * P + P], w_proj[:], start=True, stop=True)
                last.then_inc(s_pr, 1)

        @block.scalar
        def _(act):
            af = nc.scalar.activation

            with act.Fori(0, NCH) as c:
                act.wait_ge(s_xw, c + 1)
                nc.scalar.copy(g_nodes[:, ds(c * CB, CB), :].rearrange("p b c -> p (b c)"), psflat[:, 0:CC]).then_inc(s_xw_copied, 1)
            act.wait_ge(s_deg, DEG_STEPS)
            af(dis[:], ps[:, 7, 0:NB], ACT.Sqrt, bias=1.0).then_inc(s_sqrt, 1)

            def group1(q, j, first):
                g = q * 2 + j
                act.wait_ge(s_l1, g + 1)
                if not (first and j == 0):
                    act.wait_ge(s_l2, g)
                af(h1[:], ps[:, 1, 0:2 * P], ACT.Silu, bias=b1_2[:]).then_inc(s_a1, 1)
                act.wait_ge(s_l2, g + 1)
                if not (first and j == 0):
                    act.wait_ge(s_l3, g)
                af(h2[:], ps[:, 2, 0:2 * P], ACT.Silu, bias=b2_2[:]).then_inc(s_a2, 1)
            for j in range(2):
                group1(0, j, True)
            with act.Fori(1, NG // 2) as q:
                for j in range(2):
                    group1(q, j, False)

            def ln_sqrt(n):
                act.wait_ge(s_ln1, n)
                nc.scalar.sqrt(small[:, 8:8 + CB], small[:, 0:CB]).then_inc(s_ln2, 1)

            act.wait_ge(s_acc1, NG)
            def chunk3(c, first):
                if not first:
                    act.wait_ge(s_x1, c)
                nc.scalar.copy(stage[:], gcn_acc[:, ds(c * CC, CC)]).then_inc(s_stage, 1)
                ln_sqrt(c + 1)
                act.wait_ge(s_t2, c + 1)
                if not first:
                    act.wait_ge(s_mm, c)
                nc.scalar.copy(x1T[:], psflat[:, 1024:1024 + CC]).then_inc(s_x1T, 1)
                act.wait_ge(s_x1, c + 1)
                nc.scalar.copy(x1_nodes[:, ds(c * CB, CB), :], xc[:]).then_inc(s_x1c, 1)
                act.wait_ge(s_mm, c + 1)
                if not first:
                    act.wait_ge(s_tab, c * 32)
                nc.scalar.copy(md_out[:], psflat[:, 3072:3072 + CC].rearrange("p (b c) -> p b c", c=C)).then_inc(s_mdo, 1)
            chunk3(0, True)
            with act.Fori(1, NCH) as c:
                chunk3(c, False)

            def alpha_of(b, k, j, first_sb, first):
                g = b * GPS + k * 2 + j
                act.wait_ge(s_sep, g + 1)
                if not first:
                    act.wait_ge(s_u, g - 1)
                af(pre[:, j, :], ps[:, 2, :], ACT.Identity, bias=b_alpha[:])
                af(tanh[:, j, :], ps[:, 2, :], ACT.Tanh, bias=b_alpha_half[:], scale=0.5).then_inc(s_pre, 1)
                if not first_sb:
                    act.wait_ge(s_v, g - (GPS - 1))
                nc.scalar.copy(hold[:, ds(k * 2 + j, 1), :], ps[:, 3, :]).then_inc(s_held, 1)

            def accumulate(g, first):
                w = act.value_load(win_i[0:1, ds(g, 1)], min_val=0, max_val=NP - 1)
                act.wait_ge(s_agg, g + 1)
                if not first:
                    act.wait_ge(s_accd, g)
                sums = ps[:, 5, 0:2 * WIN].rearrange("p (a w) -> p a w", a=2)
                nc.scalar.copy(slot_prev[:, :, ds(g, 1)], acc[:, :, ds(w, 1)])
                nc.scalar.copy(slot_first[:, :, ds(g, 1)], sums[:, :, 0:1])
                nc.scalar.copy(acc[:, :, ds(w + 1, WIN - 1)], sums[:, :, 1:WIN]).then_inc(s_accd, 1)

            def exp_of(b):
                act.wait_ge(s_shift, b + 1)
                af(p_row[:], shifted[:], ACT.Exp).then_inc(s_exp, 1)

            def pair2(b, k, first_sb, first, sums, first_sums):
                for j in range(2):
                    if sums:
                        accumulate((b - 1) * GPS + k * 2 + j, first_sums and j == 0)
                    alpha_of(b, k, j, first_sb, first)

            act.wait_ge(s_prep, 1)
            act.wait_ge(s_zero, 1)
            pair2(0, 0, True, True, False, False)
            with act.Fori(1, PPS) as k:
                pair2(0, k, True, False, False, False)
            exp_of(0)
            pair2(1, 0, False, False, True, True)
            with act.Fori(1, PPS) as k:
                pair2(1, k, False, False, True, False)
            exp_of(1)
            with act.Fori(2, NSB) as b:
                with act.Fori(0, PPS) as k:
                    pair2(b, k, False, False, True, False)
                exp_of(b)
            with act.Fori(0, GPS) as k:
                accumulate(k + (NSB - 1) * GPS, False)

            for n in range(3):
                act.wait_ge(s_mxe, n + 1)
                af(mrg[9 + n][:], mrg[9 + n][:], ACT.Exp).then_inc(s_me, 1)
            with act.Fori(0, NCH) as c:
                ln_sqrt(c + (NCH + 1))

        @block.vector
        def _(dve):
            V = nc.vector
            tt, ts, stt = V.tensor_tensor, V.tensor_scalar, V.scalar_tensor_tensor
            own = [0]

            def chain(ins):
                own[0] += 1
                ins.then_inc(s_v_own, 1)
                dve.wait_ge(s_v_own, own[0])

            dve.wait_ge(s_in, N_IN)
            dve.wait_ge(s_const, 1)
            V.tensor_copy(iota_b[:], iota_i[:])
            V.tensor_copy(iota_f[:], iota_i[:])
            V.tensor_copy(part_f[:], part_i[:])
            V.tensor_copy(win_f[:], win_i[:])
            V.tensor_copy(last_f[:], last_i[:])
            V.tensor_copy(dst_rel[:], dst_i[:])
            ts(lo_i[:], dst_i[:], P - 1, None, ALU.bitwise_and)
            ts(b_alpha_half[:], b_alpha[:], 0.5, None, ALU.mult)
            ts(a_dot[:], a_dot[:], 0.4, None, ALU.mult)
            V.memset(neg_edge[:], -BIG)
            chain(ts(hi_i[:], dst_i[:], 7, None, ALU.arith_shift_right))
            V.tensor_copy(lo_b[:], lo_i[:])
            V.tensor_copy(hi_b[:], hi_i[:])
            ts(win_iota[:], win_f[:], part_f[:], None, ALU.add)
            chain(tt(dst_rel[:].rearrange("p (g t) -> p g t", t=TPG), dst_rel[:].rearrange("p (g t) -> p g t", t=TPG),
                     win_f[:].unsqueeze(2).broadcast_to([P, NG, TPG]), ALU.subtract))
            V.memset(gcn_acc, 0.0).then_inc(s_prep, 1)

            def hots(s, j, first):
                if not first:
                    dve.wait_ge(s_deg, s - 1)
                tt(lo_hot[:, j], iota_b[:].unsqueeze(1).broadcast_to([P, DEG_T, P]),
                   lo_b[:, ds(s * DEG_T, DEG_T)].unsqueeze(2).broadcast_to([P, DEG_T, P]), ALU.is_equal)
                tt(hi_hot[:, j], iota_b[:, 0:NB].unsqueeze(1).broadcast_to([P, DEG_T, NB]),
                   hi_b[:, ds(s * DEG_T, DEG_T)].unsqueeze(2).broadcast_to([P, DEG_T, NB]), ALU.is_equal).then_inc(s_hot, 1)
            for j in range(2):
                hots(j, j, True)
            with dve.Fori(1, DEG_STEPS // 2) as q:
                for j in range(2):
                    hots(q * 2 + j, j, False)
            dve.wait_ge(s_sqrt, 1)
            chain(V.reciprocal(dis[:], dis[:]))
            dve.wait_ge(s_xw_copied, NCH)
            tt(g_nodes, g_nodes, dis[:].unsqueeze(2).broadcast_to([P, NB, C]), ALU.mult).then_inc(s_g, 1)

            def make_onehot(g, j):
                return tt(onehot[:, j], iota_f[:, 0:WIN].unsqueeze(1).broadcast_to([P, TPG, WIN]),
                          dst_rel[:, ds(g * TPG, TPG)].unsqueeze(2).broadcast_to([P, TPG, WIN]), ALU.is_equal)

            def group1(q, j, first):
                g = q * 2 + j
                if not first:
                    dve.wait_ge(s_sum1, g - 1)
                make_onehot(g, j).then_inc(s_hot1, 1)
                w = dve.value_load(win_i[0:1, ds(g, 1)], min_val=0, max_val=NP - 1)
                if not (first and j == 0):
                    dve.wait_ge(s_acc1, g)
                dve.wait_ge(s_sum1, g + 1)
                window = gcn_acc[:, ds(w, WIN)]
                tt(window, window, ps[:, 0, 0:WIN], ALU.add).then_inc(s_acc1, 1)
                dve.wait_ge(s_l3, g + 1)
                if not first:
                    dve.wait_ge(s_st1[j], q * 16)
                halves = lambda z: z.rearrange("p (r e) -> p r e", r=2)
                stt(halves(mrad[:, j, :]), ps[:, 3:5, 0:2 * P], b3[:], halves(ea_row[:, j, :]), ALU.add, ALU.mult).then_inc(s_rad, 1)
            for j in range(2):
                group1(0, j, True)
            with dve.Fori(1, NG // 2) as q:
                for j in range(2):
                    group1(q, j, False)

            stat = small[:, 16:16 + CB]
            s_lo = s_ln_own

            def layer_norm(base, n, res):
                V.tensor_reduce(stat, y[:], AX.X, ALU.add).then_inc(s_lo, 1)
                dve.wait_ge(s_lo, base + 1)
                ts(stat, stat, 1.0 / C, None, ALU.mult).then_inc(s_lo, 1)
                dve.wait_ge(s_lo, base + 2)
                tt(y[:], y[:], stat.unsqueeze(2).broadcast_to([P, CB, C]), ALU.subtract).then_inc(s_lo, 1)
                dve.wait_ge(s_lo, base + 3)
                tt(y2[:], y[:], y[:], ALU.mult).then_inc(s_lo, 1)
                dve.wait_ge(s_lo, base + 4)
                V.tensor_reduce(small[:, 0:CB], y2[:], AX.X, ALU.add).then_inc(s_lo, 1)
                dve.wait_ge(s_lo, base + 5)
                ts(small[:, 0:CB], small[:, 0:CB], 1.0 / C, LN_EPS, ALU.mult, ALU.add).then_inc(s_ln1, 1)
                dve.wait_ge(s_ln2, n + 1)
                V.reciprocal(small[:, 24:24 + CB], small[:, 8:8 + CB]).then_inc(s_lo, 1)
                dve.wait_ge(s_lo, base + 6)
                return tt(res, y[:], small[:, 24:24 + CB].unsqueeze(2).broadcast_to([P, CB, C]), ALU.mult)

            def chunk3(c, first):
                base = c * 9
                dve.wait_ge(s_t1, c + 1)
                tt(y[:], psflat[:, 0:CC].rearrange("p (b c) -> p b c", c=C), g_nodes[:, ds(c * CB, CB), :], ALU.add).then_inc(s_lo, 1)
                dve.wait_ge(s_lo, base + 1)
                tt(y[:], y[:], dis[:, ds(c * CB, CB)].unsqueeze(2).broadcast_to([P, CB, C]), ALU.mult).then_inc(s_lo, 1)
                dve.wait_ge(s_xin, c * 16 + 16)
                tt(x_chunk[:], x_chunk[:], b_gcn[:].unsqueeze(1).broadcast_to([P, CB, C]), ALU.add).then_inc(s_lo, 1)
                dve.wait_ge(s_lo, base + 3)
                tt(y[:], y[:], x_chunk[:], ALU.add).then_inc(s_v_own2, 1)
                dve.wait_ge(s_v_own2, c + 1)
                if not first:
                    dve.wait_ge(s_x1c, c)
                    dve.wait_ge(s_t2, c)
                layer_norm(base + 3, c, xc[:]).then_inc(s_x1, 1)
                dve.wait_ge(s_mm, c + 1)
                if not first:
                    dve.wait_ge(s_tab, c * 32)
                tt(ms_out[:], psflat[:, 2048:2048 + CC].rearrange("p (b c) -> p b c", c=C),
                   b_src[:].unsqueeze(1).broadcast_to([P, CB, C]), ALU.add).then_inc(s_mso, 1)
            chunk3(0, True)
            with dve.Fori(1, NCH) as c:
                chunk3(c, False)
            dve.wait_ge(s_tab, 16 * (2 * NCH + 1))
            V.memset(acc[:], 0.0).then_inc(s_zero, 1)

            dve.wait_ge(s_mdo, NCH)

            def hotT_of(q, g, j):
                dve.wait_ge(s_in2[j], q * 48 + 48)
                ts(hotT[:, j, :], dst_row[:, j, :], win_iota[0:WIN, ds(g, 1)], None, ALU.is_equal).then_inc(s_hotT, 1)

            def msg_of(g, j):
                dve.wait_ge(s_x, g + 1)
                tt(msg[:, j, :], ps[:, j, :], mrad[:, j, :], ALU.mult).then_inc(s_m, 1)

            def act_of(g, j, first):
                dve.wait_ge(s_pre, g + 1)
                if not first:
                    dve.wait_ge(s_sc, g - 1)
                stt(act_a[:, j, :], tanh[:, j, :], 1.5, pre[:, j, :], ALU.add, ALU.mult).then_inc(s_u, 1)

            def values_of(g, k, j, first):
                dve.wait_ge(s_held, g + 1)
                if not first:
                    dve.wait_ge(s_agg, g - 1)
                make_onehot(g, j)
                V.tensor_copy(wts[:, j, :].rearrange("p (t h v) -> p t h v", t=TPG, h=H),
                              p_edge[:, :, ds(k * 2 + j, 1), :].rearrange("p t o h -> p t (o h)").unsqueeze(3).broadcast_to([P, TPG, H, K]))
                tt(wval[:, j, :].rearrange("p (t h v) -> p t h v", t=TPG, h=H),
                   hold[:, ds(k * 2 + j, 1), :].rearrange("p o (t h v) -> p (o t) h v", t=TPG, h=H),
                   p_edge[:, :, ds(k * 2 + j, 1), :].rearrange("p t o h -> p t (o h)").unsqueeze(3).broadcast_to([P, TPG, H, K]),
                   ALU.mult).then_inc(s_v, 1)

            n_sm = 7

            def softmax_of(b):
                dve.wait_ge(s_sc, b * GPS + GPS)
                V.tensor_copy(scores[:].rearrange("p t (g h) -> p g t h", g=GPS),
                              ps[:, 4, 0:GPS * TPG * H].rearrange("p (g t h) -> p g t h", g=GPS, t=TPG)).then_inc(s_sccopy, 1)
                dve.wait_ge(s_seg, b * 16 + 16)
                inner = neg_edge[:, 1:GE]
                tt(inner, seg_row[:, 1:GE], seg_row[:, 0:GE - 1], ALU.not_equal).then_inc(s_sm, 1)
                dve.wait_ge(s_sm, b * 4 + 1)
                ts(inner, inner, -BIG, None, ALU.mult).then_inc(s_sm, 1)
                dve.wait_ge(s_sm, b * 4 + 2)
                dve.wait_ge(s_turn, b + 1)
                turned = ps[0:GPS * H, 6, :]
                V.tensor_tensor_scan(fwd[:], neg_edge[:, 0:GE], turned, -BIG, ALU.add, ALU.max).then_inc(s_sm, 1)
                dve.wait_ge(s_sm, b * 4 + 3)
                V.tensor_tensor_scan(seg_max[:, ::-1], neg_edge[:, GE:0:-1], fwd[:, ::-1], -BIG, ALU.add, ALU.max).then_inc(s_sm, 1)
                dve.wait_ge(s_sm, b * 4 + 4)
                tt(shifted[:], turned, seg_max[:], ALU.subtract).then_inc(s_shift, 1)
                V.tensor_copy(max_first[:, ds(b, 1)], seg_max[:, 0:1])
                V.tensor_copy(max_last[:, ds(b, 1)], seg_max[:, GE - 1:GE]).then_inc(s_maxes, 1)
                dve.wait_ge(s_back, b + 1)
                flat = ps[:, 6, 0:TPG * GPS * H]
                V.tensor_copy(p_edge[:].rearrange("p t g h -> p (t g h)"), flat).then_inc(s_p, 1)
                dve.wait_ge(s_p, b + 1)

            def pair2(b, k, first, sums, first_sums):
                q, g = b * PPS + k, b * GPS + k * 2
                for j in range(2):
                    hotT_of(q, g + j, j)
                for j in range(2):
                    if sums:
                        values_of(g + (j - GPS), k, j, first_sums)
                    msg_of(g + j, j)
                for j in range(2):
                    act_of(g + j, j, first)

            pair2(0, 0, True, False, False)
            with dve.Fori(1, PPS) as k:
                pair2(0, k, False, False, False)
            softmax_of(0)
            pair2(1, 0, False, True, True)
            with dve.Fori(1, PPS) as k:
                pair2(1, k, False, True, False)
            softmax_of(1)
            with dve.Fori(2, NSB) as b:
                with dve.Fori(0, PPS) as k:
                    pair2(b, k, False, True, False)
                softmax_of(b)
            with dve.Fori(0, PPS) as k:
                for j in range(2):
                    values_of(k * 2 + (j + (NSB - 1) * GPS), k, j, False)

            cont, single, chained, fresh, m_f, m_l, m_tot, tmp, m_lt, e_first, e_last, e_chain = (m[:] for m in mrg)
            dve.wait_ge(s_accd, NG)
            dve.wait_ge(s_mx, 1)
            n1 = slice(1, NG)
            n0 = slice(0, NG - 1)
            V.memset(cont, 0.0)
            V.memset(chained, 0.0)
            V.memset(m_lt, -BIG)
            V.memset(e_last, 0.0)
            chain(V.memset(e_chain, 0.0))
            V.tensor_copy(m_f.rearrange("p (b g) -> p g b", g=GPS), ps[:, 0, 0:NG].rearrange("p (g b) -> p g b", b=NSB))
            V.tensor_copy(m_l.rearrange("p (b g) -> p g b", g=GPS), ps[:, 1, 0:NG].rearrange("p (g b) -> p g b", b=NSB))
            tt(single, win_f[:], last_f[:], ALU.is_equal)
            chain(tt(cont[:, n1], win_f[:, n1], last_f[:, n0], ALU.is_equal))
            chain(tt(chained[:, n1], cont[:, n1], single[:, n0], ALU.mult))
            chain(tt(fresh, cont, chained, ALU.subtract))
            chain(tt(m_lt[:, n1], m_l[:, n0], fresh[:, n1], ALU.mult))
            chain(ts(tmp, fresh, 1.0, BIG, ALU.subtract, ALU.mult))
            chain(tt(m_lt[:, n1], m_lt[:, n1], tmp[:, n1], ALU.add))
            chain(tt(m_lt, m_lt, m_f, ALU.max))
            chain(ts(tmp, chained, 1.0, BIG, ALU.subtract, ALU.mult))
            chain(V.tensor_tensor_scan(m_tot, tmp, m_lt, -BIG, ALU.add, ALU.max))
            tt(e_first, m_f, m_tot, ALU.subtract).then_inc(s_mxe, 1)
            chain(tt(e_last[:, n1], m_l[:, n0], m_tot[:, n1], ALU.subtract))
            ts(e_last, e_last, 0.0, None, ALU.min).then_inc(s_mxe, 1)
            chain(tt(e_chain[:, n1], m_tot[:, n0], m_tot[:, n1], ALU.subtract))
            ts(e_chain, e_chain, 0.0, None, ALU.min).then_inc(s_mxe, 1)
            dve.wait_ge(s_me, 3)
            tt(e_last, e_last, fresh, ALU.mult)
            chain(tt(e_chain, e_chain, chained, ALU.mult))
            chain(tt(slot_first[:], slot_first[:], e_first.unsqueeze(1).broadcast_to([P, 2, NG]), ALU.mult))
            chain(tt(slot_prev[:], slot_prev[:], e_last.unsqueeze(1).broadcast_to([P, 2, NG]), ALU.mult))
            chain(tt(mrg2[:], slot_first[:], slot_prev[:], ALU.add))
            for n in range(2):
                chain(V.tensor_tensor_scan(totals[:, n, :], e_chain, mrg2[:, n, :], 0.0, ALU.mult, ALU.add))
            def write_back(s):
                w = dve.value_load(win_i[0:1, ds(s, 1)], min_val=0, max_val=NP - 1)
                V.tensor_copy(acc[:, :, ds(w, 1)], totals[:, :, ds(s, 1)]).then_inc(s_wb, 1)
            write_back(0)
            with dve.Fori(1, NG) as s:
                dve.wait_ge(s_wb, s)
                write_back(s)
            dve.wait_ge(s_wb, NG)

            def chunk5(c, first):
                base = c * 11 + 9 * NCH
                lo = c * CC
                num, den = acc[:, 0, ds(lo, CC)], acc[:, 1, ds(lo, CC)]
                if not first:
                    dve.wait_ge(s_pr, c)
                    dve.wait_ge(s_y, c)
                t0, t1 = y2[:].rearrange("p b c -> p (b c)"), y[:].rearrange("p b c -> p (b c)")
                stt(t0, den, b_value[:], num, ALU.mult, ALU.add).then_inc(s_lo, 1)
                ts(t1, den, 1e-16, None, ALU.add).then_inc(s_lo, 1)
                dve.wait_ge(s_lo, base + 2)
                V.reciprocal(t1, t1).then_inc(s_lo, 1)
                dve.wait_ge(s_lo, base + 3)
                tt(stage[:], t0, t1, ALU.mult).then_inc(s_o, 1)
                dve.wait_ge(s_pr, c + 1)
                dve.wait_ge(s_o, c + 1)
                tt(y[:], psflat[:, 1024:1024 + CC].rearrange("p (b c) -> p b c", c=C), x1_nodes[:, ds(c * CB, CB), :], ALU.add).then_inc(s_lo, 1)
                dve.wait_ge(s_lo, base + 4)
                tt(y[:], y[:], b_proj[:].unsqueeze(1).broadcast_to([P, CB, C]), ALU.add).then_inc(s_lo, 1)
                dve.wait_ge(s_lo, base + 5)
                if not first:
                    dve.wait_ge(s_out, c * 16)
                layer_norm(base + 5, c + NCH, xc[:]).then_inc(s_y, 1)
            chunk5(0, True)
            with dve.Fori(1, NCH) as c:
                chunk5(c, False)


def kernel(**inputs):
    import concourse.bacc as bacc
    from concourse import mybir
    from concourse.bass_utils import run_bass_kernel_spmd

    v = {k: np.asarray(x) for k, x in inputs.items()}
    col = lambda x: np.ascontiguousarray(x.reshape(-1, 1))
    row = lambda x: np.ascontiguousarray(x.reshape(1, -1))
    pad = EP - N_EDGES
    src = np.concatenate([v["src"].astype(np.int32), np.zeros(pad, np.int32)])
    dst = np.concatenate([v["dst"].astype(np.int32), np.full(pad, NP - 1, np.int32)])
    ea = np.concatenate([v["edge_weight1"][:, 0], np.zeros(pad, np.float32)])
    attr = np.concatenate([v["edge_attr_32"], np.zeros((pad, RAD), np.float32)])
    x = np.concatenate([v["x"], np.zeros((NP - N_NODES, C), np.float32)])
    sep, b_sep = v["L1_gnn_w_sep"].reshape(C, H, 2, K), v["L1_gnn_b_sep"].reshape(H, 2, K)
    by_tile = lambda z: np.ascontiguousarray(z.reshape(NT, P).T)
    arrays = {
        "srcE": np.concatenate([by_tile(src), np.zeros((P, TPG), np.int32)], axis=1), "dstE": by_tile(dst),
        "dst_row": row(dst), "ea_row": row(ea), "first": dst[::GE].copy(), "last": dst[GE - 1::GE].copy(),
        "attrT": np.ascontiguousarray(attr.reshape(NG, TPG, P, RAD).transpose(1, 3, 0, 2).reshape(P, NG * P)),
        "xN": x, "xT": np.ascontiguousarray(x.T),
        "w_gcn": v["L0_gnn_W"], "b_gcn": v["L0_gnn_b"],
        "w_src": v["L1_gnn_w_src"], "b_src": v["L1_gnn_b_src"], "w_dst": v["L1_gnn_w_dst"],
        "fc_w1": v["L1_gnn_fc_w1"], "fc_b1": col(v["L1_gnn_fc_b1"]),
        "fc_w2": v["L1_gnn_fc_w2"], "fc_b2": col(v["L1_gnn_fc_b2"]),
        "fc_w3": v["L1_gnn_fc_w3"], "fc_b3": col(v["L1_gnn_fc_b3"]),
        "w_alpha": np.ascontiguousarray(sep[:, :, 0].reshape(C, P)), "w_value": np.ascontiguousarray(sep[:, :, 1].reshape(C, P)),
        "b_alpha": col(b_sep[:, 0]), "b_value": col(b_sep[:, 1]),
        "alpha_dot": col(v["L1_gnn_alpha_dot"]), "w_proj": v["L1_gnn_w_proj"], "b_proj": v["L1_gnn_b_proj"],
    }
    arrays = {k: np.ascontiguousarray(x) for k, x in arrays.items()}
    nc = bacc.Bacc("TRN2", target_bir_lowering=False, num_devices=1)
    aps = {k: nc.dram_tensor("in_" + k, x.shape, mybir.dt.from_np(x.dtype), kind="ExternalInput").ap() for k, x in arrays.items()}
    out = nc.dram_tensor("out_x", [NP, C], mybir.dt.float32, kind="ExternalOutput").ap()
    build(nc, aps, out)
    r = run_bass_kernel_spmd(nc, [{"in_" + k: x for k, x in arrays.items()}], core_ids=[0])
    return r.results[0]["out_x"][:N_NODES]
```

```python
import numpy as np
from contextlib import ExitStack

N_NODES, N_EDGES, C = 6250, 100000, 128
P = 128
NB = (N_NODES + P - 1) // P
NP = NB * P
GE = 512
TPG = GE // P
NG = (N_EDGES + GE - 1) // GE
EP = NG * GE
NT = EP // P
NSB, GPS = 14, 14
PPS = GPS // 2
WB = 7
WB_ACT, WB_DVE, WB_POOL = 11, 9, 8
WIN = 64
HOLD, LAG = 16, 17
NW = NP + WIN
CB = 7
NCH = NB // CB
CC = CB * P
H, K = 8, 16
RAD, FC = 32, 64
DEG_T = 14
DEG_STEPS = NT // DEG_T
HALF = NP // (NG // 2)
DP = NP * 8 // P
BIG = 1.0e30
LN_EPS = 1e-5
assert NSB * GPS == NG and NCH * CB == NB and DEG_STEPS * DEG_T == NT and HALF * (NG // 2) == NP and C % HALF == 0
assert (WB_ACT + WB_DVE + WB_POOL) * WB == NG and DP * P == NP * 8


def build(nc, a, out):
    import concourse.bass as bass
    from concourse import mybir

    f32, bf16, i32 = mybir.dt.float32, mybir.dt.bfloat16, mybir.dt.int32
    ALU, ACT, AX = mybir.AluOpType, mybir.ActivationFunctionType, mybir.AxisListType
    ds = bass.ds

    g_tab = nc.dram_tensor("g_tab", [NP, C], f32, kind="Internal").ap()
    ms_tab = nc.dram_tensor("ms_tab", [NP, C], f32, kind="Internal").ap()
    md_tab = nc.dram_tensor("md_tab", [NW, 3, C], bf16, kind="Internal").ap()
    rad_tab = nc.dram_tensor("rad_tab", [NG, P, GE], f32, kind="Internal").ap()

    top = ExitStack()
    sbuf = lambda name, shape, dt, st=top: st.enter_context(nc.sbuf_tensor(name, shape, dt))
    sem = lambda name: top.enter_context(nc.semaphore(name))

    with top:
        acc = sbuf("acc", [P, 2, NW], f32)
        g_nodes = acc[:, 1, 0:NP].rearrange("p (b c) -> p b c", c=C)
        x1_nodes = sbuf("x1_nodes", [P, NB, C], f32)
        hold = sbuf("hold", [P, HOLD, GE], f32)
        gcn_acc = hold[:].rearrange("p a b -> p (a b)")[:, 0:NW]
        ratio8 = hold[:].rearrange("p a b -> p (a b)")
        src_i = sbuf("src_i", [P, NT + TPG], i32)
        dst_rel = sbuf("dst_rel", [P, NT + 2 * TPG], f32)
        win_i = sbuf("win_i", [P, NG + 2], i32)
        win_f = sbuf("win_f", [P, NG + 2], f32)
        last_f = sbuf("last_f", [P, NG], f32)
        win_iota = sbuf("win_iota", [P, NG + 2], f32)
        iota_i = sbuf("iota_i", [P, P], i32)
        iota_f = sbuf("iota_f", [P, P], f32)
        part_i = sbuf("part_i", [P, 1], i32)
        part_f = sbuf("part_f", [P, 1], f32)
        part_w = sbuf("part_w", [P, 1], f32)
        ident = sbuf("ident", [P, P], f32)
        dis = sbuf("dis", [P, NB], f32)
        slot_first = sbuf("slot_first", [P, 2, NG], f32)
        slot_prev = sbuf("slot_prev", [P, 2, NG], f32)
        max_first = sbuf("max_first", [GPS * H, NSB], f32)
        max_last = sbuf("max_last", [GPS * H, NSB], f32)
        idx = sbuf("idx", [P, 4 * TPG], i32)
        gath = sbuf("gath", [P, 4, TPG, C], f32)
        onehot = sbuf("onehot", [P, 2, TPG, WIN], f32)
        mrad = sbuf("mrad", [P, 2, GE], f32)
        w_gcn = sbuf("w_gcn", [P, C], f32)
        w_sd = sbuf("w_sd", [P, 2 * C], f32)
        w1_bd = sbuf("w1_bd", [P, 2, P], f32)
        w2_bd = sbuf("w2_bd", [P, P], f32)
        w3_2 = sbuf("w3_2", [P, C], f32)
        w_alpha = sbuf("w_alpha", [P, P], f32)
        w_value = sbuf("w_value", [P, P], f32)
        a_dot = sbuf("a_dot", [P, H], f32)
        w_proj = sbuf("w_proj", [P, C], f32)
        b_gcn, b_src, b_proj = (sbuf(n, [P, C], f32) for n in ("b_gcn", "b_src", "b_proj"))
        b1_2, b2_2, b3, b_alpha, b_alpha_half, b_value = (sbuf(n, [P, 1], f32) for n in (
            "b1_2", "b2_2", "b3", "b_alpha", "b_alpha_half", "b_value"))
        neg_edge = sbuf("neg_edge", [GPS * H, GE + 1], f32)
        h_to_hv = sbuf("h_to_hv", [H, P], f32)
        bv_to_hv = sbuf("bv_to_hv", [H, P], f32)
        hv_to_h = sbuf("hv_to_h", [P, H], f32)
        ones_row = sbuf("ones_row", [1, P], f32)
        marks = sbuf("marks", [P, 4], f32)
        zeros = sbuf("zeros", [WIN, 3, C], bf16)

        with ExitStack() as st:
            dst_i = sbuf("dst_i", [P, NT], i32, st)
            lo_i, hi_i = (sbuf(n, [P, NT], i32, st) for n in ("lo_i", "hi_i"))
            lo_b = sbuf("lo_b", [P, NT], bf16, st)
            iota_rep = sbuf("iota_rep", [P, P, DEG_T], bf16, st)
            hi_b = sbuf("hi_b", [P, NT], bf16, st)
            last_i = sbuf("last_i", [P, NG], i32, st)
            lo_hot = sbuf("lo_hot", [P, 2, P, DEG_T], bf16, st)
            hi_hot = sbuf("hi_hot", [P, 2, NB, DEG_T], bf16, st)
            xT = sbuf("xT", [P, CC], f32, st)
            attr = sbuf("attr", [P, 2, P], f32, st)
            ea_row = sbuf("ea_row", [P, 2, GE], f32, st)
            h1 = sbuf("h1", [P, 2 * P], f32, st)
            h2 = sbuf("h2", [P, 2 * P], f32, st)
        with ExitStack() as st:
            stage = sbuf("stage", [P, CC], f32, st)
            y = sbuf("y", [P, CB, C], f32, st)
            bn = sbuf("bn", [P, CB, 6], f32, st)
            mean_var = sbuf("mean_var", [P, CB, 2], f32, st)
            std, rstd, shift = (sbuf(n, [P, CB], f32, st) for n in ("std", "rstd", "shift"))
            with ExitStack() as st3:
                xc = sbuf("xc", [P, CB, C], f32, st3)
                x1T = sbuf("x1T", [P, CC], f32, st3)
                ms_out = sbuf("ms_out", [P, 2, CB, C], f32, st3)
                md_rest = sbuf("md_rest", [P, CB, C], f32, st3)
                md_parts = sbuf("md_parts", [P, 2, CB, 3, C], bf16, st3)
            with ExitStack() as st5:
                scaled = sbuf("scaled", [P, CC], f32, st5)
                out_c = sbuf("out_c", [P, 2, CB, C], f32, st5)
                expand = sbuf("expand", [GPS * H, GPS, P], f32, st5)
                mrg = [sbuf(f"merge_{n}", [P, NG], f32, st5) for n in range(12)]
                mrg2 = sbuf("mrg2", [P, 2, NG], f32, st5)
                totals = sbuf("totals", [P, 2, NG], f32, st5)
                den_p = sbuf("den_p", [P, 3, DP], f32, st5)
        with ExitStack() as st:
            dst_row = sbuf("dst_row", [P, 2, GE], i32, st)
            md_hm = sbuf("md_hm", [P, 2, C], bf16, st)
            md_lz = sbuf("md_lz", [P, 2, C], bf16, st)
            hotT = sbuf("hotT", [P, 2, GE], bf16, st)
            msg = sbuf("msg", [P, 2, GE], f32, st)
            pre = sbuf("pre", [P, 2, GE], f32, st)
            tanh = sbuf("tanh", [P, 2, GE], f32, st)
            act_a = sbuf("act_a", [P, 2, GE], f32, st)
            wval = sbuf("wval", [P, 2, GE], f32, st)
            wts = sbuf("wts", [P, 2, TPG, H], f32, st)
            scores = sbuf("scores", [P, TPG, GPS * H], f32, st)
            seg_row = sbuf("seg_row", [GPS * H, GE], i32, st)
            fwd = sbuf("fwd", [GPS * H, GE], f32, st)
            seg_max = sbuf("seg_max", [GPS * H, GE], f32, st)
            shifted = sbuf("shifted", [GPS * H, GE], f32, st)
            p_row = sbuf("p_row", [GPS * H, GE], f32, st)
            p_edge = sbuf("p_edge", [P, TPG, GPS, H], f32, st)

        ps = top.enter_context(nc.psum_tensor("psum", [P, 8, 512], f32))
        psflat = ps[:].rearrange("p b n -> p (b n)")

        s_in = sem("s_inputs_loaded")
        s_const = sem("s_pool_constants")
        s_prep = sem("s_vector_prepared")
        s_xT = sem("s_xT_loaded")
        s_xw = sem("s_xw_product")
        s_xw_copied = sem("s_xw_copied")
        s_hot = sem("s_degree_onehots")
        s_in0, s_w0 = sem("s_dst_loaded"), sem("s_w_gcn_loaded")
        s_deg = sem("s_degree_products")
        s_sqrt, s_dis, s_g = sem("s_degree_sqrt"), sem("s_dis"), sem("s_g")
        s_gtab = sem("s_g_table_stored")
        s_idx = sem("s_indices_copied")
        s_g1 = [sem(f"s_pass1_rows_{j}") for j in range(4)]
        s_in1, s_ea = ([sem(f"s_{n}_{j}") for j in range(2)] for n in ("features_loaded", "edge_weights_loaded"))
        s_st1 = [sem(f"s_radial_stored_{j}") for j in range(2)]
        s_hot1, s_sum1, s_acc1 = sem("s_onehot1"), sem("s_sum1"), sem("s_acc1")
        s_l1, s_a1, s_l2, s_a2, s_l3, s_rad = (sem(n) for n in (
            "s_mlp1", "s_silu1", "s_mlp2", "s_silu2", "s_mlp3", "s_radial"))
        s_stage, s_t1, s_xin, s_x1, s_t2, s_x1T, s_mm, s_mso, s_mdo, s_mdp, s_x1c = (sem(n) for n in (
            "s_staged", "s_sums_turned", "s_x_chunk", "s_x1_chunk", "s_x1_turned", "s_x1T",
            "s_tables_product", "s_ms_ready", "s_md_ready", "s_md_parts", "s_x1_kept"))
        s_mst, s_mdt, s_padded = sem("s_ms_table_stored"), sem("s_md_table_stored"), sem("s_md_table_padded")
        s_zero = sem("s_acc_zeroed")
        s_ln1, s_ln2 = sem("s_ln_variance"), sem("s_ln_sqrt")
        s_g2 = [sem(f"s_pass2_rows_{j}") for j in range(2)]
        s_dst2, s_md2, s_rad2 = ([sem(f"s_{n}_loaded_{j}") for j in range(2)] for n in ("dst_row", "md_rows", "radial"))
        s_hotT, s_x, s_m, s_sepa, s_sepv, s_pre, s_held, s_u, s_sc = (sem(n) for n in (
            "s_hotT", "s_msg_sum", "s_msg", "s_alpha", "s_value", "s_pre", "s_held", "s_act", "s_scores"))
        s_v, s_agg, s_accd = sem("s_weighted"), sem("s_aggregated"), sem("s_accumulated")
        s_seg, s_sccopy, s_turn, s_shift, s_exp, s_back, s_p = (sem(n) for n in (
            "s_segment_rows", "s_scores_copied", "s_scores_turned", "s_shifted", "s_exp", "s_p_turned", "s_p"))
        s_mx, s_mxe, s_me, s_tot, s_wb = (sem(n) for n in (
            "s_max_product", "s_merge_shift", "s_merge_exp", "s_totals", "s_written_back"))
        s_o, s_pr, s_y, s_out = sem("s_o"), sem("s_projected"), sem("s_y_ready"), sem("s_out_stored")
        s_sm, s_maxes = sem("s_softmax_steps"), sem("s_group_maxima")
        s_stats_seen, s_store_seen = sem("s_stats_seen"), sem("s_store_seen")
        s_slot, s_part = sem("s_slot_seen_free"), sem("s_part_steps")
        s_norm, s_ln3, s_ysum, s_hi, s_mid, s_mdr, s_packed, s_inv, s_unpacked, s_spread, s_scaled, s_totals = (sem(n) for n in (
            "s_norm_steps", "s_ln_scales", "s_y_summed", "s_md_high_part", "s_md_middle_part", "s_md_rest", "s_weights_packed",
            "s_weights_inverted", "s_weights_unpacked", "s_weights_spread", "s_scaled", "s_totals_ready"))
        s_v_own, s_a_own, s_p_own = sem("s_vector_own"), sem("s_scalar_own"), sem("s_pool_own")

        block = top.enter_context(nc.Block())
        N_IN = 0
        bcast = lambda ap, n: ap.partition_broadcast(n)

        loads = [
            (src_i[:], a["srcE"]),
            (win_i[:], a["first"].partition_broadcast(P)), (last_i[:], a["last"].partition_broadcast(P)),
            (w_sd[:, 0:C], a["w_src"]), (w_sd[:, C:2 * C], a["w_dst"]),
            (w3_2[0:FC, :], a["fc_w3"]), (w3_2[FC:2 * FC, :], a["fc_w3"]),
            (w_alpha[:], a["w_alpha"]), (w_value[:], a["w_value"]), (w_proj[:], a["w_proj"]),
            (b_gcn[:], a["b_gcn"].partition_broadcast(P)), (b_src[:], a["b_src"].partition_broadcast(P)),
            (b_proj[:], a["b_proj"].partition_broadcast(P)),
            (b1_2[0:FC, :], a["fc_b1"]), (b1_2[FC:2 * FC, :], a["fc_b1"]),
            (b2_2[0:FC, :], a["fc_b2"]), (b2_2[FC:2 * FC, :], a["fc_b2"]),
            (bv_to_hv[:], a["b_value"].rearrange("p o -> o p").broadcast_to([H, P])), (x1_nodes[:], a["xN"].rearrange("(b p) c -> p b c", p=P)),
            (b3[:], a["fc_b3"]), (b_alpha[:], a["b_alpha"]), (b_value[:], a["b_value"]),
        ]
        placed = [(w1_bd[RAD * t:RAD * t + RAD, t % 2, FC * (t // 2):FC * (t // 2) + FC], a["fc_w1"]) for t in range(4)]
        placed += [(w2_bd[FC * t:FC * t + FC, FC * t:FC * t + FC], a["fc_w2"]) for t in range(2)]
        placed += [(a_dot[K * h:K * h + K, h:h + 1], a["alpha_dot"][K * h:K * h + K, :]) for h in range(H)]
        N_IN = 16 * (len(loads) + len(placed))

        def node_rows(tab, c):
            return tab[0:NP, :].rearrange("(b p) c -> p b c", p=P)[:, ds(c * CB, CB), :]

        def wait_past(eng, sem_, n):
            if not (isinstance(n, int) and n <= 0):
                eng.wait_ge(sem_, n)

        def write_back(eng, copy, first, end):
            with eng.Fori(first, end) as i:
                at = [eng.value_load(win_i[0:1, ds(i * WB + n, 1)], min_val=0, max_val=NP - 1) for n in range(WB)]
                for n in range(WB):
                    copy(acc[:, :, ds(at[n], 1)], totals[:, :, ds(i * WB + n, 1)])

        def all_steps4(eng, step):
            def pairs(b, first, end, *parts):
                with eng.Fori(first, end) as pair:
                    for j in range(2):
                        step(b, pair * 2 + j, pair, j, *parts)

            for k in range(4):
                step(0, k, k // 2, k % 2, True, k >= 1, k >= 2, False, None)
            pairs(0, 2, PPS, True, True, True, False, None)
            for k in range(6):
                step(1, k, k // 2, k % 2, True, True, True, k >= LAG - GPS, k if k < 4 else None)
            pairs(1, 3, PPS, True, True, True, True, None)
            with eng.Fori(2, NSB) as b:
                for k in range(4):
                    step(b, k, k // 2, k % 2, True, True, True, True, k)
                pairs(b, 2, PPS, True, True, True, True, None)
            for k in range(4):
                step(NSB, k, k // 2, k % 2, False, k < 1, k < 2, True, k)
            pairs(NSB, 2, LAG // 2, False, False, False, True, None)
            step(NSB, LAG - 1, LAG // 2, 0, False, False, False, True, None)

        @block.sync
        def _(sp):
            sp.dma_start(dst_i[:], a["dstE"]).then_inc(s_in0, 16)
            sp.dma_start(w_gcn[:], a["w_gcn"]).then_inc(s_w0, 16)
            sp.dma_start(xT[:], a["xT"][:, 0:CC]).then_inc(s_xT, 16)
            for dst, src in loads:
                sp.dma_start(dst, src).then_inc(s_in, 16)
            sp.wait_ge(s_const, 1)
            for dst, src in placed:
                sp.dma_start(dst, src).then_inc(s_in, 16)
            with sp.Fori(1, NCH) as c:
                sp.wait_ge(s_xw, c)
                sp.dma_start(xT[:], a["xT"][:, ds(c * CC, CC)]).then_inc(s_xT, 16)
            sp.wait_ge(s_g, 1)
            sp.dma_start(g_tab.rearrange("(b p) c -> p b c", p=P), g_nodes).then_inc(s_gtab, 16)

            def load_attr(g, j):
                sp.dma_start(attr[:, j, :], a["attrT"][:, ds(g * P, P)]).then_inc(s_in1[j], 16)

            def load_ea(g, j):
                sp.dma_start(ea_row[:, j, :], a["ea_row"][:, ds(g * GE, GE)].partition_broadcast(P)).then_inc(s_ea[j], 16)

            def store1(g, j):
                sp.wait_ge(s_rad, g + 1)
                sp.dma_start(rad_tab[ds(g, 1), :, :], mrad[:, j, :]).then_inc(s_st1[j], 16)

            for j in range(2):
                load_attr(j, j)
                load_ea(j, j)
            with sp.Fori(0, NG // 2 - 1) as q:
                for j in range(2):
                    sp.wait_ge(s_l1, q * 2 + (j + 1))
                    load_attr(q * 2 + (j + 2), j)
                    store1(q * 2 + j, j)
                    load_ea(q * 2 + (j + 2), j)
            for j in range(2):
                store1(NG - 2 + j, j)

            sp.dma_start(md_tab[NP:NW], zeros[:]).then_inc(s_padded, 16)
            def tables(c):
                sp.wait_ge(s_mso, c + 1)
                sp.sem_inc(s_store_seen, 1)
                wait_past(sp, s_mst, c * 16)
                sp.dma_start(node_rows(ms_tab, c), ms_out[:, ds(c % 2, 1)].rearrange("p o b c -> p (o b) c")).then_inc(s_mst, 16)
                sp.wait_ge(s_mdp, c + 1)
                sp.sem_inc(s_store_seen, 1)
                wait_past(sp, s_mdt, c * 16)
                sp.dma_start(md_tab[0:NP].rearrange("(b p) n c -> p b (n c)", p=P)[:, ds(c * CB, CB), :],
                             md_parts[:, ds(c % 2, 1)].rearrange("p o b n c -> p (o b) (n c)")).then_inc(s_mdt, 16)
            tables(0)
            with sp.Fori(1, NCH) as c:
                tables(c)
            sp.wait_ge(s_mst, 16 * NCH)
            sp.wait_ge(s_mdt, 16 * NCH)
            sp.wait_ge(s_padded, 16)
            for j in range(2):
                sp.wait_ge(s_st1[j], 16 * (NG // 2))

            def load_dst(g, j):
                sp.dma_start(dst_row[:, j, :], a["dst_row"][:, ds(g * GE, GE)].partition_broadcast(P)).then_inc(s_dst2[j], 16)

            def load_md(g, j):
                w = sp.value_load(win_i[0:1, ds(g, 1)], min_val=0, max_val=NP - 1)
                sp.dma_start(md_hm[:, j, :], md_tab[ds(w, WIN), 0:2, :].rearrange("r n c -> n r c")).then_inc(s_md2[j], 16)
                sp.dma_start(md_lz[0:WIN, j, :], md_tab[ds(w, WIN), 2, :]).then_inc(s_md2[j], 16)

            def load_rad(g, j):
                sp.dma_start(mrad[:, j, :], rad_tab[ds(g, 1), :, :]).then_inc(s_rad2[j], 16)

            def next_loads(g, j):
                sp.wait_ge(s_hotT, g + 1)
                load_dst(g + 2, j)
                sp.wait_ge(s_x, g + 1)
                load_md(g + 2, j)
                sp.wait_ge(s_m, g + 1)
                load_rad(g + 2, j)

            def seg_load(b):
                rows = a["dst_row"][:, ds(b * (GPS * GE), GPS * GE)].rearrange("o (g e) -> g o e", g=GPS)
                sp.dma_start(seg_row[:], rows.broadcast_to([GPS, H, GE])).then_inc(s_seg, 16)

            for j in range(2):
                load_dst(j, j)
                load_md(j, j)
                load_rad(j, j)
            seg_load(0)
            with sp.Fori(0, PPS) as k:
                for j in range(2):
                    next_loads(k * 2 + j, j)
            with sp.Fori(1, NSB - 1) as b:
                with sp.Fori(0, 2) as k:
                    for j in range(2):
                        next_loads(b * GPS + k * 2 + j, j)
                sp.wait_ge(s_shift, b)
                seg_load(b)
                with sp.Fori(2, PPS) as k:
                    for j in range(2):
                        next_loads(b * GPS + k * 2 + j, j)
            with sp.Fori(0, 2) as k:
                for j in range(2):
                    next_loads(k * 2 + (j + (NSB - 1) * GPS), j)
            sp.wait_ge(s_shift, NSB - 1)
            seg_load(NSB - 1)
            with sp.Fori(2, PPS - 1) as k:
                for j in range(2):
                    next_loads(k * 2 + (j + (NSB - 1) * GPS), j)
            for j in range(2):
                sp.wait_ge(s_hotT, NG - 1 + j)
                load_dst(NG + j, j)

            packed = lambda ap: ap.rearrange("h (i n) -> h i n", n=DP)
            sp.wait_ge(s_wb, 3)
            sp.dma_start(den_p[:, 0, :], packed(acc[0:H, 1, 0:NP])).then_inc(s_packed, 16)
            sp.wait_ge(s_inv, 1)
            sp.dma_start(packed(acc[0:H, 1, 0:NP]), den_p[:, 1, :]).then_inc(s_unpacked, 16)
            sp.dma_start(packed(ratio8[0:H, 0:NP]), den_p[:, 2, :]).then_inc(s_unpacked, 16)

            def result(c):
                sp.wait_ge(s_y, c + 1)
                sp.sem_inc(s_store_seen, 1)
                wait_past(sp, s_out, c * 16)
                sp.dma_start(node_rows(out, c), out_c[:, ds(c % 2, 1)].rearrange("p o b c -> p (o b) c")).then_inc(s_out, 16)
            result(0)
            with sp.Fori(1, NCH) as c:
                result(c)
            sp.wait_ge(s_out, 16 * NCH)

        @block.gpsimd
        def _(pool):
            for m in (w1_bd, w2_bd, a_dot, ident, marks):
                nc.gpsimd.memset(m[:], 0.0)
            nc.gpsimd.memset(ones_row[:], 1.0)
            for m in (h_to_hv, hv_to_h):
                last = nc.gpsimd.memset(m[:], 0.0)
            last.then_inc(s_p_own, 1)
            pool.wait_ge(s_p_own, 1)
            nc.gpsimd.affine_select(out=ident[:], in_=ident[:], compare_op=ALU.not_equal, fill=1.0, base=0,
                                    pattern=[[-1, P]], channel_multiplier=1)
            nc.gpsimd.affine_select(out=h_to_hv[:].rearrange("p (h v) -> p h v", h=H), in_=h_to_hv[:].rearrange("p (h v) -> p h v", h=H),
                                    compare_op=ALU.not_equal, fill=1.0, base=0, pattern=[[-1, H], [0, K]], channel_multiplier=1)
            nc.gpsimd.affine_select(out=hv_to_h[:], in_=hv_to_h[:], compare_op=ALU.not_equal, fill=1.0, base=0,
                                    pattern=[[-K, H]], channel_multiplier=1)
            nc.gpsimd.memset(zeros[:], 0.0)
            nc.gpsimd.iota(iota_i[:], pattern=[[1, P]], base=0, channel_multiplier=0)
            nc.gpsimd.iota(part_i[:], pattern=[[0, 1]], base=0, channel_multiplier=1).then_inc(s_const, 1)

            def gathers(tab, sems, used, copies_before):
                R = len(sems)

                def copy_list(g, n):
                    nc.gpsimd.tensor_copy(idx[:, n * TPG:(n + 1) * TPG], src_i[:, ds(g * TPG, TPG)]).then_inc(s_idx, 1)

                def arrived(i, m):
                    return i * (16 * TPG * 4 // R) + 16 * TPG * (m // R + 1)

                def step(i, first):
                    for n in range(4):
                        m = (n + 1) % 4
                        if not first or n == 3:
                            pool.wait_ge(sems[m % R], arrived(i if n == 3 else i - 1, m))
                            pool.sem_inc(s_slot, 1)
                        copy_list(i * 4 + (n + 1), m)
                        pool.wait_ge(s_idx, i * 4 + (n + 1 + copies_before))
                        pool.sem_inc(s_slot, 1)
                        if not (first and n < R):
                            pool.wait_ge(used, i * 4 + (n + 1 - R))
                            pool.sem_inc(s_slot, 1)
                        for t in range(TPG):
                            pool.indirect_dma_start(gath[:, n % R, t, :], None, tab,
                                                    bass.IndirectOffsetOnAxis(idx[:, n * TPG + t:n * TPG + t + 1], 0)
                                                    ).then_inc(sems[n % R], 16)
                copy_list(0, 0)
                step(0, True)
                with pool.Fori(1, NG // 4) as i:
                    step(i, False)

            pool.wait_ge(s_in, N_IN)
            pool.wait_ge(s_gtab, 16)
            gathers(g_tab, s_g1, s_sum1, 0)

            def keep(c):
                pool.wait_ge(s_x1, c + 1)
                pool.sem_inc(s_slot, 1)
                nc.gpsimd.tensor_copy(x1_nodes[:, ds(c * CB, CB), :], xc[:]).then_inc(s_x1c, 1)

            def last_part(c):
                pool.wait_ge(s_mid, c + 1)
                pool.sem_inc(s_slot, 1)
                parts = lambda n: md_parts[:, ds(c % 2, 1), :, n].rearrange("p o b c -> p (o b) c")
                nc.gpsimd.tensor_tensor(md_rest[:], md_rest[:], parts(1), ALU.subtract).then_inc(s_part, 1)
                pool.wait_ge(s_part, c + 1)
                pool.sem_inc(s_slot, 1)
                nc.gpsimd.tensor_copy(parts(2), md_rest[:]).then_inc(s_mdp, 1)
            keep(0)
            with pool.Fori(1, NCH) as c:
                keep(c)
                last_part(c - 1)
            last_part(NCH - 1)
            pool.wait_ge(s_mst, 16 * NCH)
            for j in range(4):
                pool.wait_ge(s_g1[j], 4 * TPG * NG)
            pool.wait_ge(s_idx, NG + 1)
            gathers(ms_tab, s_g2, s_x, NG + 1)
            pool.wait_ge(s_accd, NG)
            nc.gpsimd.memset(expand[:], 0.0).then_inc(s_p_own, 1)
            pool.wait_ge(s_p_own, 2)
            nc.gpsimd.affine_select(out=expand[:].rearrange("p g (h v) -> p g h v", h=H), in_=expand[:].rearrange("p g (h v) -> p g h v", h=H),
                                    compare_op=ALU.not_equal, fill=1.0, base=0,
                                    pattern=[[-H, GPS], [-1, H], [0, K]], channel_multiplier=1).then_inc(s_const, 1)
            pool.wait_ge(s_tot, 1)
            write_back(pool, nc.gpsimd.tensor_copy, WB_ACT + WB_DVE, WB_ACT + WB_DVE + WB_POOL)
            nc.gpsimd.tensor_copy(marks[:, 2:3], marks[:, 3:4]).then_inc(s_wb, 1)

        @block.tensor
        def _(pe):
            mm = nc.tensor.matmul
            pe.wait_ge(s_w0, 16)

            def xw(c, first):
                pe.wait_ge(s_xT, c * 16 + 16)
                if not first:
                    pe.wait_ge(s_xw_copied, c)
                for i in range(CB):
                    last = mm(psflat[:, i * P:i * P + P], xT[:, i * P:i * P + P], w_gcn[:], start=True, stop=True)
                last.then_inc(s_xw, 1)
            xw(0, True)
            with pe.Fori(1, NCH) as c:
                xw(c, False)

            def deg(s, j, first, final):
                pe.wait_ge(s_hot, s + 1)
                for i in range(DEG_T):
                    last = mm(ps[:, 7, 0:NB], lo_hot[:, j, :, i], hi_hot[:, j, :, i],
                              start=first and i == 0, stop=final and i == DEG_T - 1)
                last.then_inc(s_deg, 1)
            deg(0, 0, True, False)
            deg(1, 1, False, False)
            with pe.Fori(1, DEG_STEPS // 2 - 1) as q:
                deg(q * 2, 0, False, False)
                deg(q * 2 + 1, 1, False, False)
            deg(DEG_STEPS - 2, 0, False, False)
            deg(DEG_STEPS - 1, 1, False, True)

            pe.wait_ge(s_in, N_IN)

            def l3(g):
                pe.wait_ge(s_a2, g + 1)
                if not (isinstance(g, int) and g == 0):
                    pe.wait_ge(s_rad, g)
                for t in (0, 2, 1, 3):
                    r, e = t // 2, t % 2 * P
                    last = mm(ps[:, 3 + r, e:e + P], w3_2[FC * r:FC * r + FC, :], h2[FC * r:FC * r + FC, e:e + P], start=True, stop=True)
                last.then_inc(s_l3, 1)

            def group1(i, n, first):
                g, j = i * 4 + n, n % 2
                start = first and n == 0
                pe.wait_ge(s_in1[j], i * 32 + (n // 2 * 16 + 16))
                if not start:
                    pe.wait_ge(s_a1, g)
                for half in range(2):
                    last = mm(ps[:, 1, half * P:half * P + P], w1_bd[:, half, :], attr[:, j, :], start=True, stop=True)
                last.then_inc(s_l1, 1)
                if not start:
                    l3(g - 1)
                pe.wait_ge(s_a1, g + 1)
                mm(ps[:, 2, 0:2 * P], w2_bd[:], h1[:], start=True, stop=True).then_inc(s_l2, 1)
                pe.wait_ge(s_hot1, g + 1)
                pe.wait_ge(s_g1[n], i * (16 * TPG) + 16 * TPG)
                if not start:
                    pe.wait_ge(s_acc1, g)
                for t in range(TPG):
                    last = mm(ps[:, 0, 0:WIN], gath[:, n, t, :], onehot[:, j, t, :], start=t == 0, stop=t == TPG - 1)
                last.then_inc(s_sum1, 1)
            for n in range(4):
                group1(0, n, True)
            with pe.Fori(1, NG // 4) as i:
                for n in range(4):
                    group1(i, n, False)
            l3(NG - 1)

            def turn_sums(c):
                pe.wait_ge(s_stage, c + 1)
                wait_past(pe, s_ysum, c)
                for i in range(CB):
                    last = nc.tensor.transpose(psflat[:, i * P:i * P + P], stage[:, i * P:i * P + P], ident[:])
                last.then_inc(s_t1, 1)

            def tables(c):
                pe.wait_ge(s_x1, c + 1)
                for i in range(CB):
                    last = nc.tensor.transpose(psflat[:, 1024 + i * P:1024 + i * P + P], xc[:, i, :], ident[:])
                last.then_inc(s_t2, 1)
                pe.wait_ge(s_x1T, c + 1)
                wait_past(pe, s_mdr, c)
                for i in range(CB):
                    for n in range(2):
                        o = 2048 + 1024 * n + i * P
                        last = mm(psflat[:, o:o + P], x1T[:, i * P:i * P + P], w_sd[:, n * C:(n + 1) * C], start=True, stop=True)
                last.then_inc(s_mm, 1)
            turn_sums(0)
            with pe.Fori(1, NCH) as c:
                turn_sums(c)
                tables(c - 1)
            tables(NCH - 1)

            def x_of(g, q, j):
                pe.wait_ge(s_g2[j], q * (16 * TPG) + 16 * TPG)
                pe.wait_ge(s_md2[j], q * 32 + 32)
                pe.wait_ge(s_hotT, g + 1)
                mm(ps[:, j, :], md_hm[:, j, :], hotT[:, j, :], start=True, stop=False)
                mm(ps[:, j, :], md_lz[:, j, :], hotT[:, j, :], start=False, stop=False)
                for t in range(TPG):
                    last = mm(ps[:, j, t * P:t * P + P], gath[:, j, t, :], ident[:], is_transpose=True, start=False, stop=t == TPG - 1)
                last.then_inc(s_x, 1)

            def sep_of(g, j):
                pe.wait_ge(s_m, g + 1)
                wait_past(pe, s_pre, g)
                mm(ps[:, 2, :], w_alpha[:], msg[:, j, :], start=True, stop=True).then_inc(s_sepa, 1)
                wait_past(pe, s_held, g)
                for t in range(TPG):
                    last = mm(ps[:, 3, t * P:t * P + P], msg[:, j, t * P:t * P + P], w_value[:], start=True, stop=True)
                last.then_inc(s_sepv, 1)

            def score_of(g, k, j):
                pe.wait_ge(s_u, g + 1)
                for t in range(TPG):
                    last = mm(ps[:, 4, ds(k * (TPG * H) + t * H, H)], act_a[:, j, t * P:t * P + P], a_dot[:],
                              start=True, stop=True)
                last.then_inc(s_sc, 1)

            def agg_of(g, j):
                pe.wait_ge(s_v, g + 1)
                wait_past(pe, s_accd, g)
                for t in range(TPG):
                    mm(ps[:, 5, 0:WIN], wval[:, j, t * P:t * P + P], onehot[:, j, t, :], start=t == 0, stop=t == TPG - 1)
                for t in range(TPG):
                    last = mm(ps[0:H, 5, WIN:2 * WIN], wts[:, j, t, :], onehot[:, j, t, :],
                              start=t == 0, stop=t == TPG - 1)
                last.then_inc(s_agg, 1)

            def step4(b, k, pair, j, x, sep, sc, val, sm):
                g = b * GPS + k
                if x:
                    x_of(g, b * PPS + pair, j)
                if sm == 2:
                    pe.wait_ge(s_sccopy, b)
                if sc:
                    score_of(g - 2, GPS - 2 + j if sm in (0, 1) else k - 2, j)
                if sep:
                    sep_of(g - 1, 1 - j)
                if val:
                    agg_of(g - LAG, 1 - j)
                if sm == 1:
                    pe.wait_ge(s_sccopy, b)
                    for t in range(TPG):
                        last = nc.tensor.transpose(ps[0:GPS * H, 6, t * P:t * P + P], scores[:, t, :], ident[:])
                    last.then_inc(s_turn, 1)
                if sm == 2:
                    pe.wait_ge(s_exp, b)
                    for t in range(TPG):
                        last = nc.tensor.transpose(ps[:, 6, t * GPS * H:(t + 1) * GPS * H], p_row[:, t * P:t * P + P], ident[0:GPS * H, 0:GPS * H])
                    last.then_inc(s_back, 1)

            pe.wait_ge(s_zero, 1)
            all_steps4(pe, step4)

            pe.wait_ge(s_const, 2)
            for n, src in enumerate((max_first, max_last)):
                for g in range(GPS):
                    last = mm(ps[:, n, g * NSB:(g + 1) * NSB], expand[:, g, :], src[:], start=True, stop=True)
            last.then_inc(s_mx, 1)
            pe.wait_ge(s_accd, NG)
            for n, src in enumerate((slot_first, slot_prev)):
                last = mm(ps[:, 2, n * NG:(n + 1) * NG], h_to_hv[:], src[0:H, 1, :], start=True, stop=True)
            last.then_inc(s_mx, 1)
            pe.wait_ge(s_totals, 1)
            mm(ps[0:H, 3, 0:NG], hv_to_h[:], totals[:, 1, :], start=True, stop=True).then_inc(s_mx, 1)

            def spread(c):
                wait_past(pe, s_o, c)
                for n, (mat, src) in enumerate(((h_to_hv, acc[0:H, 1, :]), (bv_to_hv, ratio8[0:H, :]))):
                    for o in range(0, CC, 512):
                        w = min(512, CC - o)
                        last = mm(psflat[:, 1024 * n + o:1024 * n + o + w], mat[:], src[:, ds(c * CC + o, w)], start=True, stop=True)
                last.then_inc(s_spread, 1)

            def project(c):
                pe.wait_ge(s_o, c + 1)
                wait_past(pe, s_ysum, c + NCH)
                for i in range(CB):
                    o = 2048 + i * P
                    mm(psflat[:, o:o + P], ones_row[:], b_proj[0:1, :], start=True, stop=False)
                    last = mm(psflat[:, o:o + P], stage[:, i * P:i * P + P], w_proj[:], start=False, stop=True)
                last.then_inc(s_pr, 1)
            pe.wait_ge(s_unpacked, 32)
            spread(0)
            with pe.Fori(1, NCH) as c:
                spread(c)
                project(c - 1)
            project(NCH - 1)

        @block.scalar
        def _(act):
            af = nc.scalar.activation

            with act.Fori(0, NCH) as c:
                act.wait_ge(s_xw, c + 1)
                nc.scalar.copy(g_nodes[:, ds(c * CB, CB), :].rearrange("p b c -> p (b c)"), psflat[:, 0:CC]).then_inc(s_xw_copied, 1)
            act.wait_ge(s_deg, DEG_STEPS)
            af(dis[:], ps[:, 7, 0:NB], ACT.Sqrt, bias=1.0).then_inc(s_sqrt, 1)

            def group1(q, j, first):
                g = q * 2 + j
                act.wait_ge(s_l1, g + 1)
                if not (first and j == 0):
                    act.wait_ge(s_l2, g)
                af(h1[:], ps[:, 1, 0:2 * P], ACT.Silu, bias=b1_2[:]).then_inc(s_a1, 1)
                act.wait_ge(s_l2, g + 1)
                if not (first and j == 0):
                    act.wait_ge(s_l3, g)
                af(h2[:], ps[:, 2, 0:2 * P], ACT.Silu, bias=b2_2[:]).then_inc(s_a2, 1)
            for j in range(2):
                group1(0, j, True)
            with act.Fori(1, NG // 2) as q:
                for j in range(2):
                    group1(q, j, False)

            def normalise(n, dst, sem_):
                act.wait_ge(s_ln1, n + 1)
                nc.scalar.sqrt(std[:], rstd[:]).then_inc(s_ln2, 1)
                act.wait_ge(s_ln3, n + 1)
                for i in range(CB):
                    last = af(dst(i), y[:, i, :], ACT.Identity, bias=shift[:, i:i + 1], scale=rstd[:, i:i + 1])
                last.then_inc(sem_, 1)

            act.wait_ge(s_acc1, NG)

            def norm3(c):
                wait_past(act, s_t1, c)
                nc.scalar.copy(stage[:], gcn_acc[:, ds(c * CC, CC)]).then_inc(s_stage, 1)

            def norm3b(c):
                wait_past(act, s_x1c, c)
                wait_past(act, s_t2, c)
                normalise(c, lambda i: xc[:, i, :], s_x1)

            def tables_x1T(c):
                act.wait_ge(s_t2, c + 1)
                wait_past(act, s_mm, c)
                nc.scalar.copy(x1T[:], psflat[:, 1024:1024 + CC]).then_inc(s_x1T, 1)

            def tables_parts(c, early):
                parts = lambda n: md_parts[:, ds(c % 2, 1), :, n].rearrange("p o b c -> p (o b) c")
                act.wait_ge(s_mm, c + 1)
                if not early:
                    act.wait_ge(s_mdt, (c - 1) * 16)
                nc.scalar.copy(parts(0), psflat[:, 3072:3072 + CC].rearrange("p (b c) -> p b c", c=C)).then_inc(s_hi, 1)
                act.wait_ge(s_mdr, c + 1)
                nc.scalar.copy(parts(1), md_rest[:]).then_inc(s_mid, 1)

            norm3(0)
            norm3b(0)

            def chunk3(c, early):
                norm3(c)
                tables_x1T(c - 1)
                norm3b(c)
                tables_parts(c - 1, early)
            for c in (1, 2):
                chunk3(c, True)
            with act.Fori(3, NCH) as c:
                chunk3(c, False)
            tables_x1T(NCH - 1)
            tables_parts(NCH - 1, False)

            def accumulate(g):
                w = act.value_load(win_i[0:1, ds(g, 1)], min_val=0, max_val=NP - 1)
                act.wait_ge(s_agg, g + 1)
                wait_past(act, s_accd, g)
                sums = ps[:, 5, 0:2 * WIN].rearrange("p (a w) -> p a w", a=2)
                nc.scalar.copy(slot_prev[:, :, ds(g, 1)], acc[:, :, ds(w, 1)])
                nc.scalar.copy(slot_first[:, :, ds(g, 1)], sums[:, :, 0:1])
                nc.scalar.copy(acc[:, :, ds(w + 1, WIN - 1)], sums[:, :, 1:WIN]).then_inc(s_accd, 1)

            def step4(b, k, pair, j, x, sep, sc, val, sm):
                g = b * GPS + k
                if sep:
                    act.wait_ge(s_sepa, g)
                    wait_past(act, s_u, g - 2)
                    af(pre[:, 1 - j, :], ps[:, 2, :], ACT.Identity, bias=b_alpha[:])
                    af(tanh[:, 1 - j, :], ps[:, 2, :], ACT.Tanh, bias=b_alpha_half[:], scale=0.5).then_inc(s_pre, 1)
                    act.wait_ge(s_sepv, g)
                    if val:
                        act.wait_ge(s_v, g - (LAG - 1))
                    nc.scalar.copy(hold[:, ds((g - 1) % HOLD, 1), :], ps[:, 3, :]).then_inc(s_held, 1)
                if sm == 2:
                    act.wait_ge(s_shift, b)
                    af(p_row[:], shifted[:], ACT.Exp).then_inc(s_exp, 1)
                if val:
                    accumulate(g - LAG)

            act.wait_ge(s_prep, 1)
            act.wait_ge(s_zero, 1)
            all_steps4(act, step4)

            for n in range(3):
                act.wait_ge(s_mxe, n + 1)
                af(mrg[9 + n][:], mrg[9 + n][:], ACT.Exp).then_inc(s_me, 1)
            act.wait_ge(s_tot, 1)
            write_back(act, nc.scalar.copy, 0, WB_ACT)
            nc.scalar.copy(marks[:, 0:1], marks[:, 3:4]).then_inc(s_wb, 1)

            def norm5(c, early):
                if not early:
                    act.wait_ge(s_out, (c - 1) * 16)
                normalise(c + NCH, lambda i: out_c[:, ds(c % 2, 1), i, :], s_y)
            for c in range(2):
                norm5(c, True)
            with act.Fori(2, NCH) as c:
                norm5(c, False)

        @block.vector
        def _(dve):
            V = nc.vector
            tt, ts, stt = V.tensor_tensor, V.tensor_scalar, V.scalar_tensor_tensor
            own = [0]

            def chain(ins):
                own[0] += 1
                ins.then_inc(s_v_own, 1)
                dve.wait_ge(s_v_own, own[0])

            dve.wait_ge(s_const, 1)
            dve.wait_ge(s_in0, 16)
            V.tensor_copy(iota_rep[:], iota_i[:].unsqueeze(2).broadcast_to([P, P, DEG_T]))
            V.tensor_copy(iota_f[:], iota_i[:])
            ts(lo_i[:], dst_i[:], P - 1, None, ALU.bitwise_and)
            chain(ts(hi_i[:], dst_i[:], 7, None, ALU.arith_shift_right))
            V.tensor_copy(hi_b[:], hi_i[:])
            chain(V.tensor_copy(lo_b[:], lo_i[:]))

            def hots(s, j, first):
                if not first:
                    dve.wait_ge(s_deg, s - 1)
                tiles = lambda z, n: z[:, ds(s * DEG_T, DEG_T)].unsqueeze(1).broadcast_to([P, n, DEG_T])
                tt(lo_hot[:, j], iota_rep[:], tiles(lo_b, P), ALU.is_equal)
                tt(hi_hot[:, j], iota_rep[:, 0:NB], tiles(hi_b, NB), ALU.is_equal).then_inc(s_hot, 1)
            for j in range(2):
                hots(j, j, True)
            with dve.Fori(1, DEG_STEPS // 2) as q:
                for j in range(2):
                    hots(q * 2 + j, j, False)
            dve.wait_ge(s_sqrt, 1)
            chain(V.reciprocal(dis[:], dis[:]))
            dve.wait_ge(s_xw_copied, NCH)
            tt(g_nodes, g_nodes, dis[:].unsqueeze(2).broadcast_to([P, NB, C]), ALU.mult).then_inc(s_g, 1)

            dve.wait_ge(s_in, N_IN)
            V.tensor_copy(part_f[:], part_i[:])
            V.tensor_copy(win_f[:], win_i[:])
            V.tensor_copy(last_f[:], last_i[:])
            V.memset(dst_rel[:, NT:], 0.0)
            V.tensor_copy(dst_rel[:, 0:NT], dst_i[:])
            ts(b_alpha_half[:], b_alpha[:], 0.5, None, ALU.mult)
            ts(a_dot[:], a_dot[:], 0.4, None, ALU.mult)
            tt(bv_to_hv[:], bv_to_hv[:], h_to_hv[:], ALU.mult)
            chain(V.memset(neg_edge[:], -BIG))
            chain(ts(part_w[0:WIN, :], part_f[0:WIN, :], 0.0, None, ALU.add))
            chain(ts(part_w[WIN:P, :], part_f[WIN:P, :], float(WIN), None, ALU.subtract))
            ts(win_iota[:], win_f[:], part_w[:], None, ALU.add)
            chain(tt(dst_rel[:, 0:NT].rearrange("p (g t) -> p g t", t=TPG), dst_rel[:, 0:NT].rearrange("p (g t) -> p g t", t=TPG),
                     win_f[:, 0:NG].unsqueeze(2).broadcast_to([P, NG, TPG]), ALU.subtract))
            V.memset(gcn_acc, 0.0).then_inc(s_prep, 1)

            def make_onehot(g, j):
                return tt(onehot[:, j], iota_f[:, 0:WIN].unsqueeze(1).broadcast_to([P, TPG, WIN]),
                          dst_rel[:, ds(g * TPG, TPG)].unsqueeze(2).broadcast_to([P, TPG, WIN]), ALU.is_equal)

            def radial(g, q, j):
                dve.wait_ge(s_l3, g + 1)
                dve.wait_ge(s_ea[j], q * 16 + 16)
                wait_past(dve, s_st1[j], q * 16)
                halves = lambda z: z.rearrange("p (r e) -> p r e", r=2)
                stt(halves(mrad[:, j, :]), ps[:, 3:5, 0:2 * P], b3[:], halves(ea_row[:, j, :]), ALU.add, ALU.mult).then_inc(s_rad, 1)

            def group1(q, j, first):
                g = q * 2 + j
                if not (first and j == 0):
                    radial(g - 1, q - 1 + j, 1 - j)
                w = dve.value_load(win_i[0:1, ds(g, 1)], min_val=0, max_val=NP - 1)
                wait_past(dve, s_acc1, g)
                prepare(q, j)
                dve.wait_ge(s_sum1, g + 1)
                window = gcn_acc[:, ds(w, WIN)]
                tt(window, window, ps[:, 0, 0:WIN], ALU.add).then_inc(s_acc1, 1)
                make_onehot(g + 2, j).then_inc(s_hot1, 1)
            for j in range(2):
                make_onehot(j, j).then_inc(s_hot1, 1)
            def clear(q):
                V.tensor_copy(acc[:, :, ds(q * HALF, HALF)], marks[:, 3:4].unsqueeze(2).broadcast_to([P, 2, HALF]))

            def prepare(q, j):
                cols = lambda z, n: z[:, ds(n * HALF, HALF)]
                x1_flat = x1_nodes[:].rearrange("p b c -> p (b c)")
                if j == 0:
                    bias = b_gcn[:, ds(q % (C // HALF) * HALF, HALF)]
                    tt(cols(x1_flat, q), cols(x1_flat, q), bias, ALU.add)
                    if not (isinstance(q, int) and q == 0):
                        clear(q - 1)
                else:
                    stt(cols(x1_flat, q), cols(acc[:, 1, :], q), dis[:, ds(q // (C // HALF), 1)], cols(x1_flat, q), ALU.mult, ALU.add)

            dve.wait_ge(s_gtab, 16)
            for q in range(2):
                for j in range(2):
                    group1(q, j, q == 0)
            with dve.Fori(2, NG // 2) as q:
                for j in range(2):
                    group1(q, j, False)
            radial(NG - 1, NG // 2 - 1, 1)

            dve.wait_ge(s_acc1, NG)
            V.memset(acc[:, :, NP - HALF:NW], 0.0)

            def statistics(n):
                dve.wait_ge(s_norm, n * 4 + 1)
                for i in range(CB):
                    last = V.bn_stats(bn[:, i, :], y[:, i, :])
                last.then_inc(s_norm, 1)
                dve.wait_ge(s_norm, n * 4 + 2)
                dve.sem_inc(s_stats_seen, 1)
                for i in range(CB):
                    last = V.bn_aggr(mean_var[:, i, :], bn[:, i, :])
                last.then_inc(s_norm, 1)
                dve.wait_ge(s_norm, n * 4 + 3)
                ts(rstd[:], mean_var[:, :, 1], LN_EPS, None, ALU.add).then_inc(s_ln1, 1)

            def scales(n):
                dve.wait_ge(s_ln2, n + 1)
                V.reciprocal(rstd[:], std[:]).then_inc(s_norm, 1)
                dve.wait_ge(s_norm, n * 4 + 4)
                stt(shift[:], mean_var[:, :, 0], -1.0, rstd[:], ALU.mult, ALU.mult).then_inc(s_ln3, 1)

            def norm3(c):
                dve.wait_ge(s_t1, c + 1)
                wait_past(dve, s_x1, c)
                for i in range(CB):
                    last = stt(y[:, i, :], psflat[:, i * P:i * P + P], dis[:, ds(c * CB + i, 1)],
                               x1_nodes[:, ds(c * CB + i, 1), :].rearrange("p o c -> p (o c)"), ALU.mult, ALU.add)
                last.then_inc(s_norm, 1)
                dve.wait_ge(s_norm, c * 4 + 1)
                V.tensor_copy(marks[:, 1:2], marks[:, 3:4]).then_inc(s_ysum, 1)
                statistics(c)
                scales(c)

            def tables3(c, early):
                dve.wait_ge(s_mm, c + 1)
                if not early:
                    dve.wait_ge(s_mst, (c - 1) * 16)
                tt(ms_out[:, ds(c % 2, 1)].rearrange("p o b c -> p (o b) c"), psflat[:, 2048:2048 + CC].rearrange("p (b c) -> p b c", c=C),
                   b_src[:].unsqueeze(1).broadcast_to([P, CB, C]), ALU.add).then_inc(s_mso, 1)
                dve.wait_ge(s_hi, c + 1)
                wait_past(dve, s_mdp, c)
                tt(md_rest[:], psflat[:, 3072:3072 + CC].rearrange("p (b c) -> p b c", c=C),
                   md_parts[:, ds(c % 2, 1), :, 0].rearrange("p o b c -> p (o b) c"), ALU.subtract).then_inc(s_mdr, 1)
            norm3(0)
            for c in (1, 2):
                norm3(c)
                tables3(c - 1, True)
            with dve.Fori(3, NCH) as c:
                norm3(c)
                tables3(c - 1, False)
            tables3(NCH - 1, False)
            dve.wait_ge(s_mso, NCH)
            dve.wait_ge(s_mdr, NCH)
            V.memset(ps[:, 5, WIN:2 * WIN], 0.0).then_inc(s_zero, 1)

            dve.wait_ge(s_mdt, 16 * NCH)
            dve.wait_ge(s_mst, 16 * NCH)
            V.memset(md_lz[WIN:P], 0.0)

            def hotT_of(g, q, j):
                dve.wait_ge(s_dst2[j], q * 16 + 16)
                ts(hotT[:, j, :], dst_row[:, j, :], win_iota[:, ds(g, 1)], None, ALU.is_equal).then_inc(s_hotT, 1)

            def values_of(g, place, j):
                dve.wait_ge(s_held, g + 1)
                wait_past(dve, s_agg, g - 1)
                make_onehot(g, j)
                weights = p_edge[:, :, ds(place, 1), :].rearrange("p t o h -> p t (o h)").unsqueeze(3).broadcast_to([P, TPG, H, K])
                V.tensor_copy(wts[:, j], p_edge[:, :, ds(place, 1), :].rearrange("p t o h -> p t (o h)"))
                tt(wval[:, j, :].rearrange("p (t h v) -> p t h v", t=TPG, h=H),
                   hold[:, ds(g % HOLD, 1), :].rearrange("p o (t h v) -> p (o t) h v", t=TPG, h=H), weights, ALU.mult).then_inc(s_v, 1)

            def maxima_of(b):
                dve.wait_ge(s_seg, b * 16 + 16)
                inner = neg_edge[:, 1:GE]
                tt(inner, seg_row[:, 1:GE], seg_row[:, 0:GE - 1], ALU.not_equal).then_inc(s_sm, 1)
                dve.wait_ge(s_sm, b * 4 + 1)
                ts(inner, inner, -BIG, None, ALU.mult).then_inc(s_sm, 1)
                dve.wait_ge(s_sm, b * 4 + 2)
                dve.wait_ge(s_turn, b + 1)
                turned = ps[0:GPS * H, 6, :]
                V.tensor_tensor_scan(fwd[:], neg_edge[:, 0:GE], turned, -BIG, ALU.add, ALU.max).then_inc(s_sm, 1)
                dve.wait_ge(s_sm, b * 4 + 3)
                V.tensor_tensor_scan(seg_max[:, ::-1], neg_edge[:, GE:0:-1], fwd[:, ::-1], -BIG, ALU.add, ALU.max).then_inc(s_sm, 1)
                dve.wait_ge(s_sm, b * 4 + 4)
                tt(shifted[:], turned, seg_max[:], ALU.subtract).then_inc(s_shift, 1)
                V.tensor_copy(max_first[:, ds(b, 1)], seg_max[:, 0:1])
                V.tensor_copy(max_last[:, ds(b, 1)], seg_max[:, GE - 1:GE]).then_inc(s_maxes, 1)

            def step4(b, k, pair, j, x, sep, sc, val, sm):
                g = b * GPS + k
                if sm == 2:
                    maxima_of(b - 1)
                if sm == 3:
                    dve.wait_ge(s_back, b)
                    V.tensor_copy(p_edge[:].rearrange("p t g h -> p (t g h)"), ps[:, 6, 0:TPG * GPS * H]).then_inc(s_p, 1)
                    dve.wait_ge(s_p, b)
                if val:
                    values_of(g - LAG, GPS - 3 + k if sm in (0, 1, 2) else k - 3, 1 - j)
                if x:
                    dve.wait_ge(s_x, g + 1)
                    dve.wait_ge(s_rad2[j], (b * PPS + pair) * 16 + 16)
                    tt(msg[:, j, :], ps[:, j, :], mrad[:, j, :], ALU.mult).then_inc(s_m, 1)
                    hotT_next(b, k, pair, j)
                if sep:
                    dve.wait_ge(s_pre, g)
                    wait_past(dve, s_sc, g - 2)
                    stt(act_a[:, 1 - j, :], tanh[:, 1 - j, :], 1.5, pre[:, 1 - j, :], ALU.add, ALU.mult).then_inc(s_u, 1)
                if sm == 1:
                    dve.wait_ge(s_sc, b * GPS)
                    V.tensor_copy(scores[:].rearrange("p t (g h) -> p g t h", g=GPS),
                                  ps[:, 4, 0:GPS * TPG * H].rearrange("p (g t h) -> p g t h", g=GPS, t=TPG)).then_inc(s_sccopy, 1)

            def hotT_next(b, k, pair, j):
                hotT_of(b * GPS + (k + 2), b * PPS + (pair + 1), j)

            for j in range(2):
                hotT_of(j, 0, j)
            all_steps4(dve, step4)

            cont, single, chained, fresh, m_f, m_l, m_tot, tmp, m_lt, e_first, e_last, e_chain = (m[:] for m in mrg)
            dve.wait_ge(s_accd, NG)
            dve.wait_ge(s_mx, 2)
            n1 = slice(1, NG)
            n0 = slice(0, NG - 1)
            V.memset(cont, 0.0)
            V.memset(chained, 0.0)
            V.memset(m_lt, -BIG)
            V.memset(e_last, 0.0)
            chain(V.memset(e_chain, 0.0))
            V.tensor_copy(slot_first[:, 1, :], ps[:, 2, 0:NG])
            V.tensor_copy(slot_prev[:, 1, :], ps[:, 2, NG:2 * NG])
            V.tensor_copy(m_f.rearrange("p (b g) -> p g b", g=GPS), ps[:, 0, 0:NG].rearrange("p (g b) -> p g b", b=NSB))
            V.tensor_copy(m_l.rearrange("p (b g) -> p g b", g=GPS), ps[:, 1, 0:NG].rearrange("p (g b) -> p g b", b=NSB))
            tt(single, win_f[:, 0:NG], last_f[:], ALU.is_equal)
            chain(tt(cont[:, n1], win_f[:, n1], last_f[:, n0], ALU.is_equal))
            chain(tt(chained[:, n1], cont[:, n1], single[:, n0], ALU.mult))
            chain(tt(fresh, cont, chained, ALU.subtract))
            chain(tt(m_lt[:, n1], m_l[:, n0], fresh[:, n1], ALU.mult))
            chain(ts(tmp, fresh, 1.0, BIG, ALU.subtract, ALU.mult))
            chain(tt(m_lt[:, n1], m_lt[:, n1], tmp[:, n1], ALU.add))
            chain(tt(m_lt, m_lt, m_f, ALU.max))
            chain(ts(tmp, chained, 1.0, BIG, ALU.subtract, ALU.mult))
            chain(V.tensor_tensor_scan(m_tot, tmp, m_lt, -BIG, ALU.add, ALU.max))
            tt(e_first, m_f, m_tot, ALU.subtract).then_inc(s_mxe, 1)
            chain(tt(e_last[:, n1], m_l[:, n0], m_tot[:, n1], ALU.subtract))
            ts(e_last, e_last, 0.0, None, ALU.min).then_inc(s_mxe, 1)
            chain(tt(e_chain[:, n1], m_tot[:, n0], m_tot[:, n1], ALU.subtract))
            ts(e_chain, e_chain, 0.0, None, ALU.min).then_inc(s_mxe, 1)
            dve.wait_ge(s_me, 3)
            tt(e_last, e_last, fresh, ALU.mult)
            chain(tt(e_chain, e_chain, chained, ALU.mult))
            chain(tt(slot_first[:], slot_first[:], e_first.unsqueeze(1).broadcast_to([P, 2, NG]), ALU.mult))
            chain(tt(slot_prev[:], slot_prev[:], e_last.unsqueeze(1).broadcast_to([P, 2, NG]), ALU.mult))
            chain(tt(mrg2[:], slot_first[:], slot_prev[:], ALU.add))
            for n in range(2):
                chain(V.tensor_tensor_scan(totals[:, n, :], e_chain, mrg2[:, n, :], 0.0, ALU.mult, ALU.add))
            chain(V.memset(fresh, 0.0))
            chain(tt(fresh[:, n0], win_f[:, n0], win_f[:, n1], ALU.is_equal))
            chain(ts(tmp, fresh, 1.0, -1.0, ALU.subtract, ALU.mult))
            for n in range(2):
                chain(tt(mrg2[:, n, :], totals[:, n, :], tmp, ALU.mult))
                chain(V.tensor_tensor_scan(totals[:, n, ::-1], fresh[:, ::-1], mrg2[:, n, ::-1], 0.0, ALU.mult, ALU.add))
            V.memset(fresh[:, 0:1], 0.0).then_inc(s_totals, 1)
            dve.wait_ge(s_mx, 3)
            V.tensor_copy(totals[0:H, 1, :], ps[0:H, 3, 0:NG]).then_inc(s_tot, 1)
            dve.wait_ge(s_tot, 1)
            write_back(dve, V.tensor_copy, WB_ACT, WB_ACT + WB_DVE)
            V.tensor_copy(marks[:, 1:2], marks[:, 3:4]).then_inc(s_wb, 1)
            dve.wait_ge(s_packed, 16)
            chain(ts(den_p[:, 2, :], den_p[:, 0, :], 1e-16, None, ALU.add))
            chain(V.reciprocal(den_p[:, 1, :], den_p[:, 2, :]))
            tt(den_p[:, 2, :], den_p[:, 0, :], den_p[:, 1, :], ALU.mult).then_inc(s_inv, 1)

            def weigh5(c):
                dve.wait_ge(s_spread, c + 1)
                tt(scaled[:], psflat[:, 0:CC], acc[:, 0, ds(c * CC, CC)], ALU.mult).then_inc(s_scaled, 1)

            def add5(c):
                wait_past(dve, s_pr, c)
                dve.wait_ge(s_scaled, c + 1)
                tt(stage[:], psflat[:, 1024:1024 + CC], scaled[:], ALU.add).then_inc(s_o, 1)

            def norm5(c):
                dve.wait_ge(s_pr, c + 1)
                wait_past(dve, s_y, c)
                tt(y[:], psflat[:, 2048:2048 + CC].rearrange("p (b c) -> p b c", c=C), x1_nodes[:, ds(c * CB, CB), :], ALU.add).then_inc(s_norm, 1)
                dve.wait_ge(s_norm, c * 4 + (NCH * 4 + 1))
                V.tensor_copy(marks[:, 1:2], marks[:, 3:4]).then_inc(s_ysum, 1)
                statistics(c + NCH)
            weigh5(0)
            add5(0)
            with dve.Fori(1, NCH) as c:
                weigh5(c)
                norm5(c - 1)
                add5(c)
                scales(c + (NCH - 1))
            norm5(NCH - 1)
            scales(2 * NCH - 1)


def kernel(**inputs):
    import concourse.bacc as bacc
    from concourse import mybir
    from concourse.bass_utils import run_bass_kernel_spmd

    v = {k: np.asarray(x) for k, x in inputs.items()}
    col = lambda x: np.ascontiguousarray(x.reshape(-1, 1))
    row = lambda x: np.ascontiguousarray(x.reshape(1, -1))
    pad = EP - N_EDGES
    src = np.concatenate([v["src"].astype(np.int32), np.zeros(pad, np.int32)])
    dst = np.concatenate([v["dst"].astype(np.int32), np.full(pad, NP - 1, np.int32)])
    ea = np.concatenate([v["edge_weight1"][:, 0], np.zeros(pad, np.float32)])
    attr = np.concatenate([v["edge_attr_32"], np.zeros((pad, RAD), np.float32)])
    x = np.concatenate([v["x"], np.zeros((NP - N_NODES, C), np.float32)])
    sep, b_sep = v["L1_gnn_w_sep"].reshape(C, H, 2, K), v["L1_gnn_b_sep"].reshape(H, 2, K)
    by_tile = lambda z: np.ascontiguousarray(z.reshape(NT, P).T)
    arrays = {
        "srcE": np.concatenate([by_tile(src), np.zeros((P, TPG), np.int32)], axis=1), "dstE": by_tile(dst),
        "dst_row": row(np.concatenate([dst, np.zeros(2 * GE, np.int32)])), "ea_row": row(ea),
        "first": np.concatenate([dst[::GE], np.zeros(2, np.int32)]), "last": dst[GE - 1::GE].copy(),
        "attrT": np.ascontiguousarray(attr.reshape(NG, TPG, P, RAD).transpose(1, 3, 0, 2).reshape(P, NG * P)),
        "xN": x, "xT": np.ascontiguousarray(x.T),
        "w_gcn": v["L0_gnn_W"], "b_gcn": v["L0_gnn_b"],
        "w_src": v["L1_gnn_w_src"], "b_src": v["L1_gnn_b_src"], "w_dst": v["L1_gnn_w_dst"],
        "fc_w1": v["L1_gnn_fc_w1"], "fc_b1": col(v["L1_gnn_fc_b1"]),
        "fc_w2": v["L1_gnn_fc_w2"], "fc_b2": col(v["L1_gnn_fc_b2"]),
        "fc_w3": v["L1_gnn_fc_w3"], "fc_b3": col(v["L1_gnn_fc_b3"]),
        "w_alpha": np.ascontiguousarray(sep[:, :, 0].reshape(C, P)), "w_value": np.ascontiguousarray(sep[:, :, 1].reshape(C, P)),
        "b_alpha": col(b_sep[:, 0]), "b_value": col(b_sep[:, 1]),
        "alpha_dot": col(v["L1_gnn_alpha_dot"]), "w_proj": v["L1_gnn_w_proj"], "b_proj": v["L1_gnn_b_proj"],
    }
    arrays = {k: np.ascontiguousarray(x) for k, x in arrays.items()}
    nc = bacc.Bacc("TRN2", target_bir_lowering=False, num_devices=1)
    aps = {k: nc.dram_tensor("in_" + k, x.shape, mybir.dt.from_np(x.dtype), kind="ExternalInput").ap() for k, x in arrays.items()}
    out = nc.dram_tensor("out_x", [NP, C], mybir.dt.float32, kind="ExternalOutput").ap()
    build(nc, aps, out)
    r = run_bass_kernel_spmd(nc, [{"in_" + k: x for k, x in arrays.items()}], core_ids=[0])
    return r.results[0]["out_x"][:N_NODES]
```

```python
import numpy as np
from contextlib import ExitStack

N_NODES, N_EDGES, C = 6250, 100000, 128
P = 128
NB = (N_NODES + P - 1) // P
NP = NB * P
GE = 512
TPG = GE // P
NG = (N_EDGES + GE - 1) // GE
EP = NG * GE
NT = EP // P
NSB, GPS = 14, 14
PPS = GPS // 2
WB = 14
WB_ACT, WB_DVE, WB_POOL = 5, 4, 5
WIN = 64
HOLD, LAG = 17, 18
NW = NP + WIN
CB = 7
NCH = NB // CB
CC = CB * P
assert NW % WIN == 0
H, K = 8, 16
H3 = 3 * H
RAD, FC = 32, 64
DEG_T = 14
DEG_STEPS = NT // DEG_T
HALF = NP // (NG // 2)
DP = NP * 8 // P
BIG = 1.0e30
LN_EPS = 1e-5
assert HOLD == LAG - 1 and LAG % 2 == 0 and 4 <= LAG - GPS < 6
assert NSB * GPS == NG and NCH * CB == NB and DEG_STEPS * DEG_T == NT and DEG_STEPS % (2 * NCH) == 0 and HALF * (NG // 2) == NP and C % HALF == 0
assert (WB_ACT + WB_DVE + WB_POOL) * WB == NG and DP * P == NP * 8


def build(nc, a, out):
    import concourse.bass as bass
    from concourse import mybir

    f32, bf16, i32 = mybir.dt.float32, mybir.dt.bfloat16, mybir.dt.int32
    ALU, ACT, AX = mybir.AluOpType, mybir.ActivationFunctionType, mybir.AxisListType
    ds = bass.ds

    g_tab = nc.dram_tensor("g_tab", [NP, C], f32, kind="Internal").ap()
    ms_tab = nc.dram_tensor("ms_tab", [NP, C], f32, kind="Internal").ap()
    md_tab = nc.dram_tensor("md_tab", [NW, 3, C], bf16, kind="Internal").ap()
    edge_rows = nc.dram_tensor("edge_rows", [EP, C], f32, kind="Internal").ap()
    spill_wval = nc.dram_tensor("spill_wval", [NG, P, GE], f32, kind="Internal").ap()
    spill_wts = nc.dram_tensor("spill_wts", [NG, P, TPG * H3], bf16, kind="Internal").ap()
    rad_tab = nc.dram_tensor("rad_tab", [NG, P, GE], f32, kind="Internal").ap()

    top = ExitStack()
    sbuf = lambda name, shape, dt, st=top: st.enter_context(nc.sbuf_tensor(name, shape, dt))
    sem = lambda name: top.enter_context(nc.semaphore(name))

    with top:
        acc = sbuf("acc", [P, 2, NW], f32)
        g_nodes = acc[:, 1, 0:NP].rearrange("p (b c) -> p b c", c=C)
        x1_nodes = sbuf("x1_nodes", [P, NB, C], f32)
        hold = sbuf("hold", [P, HOLD, GE], f32)
        gcn_acc = hold[:].rearrange("p a b -> p (a b)")[:, 0:NW]
        ratios = hold[:].rearrange("p a b -> p (a b)")
        src_i = sbuf("src_i", [P, NT + TPG], i32)
        dst_rel = sbuf("dst_rel", [P, NT + 2 * TPG], f32)
        win_i = sbuf("win_i", [P, NG + 2], i32)
        win_f = sbuf("win_f", [P, NG + 2], f32)
        last_f = sbuf("last_f", [P, NG], f32)
        win_iota = sbuf("win_iota", [P, NG + 2], f32)
        iota_i = sbuf("iota_i", [P, P], i32)
        iota_f = sbuf("iota_f", [P, P], f32)
        part_i = sbuf("part_i", [P, 1], i32)
        part_f = sbuf("part_f", [P, 1], f32)
        part_w = sbuf("part_w", [P, 1], f32)
        ident = sbuf("ident", [P, P], f32)
        dis = sbuf("dis", [P, NB], f32)
        slot_first = sbuf("slot_first", [P, 2, NG], f32)
        slot_prev = sbuf("slot_prev", [P, 2, NG], f32)
        max_first = sbuf("max_first", [GPS * H, NSB], f32)
        max_last = sbuf("max_last", [GPS * H, NSB], f32)
        idx = sbuf("idx", [P, 4 * TPG], i32)
        gath = sbuf("gath", [P, 4, TPG, C], f32)
        onehot = sbuf("onehot", [P, 2, TPG, WIN], f32)
        mrad = sbuf("mrad", [P, 2, GE], f32)
        w_gcn = sbuf("w_gcn", [P, C], f32)
        w_sd = sbuf("w_sd", [P, 2 * C], f32)
        w1_bd = sbuf("w1_bd", [P, 2, P], f32)
        w2_bd = sbuf("w2_bd", [P, P], f32)
        w3_2 = sbuf("w3_2", [P, C], f32)
        w_alpha = sbuf("w_alpha", [P, P], f32)
        w_value = sbuf("w_value", [P, P], f32)
        a_dot = sbuf("a_dot", [P, H], f32)
        w_proj = sbuf("w_proj", [P, C], f32)
        b_gcn, b_src = (sbuf(n, [P, C], f32) for n in ("b_gcn", "b_src"))
        b1_2, b2_2, b3, b_alpha, b_alpha_half = (sbuf(n, [P, 1], f32) for n in (
            "b1_2", "b2_2", "b3", "b_alpha", "b_alpha_half"))
        neg_edge = sbuf("neg_edge", [GPS * H, GE + 1], f32)
        onehot_b = sbuf("onehot_b", [P, 2, TPG, WIN], bf16)
        wide_wts = sbuf("wide_wts", [P, TPG, H3], bf16)
        h_to_hv = sbuf("h_to_hv", [H3, P], f32)
        bv_heads = sbuf("bv_heads", [P, H], f32)
        biases = sbuf("biases", [H + 1, C], f32)
        hv_to_h = sbuf("hv_to_h", [P, H3], f32)
        marks = sbuf("marks", [P, 8], f32)
        zeros = sbuf("zeros", [WIN, 3, C], bf16)
        extra_i = sbuf("extra_i", [P, 3], i32)
        ahead = sbuf("ahead", [P, 1], f32)
        at_f, gap = sbuf("at_f", [P, 1], f32), sbuf("gap", [P, 1], f32)
        at_i = sbuf("at_i", [P, 1], i32)
        rel_w = sbuf("rel_w", [P, TPG], f32)

        with ExitStack() as st:
            dst_i = sbuf("dst_i", [P, NT], i32, st)
            lo_i, hi_i = (sbuf(n, [P, NT], i32, st) for n in ("lo_i", "hi_i"))
            lo_b = sbuf("lo_b", [P, NT], bf16, st)
            iota_rep = sbuf("iota_rep", [P, P, DEG_T], bf16, st)
            hi_b = sbuf("hi_b", [P, NT], bf16, st)
            last_i = sbuf("last_i", [P, NG], i32, st)
            lo_hot = sbuf("lo_hot", [P, 2, P, DEG_T], bf16, st)
            hi_hot = sbuf("hi_hot", [P, 2, NB, DEG_T], bf16, st)
            counts = sbuf("counts", [NB, P], f32, st)
            xT = sbuf("xT", [P, CC], f32, st)
            attr = sbuf("attr", [P, 2, P], f32, st)
            ea_row = sbuf("ea_row", [P, 2, GE], f32, st)
            h1 = sbuf("h1", [P, 2 * P], f32, st)
            h2 = sbuf("h2", [P, 2 * P], f32, st)
        with ExitStack() as st:
            stage = sbuf("stage", [P, CC], f32, st)
            y = sbuf("y", [P, 2, CB, C], f32, st)
            bn = sbuf("bn", [P, CB, 6], f32, st)
            mean_var = sbuf("mean_var", [P, CB, 2], f32, st)
            std, rstd, shift = (sbuf(n, [P, CB], f32, st) for n in ("std", "rstd", "shift"))
            with ExitStack() as st3:
                xc = sbuf("xc", [P, CB, C], f32, st3)
                x1T = sbuf("x1T", [P, CC], f32, st3)
                ms_out = sbuf("ms_out", [P, 2, CB, C], f32, st3)
                md_rest = sbuf("md_rest", [P, CB, C], f32, st3)
                md_parts = sbuf("md_parts", [P, 2, CB, 3, C], bf16, st3)
            with ExitStack() as st5:
                heads = sbuf("heads", [H + 1, CC], f32, st5)
                out_c = sbuf("out_c", [P, 2, CB, C], f32, st5)
                expand = sbuf("expand", [GPS * H, GPS, P], f32, st5)
                mrg = [sbuf(f"merge_{n}", [P, NG], f32, st5) for n in range(12)]
                mrg2 = sbuf("mrg2", [P, 2, NG], f32, st5)
                totals = sbuf("totals", [P, 2, NG], f32, st5)
                den_p = sbuf("den_p", [P, 3, DP], f32, st5)
        with ExitStack() as st:
            far_f = sbuf("far_f", [P, 1], f32, st)
            far_i = sbuf("far_i", [P, 1], i32, st)
            far_md = sbuf("far_md", [P, 3, C], bf16, st)
            far_row = sbuf("far_row", [P, C], f32, st)
        with ExitStack() as st:
            dst_row = sbuf("dst_row", [P, 2, GE], i32, st)
            md_hm = sbuf("md_hm", [2 * WIN, 2, C], bf16, st)
            md_lz = sbuf("md_lz", [2 * WIN, 2, C], bf16, st)
            hotT = sbuf("hotT", [P, 2, GE], bf16, st)
            msg = sbuf("msg", [P, 2, GE], f32, st)
            pre = sbuf("pre", [P, 2, GE], f32, st)
            tanh = sbuf("tanh", [P, 2, GE], f32, st)
            act_a = sbuf("act_a", [P, 2, GE], f32, st)
            wval = sbuf("wval", [P, 2, GE], f32, st)
            wts = sbuf("wts", [P, 2, TPG, H3], bf16, st)
            scores = sbuf("scores", [P, TPG, GPS * H], f32, st)
            seg_row = sbuf("seg_row", [GPS * H, GE], i32, st)
            fwd = sbuf("fwd", [GPS * H, GE], f32, st)
            seg_max = sbuf("seg_max", [GPS * H, GE], f32, st)
            shifted = sbuf("shifted", [GPS * H, GE], f32, st)
            p_row = sbuf("p_row", [GPS * H, GE], f32, st)
            p_edge = sbuf("p_edge", [P, TPG, GPS, H], f32, st)
            p_rest = sbuf("p_rest", [P, TPG, GPS, H], f32, st)
            p_parts = sbuf("p_parts", [P, TPG, GPS, 3, H], bf16, st)

        ps = top.enter_context(nc.psum_tensor("psum", [P, 8, 512], f32))
        psflat = ps[:].rearrange("p b n -> p (b n)")

        s_in = sem("s_inputs_loaded")
        s_const = sem("s_pool_constants")
        s_prep = sem("s_vector_prepared")
        s_xT = sem("s_xT_loaded")
        s_xw = sem("s_xw_product")
        s_xw_copied = sem("s_xw_copied")
        s_hot = sem("s_degree_onehots")
        s_in0, s_w0 = sem("s_dst_loaded"), sem("s_w_gcn_loaded")
        s_deg = sem("s_degree_products")
        s_sqrt, s_g = sem("s_degree_sqrt"), sem("s_g_ready")
        s_gtab = sem("s_g_table_stored")
        s_idx = sem("s_indices_copied")
        s_g1 = [sem(f"s_pass1_rows_{j}") for j in range(4)]
        s_in1, s_ea = ([sem(f"s_{n}_{j}") for j in range(2)] for n in ("features_loaded", "edge_weights_loaded"))
        s_st1 = [sem(f"s_radial_stored_{j}") for j in range(2)]
        s_hot1, s_sum1, s_acc1 = sem("s_onehot1"), sem("s_sum1"), sem("s_acc1")
        s_l1, s_a1, s_l2, s_a2, s_l3, s_rad = (sem(n) for n in (
            "s_mlp1", "s_silu1", "s_mlp2", "s_silu2", "s_mlp3", "s_radial"))
        s_stage, s_t1, s_x1, s_t2, s_x1T, s_mm, s_mso, s_mdp, s_x1c = (sem(n) for n in (
            "s_staged", "s_sums_turned", "s_x1_chunk", "s_x1_turned", "s_x1T",
            "s_tables_product", "s_ms_ready", "s_md_parts", "s_x1_kept"))
        s_mst, s_mdt, s_padded = sem("s_ms_table_stored"), sem("s_md_table_stored"), sem("s_md_table_padded")
        s_zero = sem("s_acc_zeroed")
        s_ln1, s_ln2 = sem("s_ln_variance"), sem("s_ln_sqrt")
        s_g2 = [sem(f"s_pass2_rows_{j}") for j in range(2)]
        s_dst2, s_md2, s_rad2 = ([sem(f"s_{n}_loaded_{j}") for j in range(2)] for n in ("dst_row", "md_rows", "radial"))
        s_hotT, s_x, s_m, s_sepa, s_sepv, s_pre, s_held, s_u, s_sc = (sem(n) for n in (
            "s_hotT", "s_msg_sum", "s_msg", "s_alpha", "s_value", "s_pre", "s_held", "s_act", "s_scores"))
        s_v, s_agg, s_accd = sem("s_weighted"), sem("s_aggregated"), sem("s_accumulated")
        s_seg, s_sccopy, s_turn, s_shift, s_exp, s_back, s_p = (sem(n) for n in (
            "s_segment_rows", "s_scores_copied", "s_scores_turned", "s_shifted", "s_exp", "s_p_turned", "s_p"))
        s_mx, s_mxe, s_me, s_tot, s_wb = (sem(n) for n in (
            "s_max_product", "s_merge_shift", "s_merge_exp", "s_totals", "s_written_back"))
        s_o, s_pr, s_y, s_out = sem("s_o"), sem("s_projected"), sem("s_y_ready"), sem("s_out_stored")
        s_sm, s_maxes = sem("s_softmax_steps"), sem("s_group_maxima_kept")
        s_sum1_done, s_rows_ready, s_far_zero, s_fixed = (sem(n) for n in ("s_pass1_complete", "s_rows_ready", "s_md_table_cleared", "s_sums_complete"))
        s_w1_free, s_w1_hot, s_w1_sum, s_w1_own, s_w1_rows, s_w1_idx = (sem(f"s_wide1_{n}") for n in ("free", "onehot", "sum", "own", "rows", "idx"))
        s_far_own, s_far_dst, s_far_idx, s_far_rows, s_far_sum, s_far_st = (sem(f"s_far_{n}") for n in ("own", "dst", "idx", "rows", "sum", "stored"))
        s_w2_free, s_w2_hot, s_w2_sum, s_w2_own, s_w2_rows, s_spill = (sem(f"s_wide2_{n}") for n in ("free", "onehot", "sum", "own", "rows", "spilled"))
        s_cleared = sem("s_gcn_sums_cleared")
        s_p_parts = sem("s_weight_parts")
        s_ones, s_biases = sem("s_ratios_ones"), sem("s_biases_copied")
        s_act_seen = sem("s_act_seen")
        s_stats_seen, s_store_seen = sem("s_stats_seen"), sem("s_store_seen")
        s_slot, s_part = sem("s_slot_seen_free"), sem("s_part_steps")
        s_norm, s_ln3, s_ysum, s_hi, s_mid, s_mdr, s_packed, s_inv, s_unpacked, s_spread, s_heads, s_totals = (sem(n) for n in (
            "s_norm_steps", "s_ln_scales", "s_y_summed", "s_md_high_part", "s_md_middle_part", "s_md_rest", "s_weights_packed",
            "s_weights_inverted", "s_weights_unpacked", "s_weights_spread", "s_heads_copied", "s_totals_ready"))
        s_v_own, s_p_own = sem("s_vector_own"), sem("s_pool_own")

        block = top.enter_context(nc.Block())

        loads = [
            (src_i[:], a["srcE"]),
            (win_i[:], a["first"].partition_broadcast(P)), (last_i[:], a["last"].partition_broadcast(P)),
            (w_sd[:, 0:C], a["w_src"]), (w_sd[:, C:2 * C], a["w_dst"]),
            (w3_2[0:FC, :], a["fc_w3"]), (w3_2[FC:2 * FC, :], a["fc_w3"]),
            (w_alpha[:], a["w_alpha"]), (w_value[:], a["w_value"]), (w_proj[:], a["w_proj"]),
            (b_gcn[:], a["b_gcn"].partition_broadcast(P)), (b_src[:], a["b_src"].partition_broadcast(P)),
            (biases[H:H + 1, :], a["b_proj"].partition_broadcast(1)),
            (b1_2[0:FC, :], a["fc_b1"]), (b1_2[FC:2 * FC, :], a["fc_b1"]),
            (b2_2[0:FC, :], a["fc_b2"]), (b2_2[FC:2 * FC, :], a["fc_b2"]),
            (x1_nodes[:], a["xN"].rearrange("(b p) c -> p b c", p=P)),
            (b3[:], a["fc_b3"]), (b_alpha[:], a["b_alpha"]),
        ]
        placed = [(w1_bd[RAD * t:RAD * t + RAD, t % 2, FC * (t // 2):FC * (t // 2) + FC], a["fc_w1"]) for t in range(4)]
        placed += [(w2_bd[FC * t:FC * t + FC, FC * t:FC * t + FC], a["fc_w2"]) for t in range(2)]
        placed += [(a_dot[K * h:K * h + K, h:h + 1], a["alpha_dot"][K * h:K * h + K, :]) for h in range(H)]
        placed += [(bv_heads[K * h:K * h + K, h:h + 1], a["b_value"][K * h:K * h + K, :]) for h in range(H)]
        N_IN = 16 * (len(loads) + len(placed))

        def node_rows(tab, c):
            return tab[0:NP, :].rearrange("(b p) c -> p b c", p=P)[:, ds(c * CB, CB), :]

        def wait_past(eng, sem_, n):
            if not (isinstance(n, int) and n <= 0):
                eng.wait_ge(sem_, n)

        def write_back(eng, copy, first, end):
            with eng.Fori(first, end) as i:
                at = nc.values_load_multi_w_load_instructions(win_i[0:1, ds(i * WB, WB)], engines=[eng.engine],
                                                              min_val=0, max_val=NP - 1)[1]
                for n in range(WB):
                    copy(acc[:, :, ds(at[n], 1)], totals[:, :, ds(i * WB + n, 1)])

        def extra_windows(eng):
            return eng.value_load(extra_i[0:1, 0:1], min_val=0, max_val=NP // WIN)

        def any_wide(eng):
            return eng.value_load(extra_i[0:1, 1:2], min_val=0, max_val=1)

        def visits(eng, body, extra, after=None):
            with eng.If(extra > 0):
                with eng.Fori(0, extra) as k:
                    with eng.Fori(0, NG) as g:
                        body(k * NG + g, k, g)
                    if after:
                        after(k)

        def all_steps4(eng, step):
            def pairs(b, first, end, *parts):
                with eng.Fori(first, end) as pair:
                    for j in range(2):
                        step(b, pair * 2 + j, pair, j, *parts)

            for k in range(4):
                step(0, k, k // 2, k % 2, True, k >= 1, k >= 2, False, None)
            pairs(0, 2, PPS, True, True, True, False, None)
            for k in range(6):
                step(1, k, k // 2, k % 2, True, True, True, k >= LAG - GPS, k)
            pairs(1, 3, PPS, True, True, True, True, None)
            with eng.Fori(2, NSB) as b:
                for k in range(6):
                    step(b, k, k // 2, k % 2, True, True, True, True, k)
                pairs(b, 3, PPS, True, True, True, True, None)
            for k in range(6):
                step(NSB, k, k // 2, k % 2, False, k < 1, k < 2, True, k)
            pairs(NSB, 3, LAG // 2, False, False, False, True, None)

        def place_of(k):
            return k - (LAG - GPS) if not isinstance(k, int) or k >= LAG - GPS else k + (2 * GPS - LAG)

        @block.sync
        def _(sp):
            sp.dma_start(dst_i[:], a["dstE"]).then_inc(s_in0, 16)
            sp.dma_start(w_gcn[:], a["w_gcn"]).then_inc(s_w0, 16)
            sp.dma_start(xT[:], a["xT"][:, 0:CC]).then_inc(s_xT, 16)
            for dst, src in loads:
                sp.dma_start(dst, src).then_inc(s_in, 16)
            sp.wait_ge(s_const, 1)
            for dst, src in placed:
                sp.dma_start(dst, src).then_inc(s_in, 16)
            with sp.Fori(0, NCH) as c:
                sp.wait_ge(s_g, c + 1)
                sp.dma_start(node_rows(g_tab, c), g_nodes[:, ds(c * CB, CB), :]).then_inc(s_gtab, 16)

            def load_attr(g, j):
                sp.dma_start(attr[:, j, :], a["attrT"][:, ds(g * P, P)]).then_inc(s_in1[j], 16)

            def load_ea(g, j):
                sp.dma_start(ea_row[:, j, :], a["ea_row"][:, ds(g * GE, GE)].partition_broadcast(P)).then_inc(s_ea[j], 16)

            def store1(g, j):
                sp.wait_ge(s_rad, g + 1)
                sp.dma_start(rad_tab[ds(g, 1), :, :], mrad[:, j, :]).then_inc(s_st1[j], 16)

            for j in range(2):
                load_attr(j, j)
                load_ea(j, j)
            with sp.Fori(0, NG // 2 - 1) as q:
                for j in range(2):
                    sp.wait_ge(s_l1, q * 2 + (j + 1))
                    load_attr(q * 2 + (j + 2), j)
                    store1(q * 2 + j, j)
                    load_ea(q * 2 + (j + 2), j)
            for j in range(2):
                store1(NG - 2 + j, j)

            sp.dma_start(md_tab[NP:NW], zeros[:]).then_inc(s_padded, 16)
            def tables(c):
                sp.wait_ge(s_mso, c + 1)
                sp.sem_inc(s_store_seen, 1)
                wait_past(sp, s_mst, c * 16)
                sp.dma_start(node_rows(ms_tab, c), ms_out[:, ds(c % 2, 1)].rearrange("p o b c -> p (o b) c")).then_inc(s_mst, 16)
                sp.wait_ge(s_mdp, c + 1)
                sp.sem_inc(s_store_seen, 1)
                wait_past(sp, s_mdt, c * 16)
                sp.dma_start(md_tab[0:NP].rearrange("(b p) n c -> p b (n c)", p=P)[:, ds(c * CB, CB), :],
                             md_parts[:, ds(c % 2, 1)].rearrange("p o b n c -> p (o b) (n c)")).then_inc(s_mdt, 16)
            tables(0)
            with sp.Fori(1, NCH) as c:
                tables(c)
            sp.wait_ge(s_mst, 16 * NCH)
            sp.wait_ge(s_mdt, 16 * NCH)
            sp.wait_ge(s_padded, 16)
            for j in range(2):
                sp.wait_ge(s_st1[j], 16 * (NG // 2))

            extra, wide = extra_windows(sp), any_wide(sp)
            sp.sem_inc(s_far_st, 16)
            with sp.If(wide > 0):
                with sp.Fori(0, NT) as t:
                    sp.wait_ge(s_far_sum, t + 1)
                    sp.sem_inc(s_store_seen, 1)
                    sp.dma_start(edge_rows[ds(t * P, P), :], far_row[:]).then_inc(s_far_st, 16)
                sp.wait_ge(s_far_st, 16 * NT + 16)
                with sp.Fori(0, NW // WIN) as n:
                    sp.dma_start(md_tab[ds(n * WIN, WIN)], zeros[:]).then_inc(s_far_zero, 16)
                sp.wait_ge(s_far_zero, 16 * (NW // WIN))
            sp.sem_inc(s_rows_ready, 1)

            def load_dst(g, j):
                sp.dma_start(dst_row[:, j, :], a["dst_row"][:, ds(g * GE, GE)].partition_broadcast(P)).then_inc(s_dst2[j], 16)

            def load_md(g, j):
                w = sp.value_load(win_i[0:1, ds(g, 1)], min_val=0, max_val=NP - 1)
                sp.dma_start(md_hm[:, j, :], md_tab[ds(w, WIN), 0:2, :].rearrange("r n c -> n r c")).then_inc(s_md2[j], 16)
                sp.dma_start(md_lz[0:WIN, j, :], md_tab[ds(w, WIN), 2, :]).then_inc(s_md2[j], 16)

            def load_rad(g, j):
                sp.dma_start(mrad[:, j, :], rad_tab[ds(g, 1), :, :]).then_inc(s_rad2[j], 16)

            def next_loads(g, j):
                sp.wait_ge(s_hotT, g + 1)
                load_dst(g + 2, j)
                sp.wait_ge(s_x, g + 1)
                load_md(g + 2, j)
                sp.wait_ge(s_m, g + 1)
                load_rad(g + 2, j)

            def seg_load(b):
                rows = a["dst_row"][:, ds(b * (GPS * GE), GPS * GE)].rearrange("o (g e) -> g o e", g=GPS)
                sp.dma_start(seg_row[:], rows.broadcast_to([GPS, H, GE])).then_inc(s_seg, 16)

            for j in range(2):
                load_dst(j, j)
                load_md(j, j)
                load_rad(j, j)
            seg_load(0)
            with sp.Fori(0, PPS) as k:
                for j in range(2):
                    next_loads(k * 2 + j, j)
            with sp.Fori(1, NSB - 1) as b:
                with sp.Fori(0, 2) as k:
                    for j in range(2):
                        next_loads(b * GPS + k * 2 + j, j)
                sp.wait_ge(s_shift, b)
                seg_load(b)
                with sp.Fori(2, PPS) as k:
                    for j in range(2):
                        next_loads(b * GPS + k * 2 + j, j)
            with sp.Fori(0, 2) as k:
                for j in range(2):
                    next_loads(k * 2 + (j + (NSB - 1) * GPS), j)
            sp.wait_ge(s_shift, NSB - 1)
            seg_load(NSB - 1)
            with sp.Fori(2, PPS - 1) as k:
                for j in range(2):
                    next_loads(k * 2 + (j + (NSB - 1) * GPS), j)
            for j in range(2):
                sp.wait_ge(s_hotT, NG - 1 + j)
                load_dst(NG + j, j)

            def load_spilled(n, k, g):
                sp.wait_ge(s_w2_free, n + 1)
                sp.sem_inc(s_store_seen, 1)
                sp.dma_start(gath[:, 0].rearrange("p t c -> p (t c)"), spill_wval[ds(g, 1), :, :]).then_inc(s_w2_rows, 16)
                sp.dma_start(wide_wts[:].rearrange("p t h -> p (t h)"), spill_wts[ds(g, 1), :, :]).then_inc(s_w2_rows, 16)
            visits(sp, load_spilled, extra)

            packed = lambda ap: ap.rearrange("h (i n) -> h i n", n=DP)
            sp.wait_ge(s_wb, 3)
            for n in range(3):
                sp.dma_start(den_p[:, n, :], packed(acc[n * H:n * H + H, 1, 0:NP])).then_inc(s_packed, 16)
            sp.wait_ge(s_inv, 1)
            sp.wait_ge(s_ones, 1)
            sp.dma_start(packed(acc[0:H, 1, 0:NP]), den_p[:, 1, :]).then_inc(s_unpacked, 16)
            sp.dma_start(packed(ratios[0:H, 0:NP]), den_p[:, 2, :]).then_inc(s_unpacked, 16)

            def result(c):
                sp.wait_ge(s_y, c + 1)
                sp.sem_inc(s_store_seen, 1)
                wait_past(sp, s_out, c * 16)
                sp.dma_start(node_rows(out, c), out_c[:, ds(c % 2, 1)].rearrange("p o b c -> p (o b) c")).then_inc(s_out, 16)
            result(0)
            with sp.Fori(1, NCH) as c:
                result(c)
            sp.wait_ge(s_out, 16 * NCH)

        @block.gpsimd
        def _(pool):
            for m in (w1_bd, w2_bd, a_dot, bv_heads, ident, marks):
                nc.gpsimd.memset(m[:], 0.0)
            for m in (h_to_hv, hv_to_h):
                last = nc.gpsimd.memset(m[:], 0.0)
            last.then_inc(s_p_own, 1)
            pool.wait_ge(s_p_own, 1)
            nc.gpsimd.affine_select(out=ident[:], in_=ident[:], compare_op=ALU.not_equal, fill=1.0, base=0,
                                    pattern=[[-1, P]], channel_multiplier=1)
            for n in range(3):
                if n:
                    pool.wait_ge(s_p_own, n + 1)
                heads_of = h_to_hv[:].rearrange("p (h v) -> p h v", h=H)
                nc.gpsimd.affine_select(out=heads_of, in_=heads_of, compare_op=ALU.not_equal, fill=1.0, base=-n * H,
                                        pattern=[[-1, H], [0, K]], channel_multiplier=1).then_inc(s_p_own, 1)
            nc.gpsimd.affine_select(out=hv_to_h[:, 0:H], in_=hv_to_h[:, 0:H], compare_op=ALU.not_equal, fill=1.0, base=0,
                                    pattern=[[-K, H]], channel_multiplier=1)
            nc.gpsimd.memset(zeros[:], 0.0)
            nc.gpsimd.iota(iota_i[:], pattern=[[1, P]], base=0, channel_multiplier=0)
            nc.gpsimd.iota(part_i[:], pattern=[[0, 1]], base=0, channel_multiplier=1).then_inc(s_const, 1)
            nc.gpsimd.memset(gcn_acc, 0.0).then_inc(s_cleared, 1)

            def gathers(tab, sems, used, copies_before, narrow=None, wide=None):
                R = len(sems)

                def copy_list(g, n):
                    nc.gpsimd.tensor_copy(idx[:, n * TPG:(n + 1) * TPG], src_i[:, ds(g * TPG, TPG)]).then_inc(s_idx, 1)

                def arrived(i, m):
                    return i * (16 * TPG * 4 // R) + 16 * TPG * (m // R + 1)

                def step(i, first):
                    for n in range(4):
                        m = (n + 1) % 4
                        if not first or n == 3:
                            pool.wait_ge(sems[m % R], arrived(i if n == 3 else i - 1, m))
                            pool.sem_inc(s_slot, 1)
                        copy_list(i * 4 + (n + 1), m)
                        pool.wait_ge(s_idx, i * 4 + (n + 1 + copies_before))
                        pool.sem_inc(s_slot, 1)
                        if not (first and n < R):
                            pool.wait_ge(used, i * 4 + (n + 1 - R))
                            pool.sem_inc(s_slot, 1)
                        def gather():
                            for t in range(TPG):
                                pool.indirect_dma_start(gath[:, n % R, t, :], None, tab,
                                                        bass.IndirectOffsetOnAxis(idx[:, n * TPG + t:n * TPG + t + 1], 0)
                                                        ).then_inc(sems[n % R], 16)
                        if wide is None:
                            gather()
                            continue
                        with pool.If(narrow > 0):
                            gather()
                        with pool.If(wide > 0):
                            for t in range(TPG):
                                pool.dma_start(gath[:, n % R, t, :], edge_rows[ds((i * 4 + n) * GE + t * P, P), :]).then_inc(sems[n % R], 16)
                copy_list(0, 0)
                step(0, True)
                with pool.Fori(1, NG // 4) as i:
                    step(i, False)

            pool.wait_ge(s_in, N_IN)
            pool.wait_ge(s_gtab, 16 * NCH)
            gathers(g_tab, s_g1, s_sum1, 0)

            for j in range(4):
                pool.wait_ge(s_g1[j], 4 * TPG * NG)
            pool.wait_ge(s_idx, NG + 1)
            pool.wait_ge(s_prep, 1)
            extra, wide = extra_windows(pool), any_wide(pool)

            def gather_again(n, k, g):
                pool.wait_ge(s_w1_free, n + 1)
                pool.sem_inc(s_slot, 1)
                nc.gpsimd.tensor_copy(idx[:, 0:TPG], src_i[:, ds(g * TPG, TPG)]).then_inc(s_w1_idx, 1)
                pool.wait_ge(s_w1_idx, n + 1)
                pool.sem_inc(s_slot, 1)
                for t in range(TPG):
                    pool.indirect_dma_start(gath[:, 0, t, :], None, g_tab, bass.IndirectOffsetOnAxis(idx[:, t:t + 1], 0)
                                            ).then_inc(s_w1_rows, 16)
            visits(pool, gather_again, extra)

            def keep(c):
                pool.wait_ge(s_x1, c + 1)
                pool.sem_inc(s_slot, 1)
                nc.gpsimd.tensor_copy(x1_nodes[:, ds(c * CB, CB), :], xc[:]).then_inc(s_x1c, 1)

            def last_part(c):
                pool.wait_ge(s_mid, c + 1)
                pool.sem_inc(s_slot, 1)
                parts = lambda n: md_parts[:, ds(c % 2, 1), :, n].rearrange("p o b c -> p (o b) c")
                nc.gpsimd.tensor_tensor(md_rest[:], md_rest[:], parts(1), ALU.subtract).then_inc(s_part, 1)
                pool.wait_ge(s_part, c + 1)
                pool.sem_inc(s_slot, 1)
                nc.gpsimd.tensor_copy(parts(2), md_rest[:]).then_inc(s_mdp, 1)
            keep(0)
            with pool.Fori(1, NCH) as c:
                keep(c)
                last_part(c - 1)
            last_part(NCH - 1)
            narrow = pool.value_load(extra_i[0:1, 2:3], min_val=0, max_val=1)
            pool.wait_ge(s_mst, 16 * NCH)
            with pool.If(wide > 0):
                pool.wait_ge(s_mdt, 16 * NCH)
                pool.wait_ge(s_padded, 16)
                with pool.Fori(0, NT) as t:
                    pool.wait_ge(s_far_dst, t + 1)
                    pool.sem_inc(s_slot, 1)
                    nc.gpsimd.tensor_copy(idx[:, 0:1], src_i[:, ds(t, 1)])
                    nc.gpsimd.tensor_copy(idx[:, 1:2], far_i[:]).then_inc(s_far_idx, 1)
                    pool.wait_ge(s_far_idx, t + 1)
                    pool.sem_inc(s_slot, 1)
                    for row, tab, n in ((gath[:, 0, 0, :], ms_tab, 0), (far_md[:].rearrange("p n c -> p (n c)"), md_tab.rearrange("r n c -> r (n c)"), 1)):
                        pool.indirect_dma_start(row, None, tab, bass.IndirectOffsetOnAxis(idx[:, n:n + 1], 0)).then_inc(s_far_rows, 16)
                pool.wait_ge(s_rows_ready, 1)
            gathers(ms_tab, s_g2, s_x, NG + 1, narrow, wide)
            pool.wait_ge(s_accd, NG)
            nc.gpsimd.memset(expand[:], 0.0).then_inc(s_p_own, 1)
            nc.gpsimd.memset(ratios[0:H + 1, 0:NP], 1.0).then_inc(s_ones, 1)
            pool.wait_ge(s_p_own, 5)
            nc.gpsimd.affine_select(out=expand[:].rearrange("p g (h v) -> p g h v", h=H), in_=expand[:].rearrange("p g (h v) -> p g h v", h=H),
                                    compare_op=ALU.not_equal, fill=1.0, base=0,
                                    pattern=[[-H, GPS], [-1, H], [0, K]], channel_multiplier=1).then_inc(s_const, 1)
            pool.wait_ge(s_tot, 1)
            write_back(pool, nc.gpsimd.tensor_copy, WB_ACT + WB_DVE, WB_ACT + WB_DVE + WB_POOL)
            nc.gpsimd.tensor_copy(marks[:, 2:3], marks[:, 3:4]).then_inc(s_wb, 1)

        @block.tensor
        def _(pe):
            mm = nc.tensor.matmul
            pe.wait_ge(s_w0, 16)

            def xw(c, first):
                pe.wait_ge(s_xT, c * 16 + 16)
                if not first:
                    pe.wait_ge(s_xw_copied, c)
                for i in range(CB):
                    last = mm(psflat[:, i * P:i * P + P], xT[:, i * P:i * P + P], w_gcn[:], start=True, stop=True)
                last.then_inc(s_xw, 1)

            def deg(s, j, first, final):
                pe.wait_ge(s_hot, s + 1)
                for i in range(DEG_T):
                    last = mm(ps[0:NB, 7, 0:P], hi_hot[:, j, :, i], lo_hot[:, j, :, i],
                              start=first and i == 0, stop=final and i == DEG_T - 1)
                last.then_inc(s_deg, 1)
            def step1(c, first, final):
                xw(c, first)
                for n in range(DEG_STEPS // NCH):
                    deg(c * (DEG_STEPS // NCH) + n, n % 2, first and n == 0, final and n == DEG_STEPS // NCH - 1)
            step1(0, True, False)
            with pe.Fori(1, NCH - 1) as c:
                step1(c, False, False)
            step1(NCH - 1, False, True)
            pe.wait_ge(s_sqrt, 1)
            nc.tensor.transpose(ps[:, 6, 0:NB], counts[:], ident[0:NB, 0:NB]).then_inc(s_deg, 1)

            pe.wait_ge(s_in, N_IN)

            def l3(g):
                pe.wait_ge(s_a2, g + 1)
                if not (isinstance(g, int) and g == 0):
                    pe.wait_ge(s_rad, g)
                for t in (0, 2, 1, 3):
                    r, e = t // 2, t % 2 * P
                    last = mm(ps[:, 3 + r, e:e + P], w3_2[FC * r:FC * r + FC, :], h2[FC * r:FC * r + FC, e:e + P], start=True, stop=True)
                last.then_inc(s_l3, 1)

            def group1(i, n, first):
                g, j = i * 4 + n, n % 2
                start = first and n == 0
                pe.wait_ge(s_in1[j], i * 32 + (n // 2 * 16 + 16))
                if not start:
                    pe.wait_ge(s_a1, g)
                for half in range(2):
                    last = mm(ps[:, 1, half * P:half * P + P], w1_bd[:, half, :], attr[:, j, :], start=True, stop=True)
                last.then_inc(s_l1, 1)
                if not start:
                    l3(g - 1)
                pe.wait_ge(s_a1, g + 1)
                mm(ps[:, 2, 0:2 * P], w2_bd[:], h1[:], start=True, stop=True).then_inc(s_l2, 1)
                pe.wait_ge(s_hot1, g + 1)
                pe.wait_ge(s_g1[n], i * (16 * TPG) + 16 * TPG)
                if not start:
                    pe.wait_ge(s_acc1, g)
                for t in range(TPG):
                    last = mm(ps[:, 0, 0:WIN], gath[:, n, t, :], onehot[:, j, t, :], start=t == 0, stop=t == TPG - 1)
                last.then_inc(s_sum1, 1)
            for n in range(4):
                group1(0, n, True)
            with pe.Fori(1, NG // 4) as i:
                for n in range(4):
                    group1(i, n, False)
            l3(NG - 1)
            pe.wait_ge(s_prep, 1)
            extra = extra_windows(pe)

            def sums_again(n, k, g):
                pe.wait_ge(s_w1_rows, n * (16 * TPG) + 16 * TPG)
                pe.wait_ge(s_w1_hot, n + 1)
                for t in range(TPG):
                    last = mm(ps[:, 0, 0:WIN], gath[:, 0, t, :], onehot[:, 0, t, :], start=t == 0, stop=t == TPG - 1)
                last.then_inc(s_w1_sum, 1)
            visits(pe, sums_again, extra)

            def turn_sums(c):
                pe.wait_ge(s_stage, c + 1)
                wait_past(pe, s_ysum, c)
                for i in range(CB):
                    last = nc.tensor.transpose(psflat[:, i * P:i * P + P], stage[:, i * P:i * P + P], ident[:])
                last.then_inc(s_t1, 1)

            def tables(c):
                pe.wait_ge(s_x1, c + 1)
                for i in range(CB):
                    last = nc.tensor.transpose(psflat[:, 1024 + i * P:1024 + i * P + P], xc[:, i, :], ident[:])
                last.then_inc(s_t2, 1)
                pe.wait_ge(s_x1T, c + 1)
                wait_past(pe, s_mdr, c)
                for i in range(CB):
                    for n in range(2):
                        o = 2048 + 1024 * n + i * P
                        last = mm(psflat[:, o:o + P], x1T[:, i * P:i * P + P], w_sd[:, n * C:(n + 1) * C], start=True, stop=True)
                last.then_inc(s_mm, 1)
            turn_sums(0)
            with pe.Fori(1, NCH) as c:
                turn_sums(c)
                tables(c - 1)
            tables(NCH - 1)

            def x_of(g, q, j):
                pe.wait_ge(s_g2[j], q * (16 * TPG) + 16 * TPG)
                pe.wait_ge(s_md2[j], q * 32 + 32)
                pe.wait_ge(s_hotT, g + 1)
                mm(ps[:, j, :], md_hm[:, j, :], hotT[0:2 * WIN, j, :], start=True, stop=False)
                mm(ps[:, j, :], md_lz[:, j, :], hotT[0:2 * WIN, j, :], start=False, stop=False)
                for t in range(TPG):
                    last = mm(ps[:, j, t * P:t * P + P], gath[:, j, t, :], ident[:], is_transpose=True, start=False, stop=t == TPG - 1)
                last.then_inc(s_x, 1)

            def sep_of(g, j):
                pe.wait_ge(s_m, g + 1)
                wait_past(pe, s_pre, g)
                mm(ps[:, 2, :], w_alpha[:], msg[:, j, :], start=True, stop=True).then_inc(s_sepa, 1)
                wait_past(pe, s_held, g)
                for t in range(TPG):
                    last = mm(ps[:, 3, t * P:t * P + P], msg[:, j, t * P:t * P + P], w_value[:], start=True, stop=True)
                last.then_inc(s_sepv, 1)

            def score_of(g, k, j):
                pe.wait_ge(s_u, g + 1)
                for t in range(TPG):
                    last = mm(ps[:, 4, ds(k * (TPG * H) + t * H, H)], act_a[:, j, t * P:t * P + P], a_dot[:],
                              start=True, stop=True)
                last.then_inc(s_sc, 1)

            def agg_of(g, j):
                pe.wait_ge(s_v, g + 1)
                wait_past(pe, s_accd, g - 1)
                for t in range(TPG):
                    mm(ps[:, 5 + 2 * j, 0:WIN], wval[:, j, t * P:t * P + P], onehot[:, j, t, :], start=t == 0, stop=t == TPG - 1)
                for t in range(TPG):
                    last = mm(ps[0:H3, 5 + 2 * j, WIN:2 * WIN], wts[:, j, t, :], onehot_b[:, j, t, :],
                              start=t == 0, stop=t == TPG - 1)
                last.then_inc(s_agg, 1)

            def step4(b, k, pair, j, x, sep, sc, val, sm):
                g = b * GPS + k
                if x:
                    x_of(g, b * PPS + pair, j)
                if sm == 2:
                    pe.wait_ge(s_sccopy, b)
                if sc:
                    score_of(g - 2, GPS - 2 + j if sm in (0, 1) else k - 2, j)
                if sep:
                    sep_of(g - 1, 1 - j)
                if sm == 3:
                    pe.wait_ge(s_exp, b)
                    for t in range(TPG):
                        last = nc.tensor.transpose(ps[:, 6, t * GPS * H:(t + 1) * GPS * H], p_row[:, t * P:t * P + P], ident[0:GPS * H, 0:GPS * H])
                    last.then_inc(s_back, 1)
                if val:
                    agg_of(g - LAG, j)
                if sm == 1:
                    pe.wait_ge(s_sccopy, b)
                    for t in range(TPG):
                        last = nc.tensor.transpose(ps[0:GPS * H, 6, t * P:t * P + P], scores[:, t, :], ident[:])
                    last.then_inc(s_turn, 1)

            pe.wait_ge(s_zero, 1)
            all_steps4(pe, step4)

            def weighted_again(n, k, g):
                pe.wait_ge(s_w2_rows, n * 32 + 32)
                pe.wait_ge(s_w2_hot, n + 1)
                for t in range(TPG):
                    mm(ps[:, 5, 0:WIN], gath[:, 0, t, :], onehot[:, 0, t, :], start=t == 0, stop=t == TPG - 1)
                for t in range(TPG):
                    last = mm(ps[0:H3, 5, WIN:2 * WIN], wide_wts[:, t, :], onehot_b[:, 0, t, :], start=t == 0, stop=t == TPG - 1)
                last.then_inc(s_w2_sum, 1)
            visits(pe, weighted_again, extra)

            pe.wait_ge(s_const, 2)
            for n, src in enumerate((max_first, max_last)):
                for g in range(GPS):
                    last = mm(ps[:, n, g * NSB:(g + 1) * NSB], expand[:, g, :], src[:], start=True, stop=True)
            last.then_inc(s_mx, 1)
            pe.wait_ge(s_fixed, 1)
            for n, src in enumerate((slot_first, slot_prev)):
                last = mm(ps[:, 2, n * NG:(n + 1) * NG], h_to_hv[:], src[0:H3, 1, :], start=True, stop=True)
            last.then_inc(s_mx, 1)
            pe.wait_ge(s_totals, 1)
            mm(ps[0:H3, 3, 0:NG], hv_to_h[:], totals[:, 1, :], start=True, stop=True).then_inc(s_mx, 1)

            mm(ps[0:H, 7, 0:C], bv_heads[:], w_proj[:], start=True, stop=True).then_inc(s_mx, 1)

            def spread(c):
                wait_past(pe, s_o, c - 1)
                for o in range(0, CC, 512):
                    w = min(512, CC - o)
                    last = mm(psflat[:, ds(c % 2 * 1024 + o, w)], h_to_hv[0:H, :], acc[0:H, 1, ds(c * CC + o, w)], start=True, stop=True)
                last.then_inc(s_spread, 1)

            def project(c):
                pe.wait_ge(s_heads, c + 1)
                pe.wait_ge(s_o, c + 1)
                wait_past(pe, s_ysum, c + NCH)
                for i in range(CB):
                    o = 2048 + i * P
                    mm(psflat[:, o:o + P], heads[:, i * P:i * P + P], biases[:], start=True, stop=False)
                    last = mm(psflat[:, o:o + P], stage[:, i * P:i * P + P], w_proj[:], start=False, stop=True)
                last.then_inc(s_pr, 1)
            pe.wait_ge(s_unpacked, 32)
            pe.wait_ge(s_biases, 1)
            spread(0)
            spread(1)
            project(0)
            with pe.Fori(2, NCH) as c:
                spread(c)
                project(c - 1)
            project(NCH - 1)

        @block.scalar
        def _(act):
            af = nc.scalar.activation

            with act.Fori(0, NCH - 1) as c:
                act.wait_ge(s_xw, c + 1)
                act.sem_inc(s_act_seen, 1)
                act.dma_start(xT[:], a["xT"][:, ds(c * CC + CC, CC)]).then_inc(s_xT, 16)
                nc.scalar.copy(g_nodes[:, ds(c * CB, CB), :].rearrange("p b c -> p (b c)"), psflat[:, 0:CC]).then_inc(s_xw_copied, 1)
            act.wait_ge(s_xw, NCH)
            nc.scalar.copy(g_nodes[:, (NCH - 1) * CB:, :].rearrange("p b c -> p (b c)"), psflat[:, 0:CC]).then_inc(s_xw_copied, 1)
            act.wait_ge(s_deg, DEG_STEPS)
            af(counts[:], ps[0:NB, 7, 0:P], ACT.Sqrt, bias=1.0).then_inc(s_sqrt, 1)

            def group1(q, j, first):
                g = q * 2 + j
                act.wait_ge(s_l1, g + 1)
                if not (first and j == 0):
                    act.wait_ge(s_l2, g)
                af(h1[:], ps[:, 1, 0:2 * P], ACT.Silu, bias=b1_2[:]).then_inc(s_a1, 1)
                act.wait_ge(s_l2, g + 1)
                if not (first and j == 0):
                    act.wait_ge(s_l3, g)
                af(h2[:], ps[:, 2, 0:2 * P], ACT.Silu, bias=b2_2[:]).then_inc(s_a2, 1)
            for j in range(2):
                group1(0, j, True)
            with act.Fori(1, NG // 2) as q:
                for j in range(2):
                    group1(q, j, False)

            def y_block(n, i):
                return y[:, ds(n % 2, 1), i, :].rearrange("p o c -> p (o c)")

            def normalise(n, dst, sem_):
                act.wait_ge(s_ln1, n + 1)
                nc.scalar.sqrt(std[:], rstd[:]).then_inc(s_ln2, 1)
                act.wait_ge(s_ln3, n + 1)
                for i in range(CB):
                    last = af(dst(i), y_block(n, i), ACT.Identity, bias=shift[:, i:i + 1], scale=rstd[:, i:i + 1])
                last.then_inc(sem_, 1)

            act.wait_ge(s_sum1_done, 1)

            def stage3(c):
                wait_past(act, s_t1, c)
                nc.scalar.copy(stage[:], gcn_acc[:, ds(c * CC, CC)]).then_inc(s_stage, 1)

            def norm3(c):
                wait_past(act, s_x1c, c)
                wait_past(act, s_t2, c)
                normalise(c, lambda i: xc[:, i, :], s_x1)

            def tables_x1T(c):
                act.wait_ge(s_t2, c + 1)
                wait_past(act, s_mm, c)
                nc.scalar.copy(x1T[:], psflat[:, 1024:1024 + CC]).then_inc(s_x1T, 1)

            def tables_parts(c, early):
                parts = lambda n: md_parts[:, ds(c % 2, 1), :, n].rearrange("p o b c -> p (o b) c")
                act.wait_ge(s_mm, c + 1)
                if not early:
                    act.wait_ge(s_mdt, (c - 1) * 16)
                nc.scalar.copy(parts(0), psflat[:, 3072:3072 + CC].rearrange("p (b c) -> p b c", c=C)).then_inc(s_hi, 1)
                act.wait_ge(s_mdr, c + 1)
                nc.scalar.copy(parts(1), md_rest[:]).then_inc(s_mid, 1)

            stage3(0)
            norm3(0)
            stage3(1)

            def chunk3(c, early):
                tables_x1T(c - 1)
                norm3(c)
                if not (isinstance(c, int) and c == NCH - 1):
                    stage3(c + 1)
                tables_parts(c - 1, early)
            for c in (1, 2):
                chunk3(c, True)
            with act.Fori(3, NCH - 1) as c:
                chunk3(c, False)
            chunk3(NCH - 1, False)
            tables_x1T(NCH - 1)
            tables_parts(NCH - 1, False)

            act.wait_ge(s_prep, 1)
            wide = any_wide(act)

            def accumulate(g, j):
                with act.If(wide > 0):
                    act.wait_ge(s_v, g + 1)
                    act.dma_start(spill_wval[ds(g, 1), :, :], wval[:, j, :]).then_inc(s_spill, 16)
                    act.dma_start(spill_wts[ds(g, 1), :, :], wts[:, j].rearrange("p t h -> p (t h)")).then_inc(s_spill, 16)
                    act.wait_ge(s_spill, g * 32 + 32)
                    act.sem_inc(s_act_seen, 1)
                w = act.value_load(win_i[0:1, ds(g, 1)], min_val=0, max_val=NP - 1)
                act.wait_ge(s_agg, g + 1)
                wait_past(act, s_accd, g)
                sums = ps[:, 5 + 2 * j, 0:2 * WIN].rearrange("p (a w) -> p a w", a=2)
                nc.scalar.copy(slot_prev[:, :, ds(g, 1)], acc[:, :, ds(w, 1)])
                nc.scalar.copy(slot_first[:, :, ds(g, 1)], sums[:, :, 0:1])
                nc.scalar.copy(acc[:, :, ds(w + 1, WIN - 1)], sums[:, :, 1:WIN]).then_inc(s_accd, 1)

            def step4(b, k, pair, j, x, sep, sc, val, sm):
                g = b * GPS + k
                if sep:
                    act.wait_ge(s_sepa, g)
                    wait_past(act, s_u, g - 2)
                    af(pre[:, 1 - j, :], ps[:, 2, :], ACT.Identity, bias=b_alpha[:])
                    af(tanh[:, 1 - j, :], ps[:, 2, :], ACT.Tanh, bias=b_alpha_half[:], scale=0.5).then_inc(s_pre, 1)
                    act.wait_ge(s_sepv, g)
                    if val:
                        act.wait_ge(s_v, g - (LAG - 1))
                    nc.scalar.copy(hold[:, ds((g - 1) % HOLD, 1), :], ps[:, 3, :]).then_inc(s_held, 1)
                if val:
                    accumulate(g - LAG, j)
                if sm == 2:
                    act.wait_ge(s_shift, b)
                    af(p_row[:], shifted[:], ACT.Exp).then_inc(s_exp, 1)

            act.wait_ge(s_zero, 1)
            all_steps4(act, step4)

            for n in range(3):
                act.wait_ge(s_mxe, n + 1)
                af(mrg[9 + n][:], mrg[9 + n][:], ACT.Exp).then_inc(s_me, 1)
            act.wait_ge(s_tot, 1)
            write_back(act, nc.scalar.copy, 0, WB_ACT)
            nc.scalar.copy(marks[:, 0:1], marks[:, 3:4]).then_inc(s_wb, 1)

            act.wait_ge(s_mx, 4)
            nc.scalar.copy(biases[0:H, :], ps[0:H, 7, 0:C]).then_inc(s_biases, 1)

            def heads5(c):
                wait_past(act, s_pr, c)
                nc.scalar.copy(heads[:], ratios[0:H + 1, ds(c * CC, CC)]).then_inc(s_heads, 1)

            def norm5(c, early):
                if not early:
                    act.wait_ge(s_out, (c - 1) * 16)
                normalise(c + NCH, lambda i: out_c[:, ds(c % 2, 1), i, :], s_y)
            act.wait_ge(s_unpacked, 32)
            heads5(0)
            for c in range(2):
                heads5(c + 1)
                norm5(c, True)
            with act.Fori(2, NCH - 1) as c:
                heads5(c + 1)
                norm5(c, False)
            norm5(NCH - 1, False)

        @block.vector
        def _(dve):
            V = nc.vector
            tt, ts, stt = V.tensor_tensor, V.tensor_scalar, V.scalar_tensor_tensor
            own = [0]

            def chain(ins):
                own[0] += 1
                ins.then_inc(s_v_own, 1)
                dve.wait_ge(s_v_own, own[0])

            dve.wait_ge(s_const, 1)
            dve.wait_ge(s_in0, 16)
            V.tensor_copy(iota_rep[:], iota_i[:].unsqueeze(2).broadcast_to([P, P, DEG_T]))
            V.tensor_copy(iota_f[:], iota_i[:])
            ts(lo_i[:], dst_i[:], P - 1, None, ALU.bitwise_and)
            chain(ts(hi_i[:], dst_i[:], 7, None, ALU.arith_shift_right))
            V.tensor_copy(hi_b[:], hi_i[:])
            chain(V.tensor_copy(lo_b[:], lo_i[:]))

            def hots(s, j, first):
                if not first:
                    dve.wait_ge(s_deg, s - 1)
                tiles = lambda z, n: z[:, ds(s * DEG_T, DEG_T)].unsqueeze(1).broadcast_to([P, n, DEG_T])
                tt(lo_hot[:, j], iota_rep[:], tiles(lo_b, P), ALU.is_equal)
                tt(hi_hot[:, j], iota_rep[:, 0:NB], tiles(hi_b, NB), ALU.is_equal).then_inc(s_hot, 1)
            for j in range(2):
                hots(j, j, True)
            with dve.Fori(1, DEG_STEPS // 2) as q:
                for j in range(2):
                    hots(q * 2 + j, j, False)
            dve.wait_ge(s_deg, DEG_STEPS + 1)
            chain(V.reciprocal(dis[:], ps[:, 6, 0:NB]))
            dve.wait_ge(s_xw_copied, NCH)
            with dve.Fori(0, NCH) as c:
                g_chunk = g_nodes[:, ds(c * CB, CB), :]
                tt(g_chunk, g_chunk, dis[:, ds(c * CB, CB)].unsqueeze(2).broadcast_to([P, CB, C]), ALU.mult).then_inc(s_g, 1)
            dve.wait_ge(s_g, NCH)

            dve.wait_ge(s_in, N_IN)
            V.tensor_copy(part_f[:], part_i[:])
            V.tensor_copy(win_f[:], win_i[:])
            V.tensor_copy(last_f[:], last_i[:])
            V.memset(dst_rel[:, NT:], 0.0)
            V.tensor_copy(dst_rel[:, 0:NT], dst_i[:])
            ts(b_alpha_half[:], b_alpha[:], 0.5, None, ALU.mult)
            ts(a_dot[:], a_dot[:], 0.4, None, ALU.mult)
            chain(V.memset(neg_edge[:], -BIG))
            chain(ts(part_w[0:WIN, :], part_f[0:WIN, :], 0.0, None, ALU.add))
            chain(ts(part_w[WIN:2 * WIN, :], part_f[WIN:2 * WIN, :], float(WIN), None, ALU.subtract))
            ts(win_iota[0:2 * WIN], win_f[0:2 * WIN], part_w[0:2 * WIN], None, ALU.add)
            chain(tt(dst_rel[:, 0:NT].rearrange("p (g t) -> p g t", t=TPG), dst_rel[:, 0:NT].rearrange("p (g t) -> p g t", t=TPG),
                     win_f[:, 0:NG].unsqueeze(2).broadcast_to([P, NG, TPG]), ALU.subtract))
            chain(tt(last_f[:], last_f[:], win_f[:, 0:NG], ALU.subtract))
            chain(V.tensor_reduce(at_f[:], last_f[:], AX.X, ALU.max))
            chain(V.tensor_copy(at_i[:], at_f[:]))
            chain(ts(extra_i[:, 0:1], at_i[:], WIN.bit_length() - 1, None, ALU.arith_shift_right))
            chain(ts(extra_i[:, 1:2], extra_i[:, 0:1], 1, None, ALU.min))
            chain(ts(extra_i[:, 2:3], extra_i[:, 1:2], 0, None, ALU.is_equal))
            chain(V.tensor_copy(last_f[:], last_i[:]))
            V.tensor_copy(marks[:, 1:2], marks[:, 3:4]).then_inc(s_prep, 1)
            dve.wait_ge(s_prep, 1)
            dve.wait_ge(s_cleared, 1)
            extra, wide = extra_windows(dve), any_wide(dve)

            def further_windows(free, hot, summed, steps, add, mark):
                V.memset(ahead[:], float(WIN)).then_inc(steps, 1)
                V.tensor_copy(marks[:, mark:mark + 1], marks[:, 3:4]).then_inc(free, 1)

                def visit(n, k, g):
                    done = n * 3 + k
                    dve.wait_ge(free, n + 1)
                    dve.sem_inc(s_stats_seen, 1)
                    dve.wait_ge(steps, done + 1)
                    dve.sem_inc(s_stats_seen, 1)
                    ts(at_f[:], win_f[:, ds(g, 1)], ahead[:], float(NP), ALU.add, ALU.min).then_inc(steps, 1)
                    dve.wait_ge(steps, done + 2)
                    dve.sem_inc(s_stats_seen, 1)
                    V.tensor_copy(at_i[:], at_f[:])
                    tt(gap[:], win_f[:, ds(g, 1)], at_f[:], ALU.subtract).then_inc(steps, 1)
                    dve.wait_ge(steps, done + 3)
                    dve.sem_inc(s_stats_seen, 1)
                    ts(rel_w[:], dst_rel[:, ds(g * TPG, TPG)], gap[:], None, ALU.add).then_inc(steps, 1)
                    dve.wait_ge(steps, done + 4)
                    dve.sem_inc(s_stats_seen, 1)
                    for hots in (onehot, onehot_b):
                        last = tt(hots[:, 0], iota_f[:, 0:WIN].unsqueeze(1).broadcast_to([P, TPG, WIN]),
                                  rel_w[:].unsqueeze(2).broadcast_to([P, TPG, WIN]), ALU.is_equal)
                    last.then_inc(hot, 1)
                    w = dve.value_load(at_i[0:1, 0:1], min_val=0, max_val=NP)
                    dve.wait_ge(summed, n + 1)
                    add(w).then_inc(free, 1)
                visits(dve, visit, extra, lambda k: ts(ahead[:], ahead[:], float(WIN), None, ALU.add).then_inc(steps, 1))

            def make_onehot(g, j, hots=onehot):
                return tt(hots[:, j], iota_f[:, 0:WIN].unsqueeze(1).broadcast_to([P, TPG, WIN]),
                          dst_rel[:, ds(g * TPG, TPG)].unsqueeze(2).broadcast_to([P, TPG, WIN]), ALU.is_equal)

            def radial(g, q, j):
                dve.wait_ge(s_l3, g + 1)
                dve.wait_ge(s_ea[j], q * 16 + 16)
                wait_past(dve, s_st1[j], q * 16)
                halves = lambda z: z.rearrange("p (r e) -> p r e", r=2)
                stt(halves(mrad[:, j, :]), ps[:, 3:5, 0:2 * P], b3[:], halves(ea_row[:, j, :]), ALU.add, ALU.mult).then_inc(s_rad, 1)

            def group1(q, j, first):
                g = q * 2 + j
                if not (first and j == 0):
                    radial(g - 1, q - 1 + j, 1 - j)
                w = dve.value_load(win_i[0:1, ds(g, 1)], min_val=0, max_val=NP - 1)
                wait_past(dve, s_acc1, g)
                prepare(q, j)
                dve.wait_ge(s_sum1, g + 1)
                window = gcn_acc[:, ds(w, WIN)]
                tt(window, window, ps[:, 0, 0:WIN], ALU.add).then_inc(s_acc1, 1)
                make_onehot(g + 2, j).then_inc(s_hot1, 1)
            for j in range(2):
                make_onehot(j, j).then_inc(s_hot1, 1)
            def clear(q):
                V.tensor_copy(acc[:, :, ds(q * HALF, HALF)], marks[:, 3:4].unsqueeze(2).broadcast_to([P, 2, HALF]))

            def prepare(q, j):
                cols = lambda z, n: z[:, ds(n * HALF, HALF)]
                x1_flat = x1_nodes[:].rearrange("p b c -> p (b c)")
                if j == 0:
                    bias = b_gcn[:, ds(q % (C // HALF) * HALF, HALF)]
                    tt(cols(x1_flat, q), cols(x1_flat, q), bias, ALU.add)
                    if not (isinstance(q, int) and q == 0):
                        clear(q - 1)
                else:
                    stt(cols(x1_flat, q), cols(acc[:, 1, :], q), dis[:, ds(q // (C // HALF), 1)], cols(x1_flat, q), ALU.mult, ALU.add)

            dve.wait_ge(s_gtab, 16 * NCH)
            for q in range(2):
                for j in range(2):
                    group1(q, j, q == 0)
            with dve.Fori(2, NG // 2) as q:
                for j in range(2):
                    group1(q, j, False)
            radial(NG - 1, NG // 2 - 1, 1)

            dve.wait_ge(s_acc1, NG)
            V.memset(acc[:, :, NP - HALF:NW], 0.0)

            def add_window(w):
                window = gcn_acc[:, ds(w, WIN)]
                return tt(window, window, ps[:, 0, 0:WIN], ALU.add)
            further_windows(s_w1_free, s_w1_hot, s_w1_sum, s_w1_own, add_window, 4)
            V.tensor_copy(marks[:, 6:7], marks[:, 3:4]).then_inc(s_sum1_done, 1)

            def statistics(n, normalised, before):
                dve.wait_ge(s_norm, n * 4 + 1)
                dve.sem_inc(s_stats_seen, 1)
                for i in range(CB):
                    last = V.bn_stats(bn[:, i, :], y[:, ds(n % 2, 1), i, :].rearrange("p o c -> p (o c)"))
                last.then_inc(s_norm, 1)
                dve.wait_ge(s_norm, n * 4 + 2)
                dve.sem_inc(s_stats_seen, 1)
                for i in range(CB):
                    last = V.bn_aggr(mean_var[:, i, :], bn[:, i, :])
                last.then_inc(s_norm, 1)
                dve.wait_ge(s_norm, n * 4 + 3)
                if not (isinstance(before, int) and before == 0):
                    dve.sem_inc(s_stats_seen, 1)
                    dve.wait_ge(normalised, before)
                ts(rstd[:], mean_var[:, :, 1], LN_EPS, None, ALU.add).then_inc(s_ln1, 1)

            def scales(n):
                dve.wait_ge(s_ln2, n + 1)
                V.reciprocal(rstd[:], std[:]).then_inc(s_norm, 1)
                dve.wait_ge(s_norm, n * 4 + 4)
                stt(shift[:], mean_var[:, :, 0], -1.0, rstd[:], ALU.mult, ALU.mult).then_inc(s_ln3, 1)

            def norm3(c):
                dve.wait_ge(s_t1, c + 1)
                wait_past(dve, s_x1, c - 1)
                for i in range(CB):
                    last = stt(y[:, ds(c % 2, 1), i, :].rearrange("p o c -> p (o c)"), psflat[:, i * P:i * P + P], dis[:, ds(c * CB + i, 1)],
                               x1_nodes[:, ds(c * CB + i, 1), :].rearrange("p o c -> p (o c)"), ALU.mult, ALU.add)
                last.then_inc(s_norm, 1)
                dve.wait_ge(s_norm, c * 4 + 1)
                V.tensor_copy(marks[:, 1:2], marks[:, 3:4]).then_inc(s_ysum, 1)
                statistics(c, s_x1, c)
                scales(c)

            def tables3(c, early):
                dve.wait_ge(s_mm, c + 1)
                if not early:
                    dve.wait_ge(s_mst, (c - 1) * 16)
                tt(ms_out[:, ds(c % 2, 1)].rearrange("p o b c -> p (o b) c"), psflat[:, 2048:2048 + CC].rearrange("p (b c) -> p b c", c=C),
                   b_src[:].unsqueeze(1).broadcast_to([P, CB, C]), ALU.add).then_inc(s_mso, 1)
                dve.wait_ge(s_hi, c + 1)
                wait_past(dve, s_mdp, c)
                tt(md_rest[:], psflat[:, 3072:3072 + CC].rearrange("p (b c) -> p b c", c=C),
                   md_parts[:, ds(c % 2, 1), :, 0].rearrange("p o b c -> p (o b) c"), ALU.subtract).then_inc(s_mdr, 1)
            norm3(0)
            for c in (1, 2):
                norm3(c)
                tables3(c - 1, True)
            with dve.Fori(3, NCH) as c:
                norm3(c)
                tables3(c - 1, False)
            tables3(NCH - 1, False)
            dve.wait_ge(s_mso, NCH)
            dve.wait_ge(s_mdr, NCH)
            V.memset(ps[:, 5, WIN:2 * WIN], 0.0)
            V.memset(ps[:, 7, WIN:2 * WIN], 0.0).then_inc(s_zero, 1)

            dve.wait_ge(s_mdt, 16 * NCH)
            dve.wait_ge(s_mst, 16 * NCH)
            with dve.If(wide > 0):
                with dve.Fori(0, NT) as t:
                    dve.wait_ge(s_far_st, t * 16 + 16)
                    dve.sem_inc(s_stats_seen, 1)
                    ts(far_f[:], dst_rel[:, ds(t, 1)], win_f[:, ds(t // TPG, 1)], None, ALU.add).then_inc(s_far_own, 1)
                    dve.wait_ge(s_far_own, t * 3 + 1)
                    dve.sem_inc(s_stats_seen, 1)
                    V.tensor_copy(far_i[:], far_f[:]).then_inc(s_far_dst, 1)
                    dve.wait_ge(s_far_rows, t * 32 + 32)
                    dve.sem_inc(s_stats_seen, 1)
                    tt(far_row[:], far_md[:, 0], far_md[:, 1], ALU.add).then_inc(s_far_own, 1)
                    dve.wait_ge(s_far_own, t * 3 + 2)
                    dve.sem_inc(s_stats_seen, 1)
                    tt(far_row[:], far_row[:], far_md[:, 2], ALU.add).then_inc(s_far_own, 1)
                    dve.wait_ge(s_far_own, t * 3 + 3)
                    dve.sem_inc(s_stats_seen, 1)
                    tt(far_row[:], far_row[:], gath[:, 0, 0, :], ALU.add).then_inc(s_far_sum, 1)
            dve.wait_ge(s_rows_ready, 1)
            V.memset(md_lz[WIN:2 * WIN], 0.0)

            def hotT_of(g, q, j):
                dve.wait_ge(s_dst2[j], q * 16 + 16)
                ts(hotT[0:2 * WIN, j, :], dst_row[0:2 * WIN, j, :], win_iota[0:2 * WIN, ds(g, 1)], None, ALU.is_equal).then_inc(s_hotT, 1)

            def values_of(g, place, j):
                dve.wait_ge(s_held, g + 1)
                wait_past(dve, s_accd, g - 1)
                make_onehot(g, j)
                make_onehot(g, j, onehot_b)
                weights = p_edge[:, :, ds(place, 1), :].rearrange("p t o h -> p t (o h)").unsqueeze(3).broadcast_to([P, TPG, H, K])
                V.tensor_copy(wts[:, j], p_parts[:, :, ds(place, 1)].rearrange("p t o n h -> p t (o n h)"))
                tt(wval[:, j, :].rearrange("p (t h v) -> p t h v", t=TPG, h=H),
                   hold[:, ds(g % HOLD, 1), :].rearrange("p o (t h v) -> p (o t) h v", t=TPG, h=H), weights, ALU.mult).then_inc(s_v, 1)

            def starts_of(b):
                dve.wait_ge(s_seg, b * 16 + 16)
                inner = neg_edge[:, 1:GE]
                tt(inner, seg_row[:, 1:GE], seg_row[:, 0:GE - 1], ALU.not_equal).then_inc(s_sm, 1)
                dve.wait_ge(s_sm, b * 4 + 1)
                ts(inner, inner, -BIG, None, ALU.mult).then_inc(s_sm, 1)

            def maxima_of(b):
                dve.wait_ge(s_sm, b * 4 + 2)
                dve.wait_ge(s_turn, b + 1)
                turned = ps[0:GPS * H, 6, :]
                V.tensor_tensor_scan(fwd[:], neg_edge[:, 0:GE], turned, -BIG, ALU.add, ALU.max).then_inc(s_sm, 1)
                dve.wait_ge(s_sm, b * 4 + 3)
                V.tensor_tensor_scan(seg_max[:, ::-1], neg_edge[:, GE:0:-1], fwd[:, ::-1], -BIG, ALU.add, ALU.max).then_inc(s_sm, 1)
                dve.wait_ge(s_sm, b * 4 + 4)
                tt(shifted[:], turned, seg_max[:], ALU.subtract).then_inc(s_shift, 1)
                V.tensor_copy(max_first[:, ds(b, 1)], seg_max[:, 0:1])
                V.tensor_copy(max_last[:, ds(b, 1)], seg_max[:, GE - 1:GE]).then_inc(s_maxes, 1)

            def weight_parts(b, which):
                part = lambda n: p_parts[:, :, :, n].rearrange("p t g h -> p (t g) h")
                rest, edge = (z[:].rearrange("p t g h -> p (t g) h") for z in (p_rest, p_edge))
                steps = (lambda: V.tensor_copy(part(0), edge),
                         lambda: tt(rest, edge, part(0), ALU.subtract),
                         lambda: V.tensor_copy(part(1), rest),
                         lambda: tt(rest, rest, part(1), ALU.subtract),
                         lambda: V.tensor_copy(part(2), rest))
                for n in which:
                    steps[n]().then_inc(s_p_parts, 1)
                    dve.wait_ge(s_p_parts, b * 5 + (n - 4))

            def step4(b, k, pair, j, x, sep, sc, val, sm):
                g = b * GPS + k
                if sm == 4:
                    weight_parts(b, (2, 3, 4))
                if val:
                    values_of(g - LAG, place_of(k), j)
                if x:
                    dve.wait_ge(s_x, g + 1)
                    dve.wait_ge(s_rad2[j], (b * PPS + pair) * 16 + 16)
                    tt(msg[:, j, :], ps[:, j, :], mrad[:, j, :], ALU.mult).then_inc(s_m, 1)
                    hotT_next(b, k, pair, j)
                if sm == 0:
                    starts_of(b - 1)
                if sm == 2:
                    maxima_of(b - 1)
                if sm == 3:
                    dve.wait_ge(s_back, b)
                    wait_past(dve, s_v, b * GPS - GPS)
                    V.tensor_copy(p_edge[:].rearrange("p t g h -> p (t g h)"), ps[:, 6, 0:TPG * GPS * H]).then_inc(s_p, 1)
                    dve.wait_ge(s_p, b)
                    weight_parts(b, (0, 1))
                if sep:
                    dve.wait_ge(s_pre, g)
                    wait_past(dve, s_sc, g - 2)
                    stt(act_a[:, 1 - j, :], tanh[:, 1 - j, :], 1.5, pre[:, 1 - j, :], ALU.add, ALU.mult).then_inc(s_u, 1)
                if sm == 1:
                    dve.wait_ge(s_sc, b * GPS)
                    V.tensor_copy(scores[:].rearrange("p t (g h) -> p g t h", g=GPS),
                                  ps[:, 4, 0:GPS * TPG * H].rearrange("p (g t h) -> p g t h", g=GPS, t=TPG)).then_inc(s_sccopy, 1)

            def hotT_next(b, k, pair, j):
                hotT_of(b * GPS + (k + 2), b * PPS + (pair + 1), j)

            for j in range(2):
                hotT_of(j, 0, j)
            all_steps4(dve, step4)

            cont, single, chained, fresh, m_f, m_l, m_tot, tmp, m_lt, e_first, e_last, e_chain = (m[:] for m in mrg)
            dve.wait_ge(s_accd, NG)

            def add_windows(w):
                window = acc[:, :, ds(w, WIN)]
                return tt(window, window, ps[:, 5, 0:2 * WIN].rearrange("p (a w) -> p a w", a=2), ALU.add)
            further_windows(s_w2_free, s_w2_hot, s_w2_sum, s_w2_own, add_windows, 5)
            with dve.If(wide > 0):
                dve.wait_ge(s_w2_free, extra * NG + 1)
                dve.sem_inc(s_stats_seen, 1)
                with dve.Fori(0, NG) as g:
                    w = dve.value_load(win_i[0:1, ds(g, 1)], min_val=0, max_val=NP - 1)
                    V.tensor_copy(slot_prev[:, :, ds(g, 1)], acc[:, :, ds(w, 1)])
            V.tensor_copy(marks[:, 7:8], marks[:, 3:4]).then_inc(s_fixed, 1)
            dve.wait_ge(s_mx, 2)
            n1 = slice(1, NG)
            n0 = slice(0, NG - 1)
            V.memset(cont, 0.0)
            V.memset(chained, 0.0)
            V.memset(m_lt, -BIG)
            V.memset(e_last, 0.0)
            chain(V.memset(e_chain, 0.0))
            V.tensor_copy(slot_first[:, 1, :], ps[:, 2, 0:NG])
            V.tensor_copy(slot_prev[:, 1, :], ps[:, 2, NG:2 * NG])
            V.tensor_copy(m_f.rearrange("p (b g) -> p g b", g=GPS), ps[:, 0, 0:NG].rearrange("p (g b) -> p g b", b=NSB))
            V.tensor_copy(m_l.rearrange("p (b g) -> p g b", g=GPS), ps[:, 1, 0:NG].rearrange("p (g b) -> p g b", b=NSB))
            tt(single, win_f[:, 0:NG], last_f[:], ALU.is_equal)
            chain(tt(cont[:, n1], win_f[:, n1], last_f[:, n0], ALU.is_equal))
            chain(tt(chained[:, n1], cont[:, n1], single[:, n0], ALU.mult))
            chain(tt(fresh, cont, chained, ALU.subtract))
            chain(tt(m_lt[:, n1], m_l[:, n0], fresh[:, n1], ALU.mult))
            chain(ts(tmp, fresh, 1.0, BIG, ALU.subtract, ALU.mult))
            chain(tt(m_lt[:, n1], m_lt[:, n1], tmp[:, n1], ALU.add))
            chain(tt(m_lt, m_lt, m_f, ALU.max))
            chain(ts(tmp, chained, 1.0, BIG, ALU.subtract, ALU.mult))
            chain(V.tensor_tensor_scan(m_tot, tmp, m_lt, -BIG, ALU.add, ALU.max))
            tt(e_first, m_f, m_tot, ALU.subtract).then_inc(s_mxe, 1)
            chain(tt(e_last[:, n1], m_l[:, n0], m_tot[:, n1], ALU.subtract))
            ts(e_last, e_last, 0.0, None, ALU.min).then_inc(s_mxe, 1)
            chain(tt(e_chain[:, n1], m_tot[:, n0], m_tot[:, n1], ALU.subtract))
            ts(e_chain, e_chain, 0.0, None, ALU.min).then_inc(s_mxe, 1)
            dve.wait_ge(s_me, 3)
            tt(e_last, e_last, fresh, ALU.mult)
            chain(tt(e_chain, e_chain, chained, ALU.mult))
            chain(tt(slot_first[:], slot_first[:], e_first.unsqueeze(1).broadcast_to([P, 2, NG]), ALU.mult))
            chain(tt(slot_prev[:], slot_prev[:], e_last.unsqueeze(1).broadcast_to([P, 2, NG]), ALU.mult))
            chain(tt(mrg2[:], slot_first[:], slot_prev[:], ALU.add))
            for n in range(2):
                chain(V.tensor_tensor_scan(totals[:, n, :], e_chain, mrg2[:, n, :], 0.0, ALU.mult, ALU.add))
            chain(V.memset(fresh, 0.0))
            chain(tt(fresh[:, n0], win_f[:, n0], win_f[:, n1], ALU.is_equal))
            chain(ts(tmp, fresh, 1.0, -1.0, ALU.subtract, ALU.mult))
            for n in range(2):
                chain(tt(mrg2[:, n, :], totals[:, n, :], tmp, ALU.mult))
                chain(V.tensor_tensor_scan(totals[:, n, ::-1], fresh[:, ::-1], mrg2[:, n, ::-1], 0.0, ALU.mult, ALU.add))
            V.memset(fresh[:, 0:1], 0.0).then_inc(s_totals, 1)
            dve.wait_ge(s_mx, 3)
            V.tensor_copy(totals[0:H3, 1, :], ps[0:H3, 3, 0:NG]).then_inc(s_tot, 1)
            dve.wait_ge(s_tot, 1)
            write_back(dve, V.tensor_copy, WB_ACT, WB_ACT + WB_DVE)
            V.tensor_copy(marks[:, 1:2], marks[:, 3:4]).then_inc(s_wb, 1)
            dve.wait_ge(s_packed, 48)
            for n in (1, 2):
                chain(tt(den_p[:, 0, :], den_p[:, 0, :], den_p[:, n, :], ALU.add))
            chain(ts(den_p[:, 2, :], den_p[:, 0, :], 1e-16, None, ALU.add))
            chain(V.reciprocal(den_p[:, 1, :], den_p[:, 2, :]))
            tt(den_p[:, 2, :], den_p[:, 0, :], den_p[:, 1, :], ALU.mult).then_inc(s_inv, 1)

            def weigh5(c):
                dve.wait_ge(s_spread, c + 1)
                wait_past(dve, s_pr, c)
                tt(stage[:], psflat[:, ds(c % 2 * 1024, CC)], acc[:, 0, ds(c * CC, CC)], ALU.mult).then_inc(s_o, 1)

            def norm5(c):
                dve.wait_ge(s_pr, c + 1)
                wait_past(dve, s_y, c - 1)
                tt(y[:, ds((c + NCH) % 2, 1)].rearrange("p o b c -> p (o b) c"), psflat[:, 2048:2048 + CC].rearrange("p (b c) -> p b c", c=C),
                   x1_nodes[:, ds(c * CB, CB), :], ALU.add).then_inc(s_norm, 1)
                dve.wait_ge(s_norm, c * 4 + (NCH * 4 + 1))
                V.tensor_copy(marks[:, 1:2], marks[:, 3:4]).then_inc(s_ysum, 1)
                statistics(c + NCH, s_y, c)
                scales(c + NCH)
            weigh5(0)
            weigh5(1)
            norm5(0)
            weigh5(2)
            norm5(1)
            with dve.Fori(2, NCH - 1) as c:
                weigh5(c + 1)
                norm5(c)
            norm5(NCH - 1)


def kernel(**inputs):
    import concourse.bacc as bacc
    from concourse import mybir
    from concourse.bass_utils import run_bass_kernel_spmd

    v = {k: np.asarray(x) for k, x in inputs.items()}
    col = lambda x: np.ascontiguousarray(x.reshape(-1, 1))
    row = lambda x: np.ascontiguousarray(x.reshape(1, -1))
    pad = EP - N_EDGES
    src = np.concatenate([v["src"].astype(np.int32), np.zeros(pad, np.int32)])
    dst = np.concatenate([v["dst"].astype(np.int32), np.full(pad, NP - 1, np.int32)])
    ea = np.concatenate([v["edge_weight1"][:, 0], np.zeros(pad, np.float32)])
    attr = np.concatenate([v["edge_attr_32"], np.zeros((pad, RAD), np.float32)])
    x = np.concatenate([v["x"], np.zeros((NP - N_NODES, C), np.float32)])
    sep, b_sep = v["L1_gnn_w_sep"].reshape(C, H, 2, K), v["L1_gnn_b_sep"].reshape(H, 2, K)
    by_tile = lambda z: np.ascontiguousarray(z.reshape(NT, P).T)
    arrays = {
        "srcE": np.concatenate([by_tile(src), np.zeros((P, TPG), np.int32)], axis=1), "dstE": by_tile(dst),
        "dst_row": row(np.concatenate([dst, np.zeros(2 * GE, np.int32)])), "ea_row": row(ea),
        "first": np.concatenate([dst[::GE], np.zeros(2, np.int32)]), "last": dst[GE - 1::GE].copy(),
        "attrT": np.ascontiguousarray(attr.reshape(NG, TPG, P, RAD).transpose(1, 3, 0, 2).reshape(P, NG * P)),
        "xN": x, "xT": np.ascontiguousarray(x.T),
        "w_gcn": v["L0_gnn_W"], "b_gcn": v["L0_gnn_b"],
        "w_src": v["L1_gnn_w_src"], "b_src": v["L1_gnn_b_src"], "w_dst": v["L1_gnn_w_dst"],
        "fc_w1": v["L1_gnn_fc_w1"], "fc_b1": col(v["L1_gnn_fc_b1"]),
        "fc_w2": v["L1_gnn_fc_w2"], "fc_b2": col(v["L1_gnn_fc_b2"]),
        "fc_w3": v["L1_gnn_fc_w3"], "fc_b3": col(v["L1_gnn_fc_b3"]),
        "w_alpha": np.ascontiguousarray(sep[:, :, 0].reshape(C, P)), "w_value": np.ascontiguousarray(sep[:, :, 1].reshape(C, P)),
        "b_alpha": col(b_sep[:, 0]), "b_value": col(b_sep[:, 1]),
        "alpha_dot": col(v["L1_gnn_alpha_dot"]), "w_proj": v["L1_gnn_w_proj"], "b_proj": v["L1_gnn_b_proj"],
    }
    arrays = {k: np.ascontiguousarray(x) for k, x in arrays.items()}
    nc = bacc.Bacc("TRN2", target_bir_lowering=False, num_devices=1)
    aps = {k: nc.dram_tensor("in_" + k, x.shape, mybir.dt.from_np(x.dtype), kind="ExternalInput").ap() for k, x in arrays.items()}
    out = nc.dram_tensor("out_x", [NP, C], mybir.dt.float32, kind="ExternalOutput").ap()
    build(nc, aps, out)
    r = run_bass_kernel_spmd(nc, [{"in_" + k: x for k, x in arrays.items()}], core_ids=[0])
    return r.results[0]["out_x"][:N_NODES]
```
